# Optimizing a Trainium2 kernel written in Bass

```python
import numpy as np
import jax
import jax.numpy as jnp

def _softmax(x, axis=-1):
    return jax.nn.softmax(x, axis=axis)

def _gelu(x):
    return jax.nn.gelu(x, approximate=True)

def _silu(x):
    return jax.nn.silu(x)

def _sigmoid(x):
    return jax.nn.sigmoid(x)

def _layernorm(x, axis=-1, eps=1e-05):
    m = jnp.mean(x, axis=axis, keepdims=True)
    v = jnp.var(x, axis=axis, keepdims=True)
    return (x - m) / jnp.sqrt(v + eps)

def _scatter_add(tgt, idx, src, axis=0):
    return tgt.at[idx].add(src)

def _segment_sum(src, seg, n):
    return jax.ops.segment_sum(src, seg, n)
kernel_name = 'mk_xattn_ffn_d4_seqx_r4_221e99'

def setup_inputs(seed: int=0):
    np.random.seed(seed)
    _w = jnp.asarray

    def _rec_inputs():
        import jax
        import jax.numpy as jnp
        _rk = jax.random.key(seed)
        x = -0.0002928 + 1 * jax.random.normal(jax.random.fold_in(_rk, 1), (16, 256, 256), jnp.float32)
        _lenS = 256 - jax.random.randint(jax.random.fold_in(_rk, 7), (16,), 0, max(1, 256 // 4) + 1, jnp.int32)
        _lenS2 = 256 - jax.random.randint(jax.random.fold_in(_rk, 8), (16,), 0, max(1, 256 // 4) + 1, jnp.int32)
        _ctx_1024P = jax.random.normal(jax.random.fold_in(_rk, 11), (16, 16, 256), jnp.float32)
        _ctx_1024c = jax.random.dirichlet(jax.random.fold_in(_rk, 511), 0.3 * jnp.ones((16,), jnp.float32), (16, 256))
        _ctx_1024t = jnp.einsum('bsk,bkd->bsd', _ctx_1024c, _ctx_1024P)
        _ctx_1024t = _ctx_1024t * jax.lax.rsqrt(jnp.mean(jnp.square(_ctx_1024t)) + 1e-12) * 0.953939
        ctx_1024 = -1.39393e-06 + 0.999914 * (_ctx_1024t + 0.3 * jax.random.normal(jax.random.fold_in(_rk, 611), (16, 256, 256), jnp.float32))
        return (x, ctx_1024)
    x, ctx_1024 = _rec_inputs()

    def _L0_xattn_setup():
        import jax, jax.numpy as jnp
        import numpy as np
        D_MODEL = 256
        N_HEADS = 16
        D_K = D_MODEL // N_HEADS

        def _xavier(key, shape):
            fan_in, fan_out = (shape[1], shape[0])
            a = float(np.sqrt(6.0 / (fan_in + fan_out)))
            return jax.random.uniform(key, shape, jnp.float32, -a, a)
        key = jax.random.key(seed)
        ks = jax.random.split(key, 7)
        B, S = (2, 512)
        return {'query': jax.random.normal(ks[0], (B, S, D_MODEL), jnp.float32), 'key': jax.random.normal(ks[1], (B, S, D_MODEL), jnp.float32), 'value': jax.random.normal(ks[2], (B, S, D_MODEL), jnp.float32), 'w_q': _xavier(ks[3], (D_MODEL, D_MODEL)), 'w_k': _xavier(ks[4], (D_MODEL, D_MODEL)), 'w_v': _xavier(ks[5], (D_MODEL, D_MODEL)), 'w_o': _xavier(ks[6], (D_MODEL, D_MODEL)), 'b_q': jnp.zeros((D_MODEL,), jnp.float32), 'b_k': jnp.zeros((D_MODEL,), jnp.float32), 'b_v': jnp.zeros((D_MODEL,), jnp.float32), 'b_o': jnp.zeros((D_MODEL,), jnp.float32)}
    _L0_xattn_all = _L0_xattn_setup()
    _L0_xattn_in = {k: v for k, v in _L0_xattn_all.items() if k in ('w_q', 'w_k', 'w_v', 'w_o', 'b_q', 'b_k', 'b_v', 'b_o')}
    del _L0_xattn_all

    def _L0_ffn_setup():
        import jax, jax.numpy as jnp
        import numpy as np
        HIDDEN = 256
        INNER = 1024

        def _weight_quant(w):
            scale = 1.0 / jnp.clip(jnp.mean(jnp.abs(w)), 1e-05)
            wq = jnp.clip(jnp.round(w * scale), -1.0, 1.0) / scale
            return w + jax.lax.stop_gradient(wq - w)

        def _act_quant(x):
            scale = 127.0 / jnp.clip(jnp.max(jnp.abs(x), axis=-1, keepdims=True), 1e-05)
            xq = jnp.clip(jnp.round(x * scale), -128.0, 127.0) / scale
            return x + jax.lax.stop_gradient(xq - x)

        def _bitlinear(x, w):
            return jnp.einsum('bsi,oi->bso', _act_quant(x), _weight_quant(w))
        key = jax.random.key(seed)
        k0, k1, k2, k3 = jax.random.split(key, 4)
        x = jax.random.normal(k0, (4, 512, HIDDEN), dtype=jnp.float32)
        w_gate = jax.random.normal(k1, (INNER, HIDDEN), dtype=jnp.float32) / np.sqrt(HIDDEN)
        w_up = jax.random.normal(k2, (INNER, HIDDEN), dtype=jnp.float32) / np.sqrt(HIDDEN)
        w_down = jax.random.normal(k3, (HIDDEN, INNER), dtype=jnp.float32) / np.sqrt(INNER)
        return {'x': x, 'w_gate': w_gate, 'w_up': w_up, 'w_down': w_down}
    _L0_ffn_all = _L0_ffn_setup()
    _L0_ffn_in = {k: v for k, v in _L0_ffn_all.items() if k in ('w_gate', 'w_up', 'w_down')}
    del _L0_ffn_all

    def _L1_xattn_setup():
        import jax, jax.numpy as jnp
        import numpy as np
        B, S, H, NH = (2, 512, 256, 4)
        DH = H // NH
        EPS_BACKEND = 1e-06
        EPS_LN = 1e-06

        def _mlstm_parallel_stabilized(q, k, v, igate_preact, fgate_preact):
            b, nh, s, dh = q.shape
            log_fg = jax.nn.log_sigmoid(fgate_preact)
            cs = jnp.concatenate([jnp.zeros((b, nh, 1), q.dtype), jnp.cumsum(log_fg[..., 0], axis=2)], axis=2)
            fg_matrix = cs[:, :, :, None] - cs[:, :, None, :]
            fg_matrix = fg_matrix[:, :, 1:, 1:]
            causal = jnp.tril(jnp.ones((s, s), dtype=bool))
            log_fg_matrix = jnp.where(causal, fg_matrix, -jnp.inf)
            log_D = log_fg_matrix + jnp.swapaxes(igate_preact, -2, -1)
            max_log_D = jnp.max(log_D, axis=-1, keepdims=True)
            D = jnp.exp(log_D - max_log_D)
            qk = jnp.einsum('bhsd,bhtd->bhst', q, k) / jnp.sqrt(jnp.asarray(dh, q.dtype))
            C = qk * D
            normalizer = jnp.maximum(jnp.abs(jnp.sum(C, axis=-1, keepdims=True)), jnp.exp(-max_log_D))
            C_norm = C / (normalizer + EPS_BACKEND)
            return jnp.einsum('bhst,bhtd->bhsd', C_norm, v)

        def _multihead_layernorm(x, scale):
            mean = jnp.mean(x, axis=-1, keepdims=True)
            var = jnp.var(x, axis=-1, keepdims=True)
            xn = (x - mean) * jax.lax.rsqrt(var + EPS_LN)
            return xn * scale.reshape(NH, 1, DH)
        key = jax.random.key(seed)
        kq, kk, kv, kib = jax.random.split(key, 4)
        q = jax.random.normal(kq, (B, S, H), dtype=jnp.float32)
        k = jax.random.normal(kk, (B, S, H), dtype=jnp.float32)
        v = jax.random.normal(kv, (B, S, H), dtype=jnp.float32)
        igate_kernel = jnp.zeros((3 * H, NH), dtype=jnp.float32)
        igate_bias = 0.1 * jax.random.normal(kib, (NH,), dtype=jnp.float32)
        fgate_kernel = jnp.zeros((3 * H, NH), dtype=jnp.float32)
        fgate_bias = jnp.linspace(3.0, 6.0, NH, dtype=jnp.float32)
        outnorm_scale = jnp.ones((H,), dtype=jnp.float32)
        return {'q': q, 'k': k, 'v': v, 'igate_kernel': igate_kernel, 'igate_bias': igate_bias, 'fgate_kernel': fgate_kernel, 'fgate_bias': fgate_bias, 'outnorm_scale': outnorm_scale}
    _L1_xattn_all = _L1_xattn_setup()
    _L1_xattn_in = {k: v for k, v in _L1_xattn_all.items() if k in ('igate_kernel', 'igate_bias', 'fgate_kernel', 'fgate_bias', 'outnorm_scale')}
    del _L1_xattn_all

    def _L1_ffn_setup():
        import jax, jax.numpy as jnp
        import numpy as np
        B, C, D, O = (4, 1024, 256, 256)
        PROJ = 64
        RANKS = [1, 2, 4, 8]
        E = len(RANKS)
        CLAMP_MAX = float(np.log(1.0 / 0.01))

        def _l2norm(v, axis):
            return v / jnp.maximum(jnp.linalg.norm(v, axis=axis, keepdims=True), 1e-12)
        key = jax.random.key(seed)
        ks = jax.random.split(key, 16)
        inp = {'x': jax.random.normal(ks[0], (B, C, D), dtype=jnp.float32), 'W': jax.random.normal(ks[1], (O, D), dtype=jnp.float32) / np.sqrt(D), 'Wp': jax.random.normal(ks[2], (PROJ, D), dtype=jnp.float32) / np.sqrt(D), 'bp': jnp.zeros((PROJ,), dtype=jnp.float32), 'sim': jax.random.normal(ks[3], (PROJ, E), dtype=jnp.float32) * 0.01, 'temp': jnp.full((1,), np.log(1.0 / 0.5), dtype=jnp.float32)}
        for i, r in enumerate(RANKS):
            inp[f'Wd{i}'] = jax.random.normal(ks[4 + 2 * i], (r, D), dtype=jnp.float32) / r
            inp[f'Wu{i}'] = jax.random.normal(ks[5 + 2 * i], (O, r), dtype=jnp.float32) * 0.01
        return inp
    _L1_ffn_all = _L1_ffn_setup()
    _L1_ffn_in = {k: v for k, v in _L1_ffn_all.items() if k in ('W', 'Wp', 'bp', 'sim', 'temp', 'Wd0', 'Wu0', 'Wd1', 'Wu1', 'Wd2', 'Wu2', 'Wd3', 'Wu3')}
    del _L1_ffn_all

    def _L2_xattn_setup():
        import jax, jax.numpy as jnp
        import numpy as np
        DIM = 256
        NUM_HEADS = 16
        DIM_HEAD = 64
        INNER = NUM_HEADS * DIM_HEAD
        SCALE = DIM_HEAD ** (-0.5)

        def _layernorm(x, gamma, beta, eps=1e-05):
            mu = jnp.mean(x, axis=-1, keepdims=True)
            var = jnp.mean(jnp.square(x - mu), axis=-1, keepdims=True)
            return (x - mu) * jax.lax.rsqrt(var + eps) * gamma + beta
        key = jax.random.key(seed)
        ks = jax.random.split(key, 8)
        B, SQ, SK = (2, 512, 1024)
        x = jax.random.normal(ks[0], (B, SQ, DIM), dtype=jnp.float32)
        context = jax.random.normal(ks[1], (B, SK, DIM), dtype=jnp.float32)
        ln_gamma = jnp.ones((DIM,), jnp.float32)
        ln_beta = jnp.zeros((DIM,), jnp.float32)
        w_q = jax.random.normal(ks[2], (DIM, INNER), dtype=jnp.float32) / np.sqrt(DIM)
        w_kv = jax.random.normal(ks[3], (DIM, 2 * INNER), dtype=jnp.float32) / np.sqrt(DIM)
        w_out = jax.random.normal(ks[4], (INNER, DIM), dtype=jnp.float32) / np.sqrt(INNER)
        b_out = jnp.zeros((DIM,), jnp.float32)
        gate = jnp.array([0.5], jnp.float32)
        return {'x': x, 'context': context, 'ln_gamma': ln_gamma, 'ln_beta': ln_beta, 'w_q': w_q, 'w_kv': w_kv, 'w_out': w_out, 'b_out': b_out, 'gate': gate}
    _L2_xattn_all = _L2_xattn_setup()
    _L2_xattn_in = {k: v for k, v in _L2_xattn_all.items() if k in ('ln_gamma', 'ln_beta', 'w_q', 'w_kv', 'w_out', 'b_out', 'gate')}
    del _L2_xattn_all

    def _L2_ffn_setup():
        import jax, jax.numpy as jnp
        import numpy as np
        QMAX = 127.0

        def _ste_round(v):
            return v + jax.lax.stop_gradient(jnp.round(v) - v)

        def _act_fake_quant(x, clip_factor):
            scale = jax.nn.sigmoid(clip_factor) * jnp.max(jnp.abs(x)) / QMAX
            return jnp.clip(_ste_round(x / scale), -QMAX - 1.0, QMAX) * scale

        def _weight_fake_quant(w):
            scale = jnp.max(jnp.abs(w), axis=1, keepdims=True) / QMAX
            return jnp.clip(_ste_round(w / scale), -QMAX - 1.0, QMAX) * scale
        key = jax.random.key(seed)
        k1, k2, k3, k4 = jax.random.split(key, 4)
        B, S, H, I = (8, 2048, 256, 704)
        return {'x': jax.random.normal(k1, (B, S, H), dtype=jnp.float32), 'clip_x': jnp.full((1,), 4.0, dtype=jnp.float32), 'clip_down': jnp.full((1,), 4.0, dtype=jnp.float32), 'w_gate': jax.random.normal(k2, (I, H), dtype=jnp.float32) * 0.02, 'w_up': jax.random.normal(k3, (I, H), dtype=jnp.float32) * 0.02, 'w_down': jax.random.normal(k4, (H, I), dtype=jnp.float32) * 0.02}
    _L2_ffn_all = _L2_ffn_setup()
    _L2_ffn_in = {k: v for k, v in _L2_ffn_all.items() if k in ('clip_x', 'clip_down', 'w_gate', 'w_up', 'w_down')}
    del _L2_ffn_all

    def _L3_xattn_setup():
        import jax, jax.numpy as jnp
        import numpy as np
        DIM = 256
        N_HEADS = 16
        HEAD_DIM = DIM // N_HEADS
        B, L, M = (2, 512, 512)
        key = jax.random.key(seed)
        ks = jax.random.split(key, 7)
        s = 1.0 / np.sqrt(DIM)
        return {'q': jax.random.normal(ks[0], (B, L, DIM), dtype=jnp.float32), 'k': jax.random.normal(ks[1], (B, M, DIM), dtype=jnp.float32), 'v': jax.random.normal(ks[2], (B, M, DIM), dtype=jnp.float32), 'Wq': jax.random.normal(ks[3], (DIM, DIM), dtype=jnp.float32) * s, 'Wk': jax.random.normal(ks[4], (DIM, DIM), dtype=jnp.float32) * s, 'Wv': jax.random.normal(ks[5], (DIM, DIM), dtype=jnp.float32) * s, 'Wo': jax.random.normal(ks[6], (DIM, DIM), dtype=jnp.float32) * s}
    _L3_xattn_all = _L3_xattn_setup()
    _L3_xattn_in = {k: v for k, v in _L3_xattn_all.items() if k in ('Wq', 'Wk', 'Wv', 'Wo')}
    del _L3_xattn_all

    def _L3_ffn_setup():
        import jax, jax.numpy as jnp
        import numpy as np
        N_EMBD = 256
        N_EXPERTS = 8
        TOP_K = 2
        B, T = (4, 512)
        key = jax.random.key(seed)
        ks = jax.random.split(key, 8)
        C, E, H = (N_EMBD, N_EXPERTS, 4 * N_EMBD)
        s_in = 1.0 / np.sqrt(C)
        s_hid = 1.0 / np.sqrt(H)
        x = jax.random.normal(ks[0], (B, T, C), dtype=jnp.float32)
        W1 = jax.random.uniform(ks[1], (E, C, H), minval=-s_in, maxval=s_in, dtype=jnp.float32)
        b1 = jax.random.uniform(ks[2], (E, H), minval=-s_in, maxval=s_in, dtype=jnp.float32)
        W2 = jax.random.uniform(ks[3], (E, H, C), minval=-s_hid, maxval=s_hid, dtype=jnp.float32)
        b2 = jax.random.uniform(ks[4], (E, C), minval=-s_hid, maxval=s_hid, dtype=jnp.float32)
        Wg = jax.random.uniform(ks[5], (C, E), minval=-s_in, maxval=s_in, dtype=jnp.float32)
        bg = jax.random.uniform(ks[6], (E,), minval=-s_in, maxval=s_in, dtype=jnp.float32)
        return {'x': x, 'W1': W1, 'b1': b1, 'W2': W2, 'b2': b2, 'Wg': Wg, 'bg': bg}
    _L3_ffn_all = _L3_ffn_setup()
    _L3_ffn_in = {k: v for k, v in _L3_ffn_all.items() if k in ('W1', 'b1', 'W2', 'b2', 'Wg', 'bg')}
    del _L3_ffn_all
    return {'x': x, 'ctx_1024': ctx_1024, 'L0_xattn_w_q': _L0_xattn_in['w_q'], 'L0_xattn_w_k': _L0_xattn_in['w_k'], 'L0_xattn_w_v': _L0_xattn_in['w_v'], 'L0_xattn_w_o': _L0_xattn_in['w_o'], 'L0_xattn_b_q': _L0_xattn_in['b_q'], 'L0_xattn_b_k': _L0_xattn_in['b_k'], 'L0_xattn_b_v': _L0_xattn_in['b_v'], 'L0_xattn_b_o': _L0_xattn_in['b_o'], 'L0_ffn_w_gate': _L0_ffn_in['w_gate'], 'L0_ffn_w_up': _L0_ffn_in['w_up'], 'L0_ffn_w_down': _L0_ffn_in['w_down'], 'L1_xattn_igate_kernel': _L1_xattn_in['igate_kernel'], 'L1_xattn_igate_bias': _L1_xattn_in['igate_bias'], 'L1_xattn_fgate_kernel': _L1_xattn_in['fgate_kernel'], 'L1_xattn_fgate_bias': _L1_xattn_in['fgate_bias'], 'L1_xattn_outnorm_scale': _L1_xattn_in['outnorm_scale'], 'L1_ffn_W': _L1_ffn_in['W'], 'L1_ffn_Wp': _L1_ffn_in['Wp'], 'L1_ffn_bp': _L1_ffn_in['bp'], 'L1_ffn_sim': _L1_ffn_in['sim'], 'L1_ffn_temp': _L1_ffn_in['temp'], 'L1_ffn_Wd0': _L1_ffn_in['Wd0'], 'L1_ffn_Wu0': _L1_ffn_in['Wu0'], 'L1_ffn_Wd1': _L1_ffn_in['Wd1'], 'L1_ffn_Wu1': _L1_ffn_in['Wu1'], 'L1_ffn_Wd2': _L1_ffn_in['Wd2'], 'L1_ffn_Wu2': _L1_ffn_in['Wu2'], 'L1_ffn_Wd3': _L1_ffn_in['Wd3'], 'L1_ffn_Wu3': _L1_ffn_in['Wu3'], 'L2_xattn_ln_gamma': _L2_xattn_in['ln_gamma'], 'L2_xattn_ln_beta': _L2_xattn_in['ln_beta'], 'L2_xattn_w_q': _L2_xattn_in['w_q'], 'L2_xattn_w_kv': _L2_xattn_in['w_kv'], 'L2_xattn_w_out': _L2_xattn_in['w_out'], 'L2_xattn_b_out': _L2_xattn_in['b_out'], 'L2_xattn_gate': _L2_xattn_in['gate'], 'L2_ffn_clip_x': _L2_ffn_in['clip_x'], 'L2_ffn_clip_down': _L2_ffn_in['clip_down'], 'L2_ffn_w_gate': _L2_ffn_in['w_gate'], 'L2_ffn_w_up': _L2_ffn_in['w_up'], 'L2_ffn_w_down': _L2_ffn_in['w_down'], 'L3_xattn_Wq': _L3_xattn_in['Wq'], 'L3_xattn_Wk': _L3_xattn_in['Wk'], 'L3_xattn_Wv': _L3_xattn_in['Wv'], 'L3_xattn_Wo': _L3_xattn_in['Wo'], 'L3_ffn_W1': _L3_ffn_in['W1'], 'L3_ffn_b1': _L3_ffn_in['b1'], 'L3_ffn_W2': _L3_ffn_in['W2'], 'L3_ffn_b2': _L3_ffn_in['b2'], 'L3_ffn_Wg': _L3_ffn_in['Wg'], 'L3_ffn_bg': _L3_ffn_in['bg']}

def reference(x, ctx_1024, L0_xattn_w_q, L0_xattn_w_k, L0_xattn_w_v, L0_xattn_w_o, L0_xattn_b_q, L0_xattn_b_k, L0_xattn_b_v, L0_xattn_b_o, L0_ffn_w_gate, L0_ffn_w_up, L0_ffn_w_down, L1_xattn_igate_kernel, L1_xattn_igate_bias, L1_xattn_fgate_kernel, L1_xattn_fgate_bias, L1_xattn_outnorm_scale, L1_ffn_W, L1_ffn_Wp, L1_ffn_bp, L1_ffn_sim, L1_ffn_temp, L1_ffn_Wd0, L1_ffn_Wu0, L1_ffn_Wd1, L1_ffn_Wu1, L1_ffn_Wd2, L1_ffn_Wu2, L1_ffn_Wd3, L1_ffn_Wu3, L2_xattn_ln_gamma, L2_xattn_ln_beta, L2_xattn_w_q, L2_xattn_w_kv, L2_xattn_w_out, L2_xattn_b_out, L2_xattn_gate, L2_ffn_clip_x, L2_ffn_clip_down, L2_ffn_w_gate, L2_ffn_w_up, L2_ffn_w_down, L3_xattn_Wq, L3_xattn_Wk, L3_xattn_Wv, L3_xattn_Wo, L3_ffn_W1, L3_ffn_b1, L3_ffn_W2, L3_ffn_b2, L3_ffn_Wg, L3_ffn_bg):
    import jax
    import jax.numpy as jnp

    def _L0_xattn_ref(query, key, value, w_q, w_k, w_v, w_o, b_q, b_k, b_v, b_o):
        import jax, jax.numpy as jnp
        import numpy as np
        D_MODEL = 256
        N_HEADS = 16
        D_K = D_MODEL // N_HEADS

        def _xavier(key, shape):
            fan_in, fan_out = (shape[1], shape[0])
            a = float(np.sqrt(6.0 / (fan_in + fan_out)))
            return jax.random.uniform(key, shape, jnp.float32, -a, a)
        B = query.shape[0]
        scale = jnp.sqrt(jnp.asarray(D_K, query.dtype))

        def split_heads(x):
            return x.reshape(B, -1, N_HEADS, D_K).transpose(0, 2, 1, 3)
        q = split_heads(query @ w_q.T + b_q)
        k = split_heads(key @ w_k.T + b_k)
        v = split_heads(value @ w_v.T + b_v)
        scores = jnp.einsum('bhqd,bhkd->bhqk', q, k) / scale
        attn = jax.nn.softmax(scores, axis=-1)
        ctx = jnp.einsum('bhqk,bhkd->bhqd', attn, v)
        ctx = ctx.transpose(0, 2, 1, 3).reshape(B, -1, D_MODEL)
        out = ctx @ w_o.T + b_o
        return out

    def _L0_ffn_ref(x, w_gate, w_up, w_down):
        import jax, jax.numpy as jnp
        import numpy as np
        HIDDEN = 256
        INNER = 1024

        def _weight_quant(w):
            scale = 1.0 / jnp.clip(jnp.mean(jnp.abs(w)), 1e-05)
            wq = jnp.clip(jnp.round(w * scale), -1.0, 1.0) / scale
            return w + jax.lax.stop_gradient(wq - w)

        def _act_quant(x):
            scale = 127.0 / jnp.clip(jnp.max(jnp.abs(x), axis=-1, keepdims=True), 1e-05)
            xq = jnp.clip(jnp.round(x * scale), -128.0, 127.0) / scale
            return x + jax.lax.stop_gradient(xq - x)

        def _bitlinear(x, w):
            return jnp.einsum('bsi,oi->bso', _act_quant(x), _weight_quant(w))
        gate = jax.nn.silu(_bitlinear(x, w_gate))
        up = _bitlinear(x, w_up)
        return _bitlinear(gate * up, w_down)

    def _L1_xattn_ref(q, k, v, igate_kernel, igate_bias, fgate_kernel, fgate_bias, outnorm_scale):
        import jax, jax.numpy as jnp
        import numpy as np
        B, S, H, NH = (2, 512, 256, 4)
        DH = H // NH
        EPS_BACKEND = 1e-06
        EPS_LN = 1e-06

        def _mlstm_parallel_stabilized(q, k, v, igate_preact, fgate_preact):
            b, nh, s, dh = q.shape
            log_fg = jax.nn.log_sigmoid(fgate_preact)
            cs = jnp.concatenate([jnp.zeros((b, nh, 1), q.dtype), jnp.cumsum(log_fg[..., 0], axis=2)], axis=2)
            fg_matrix = cs[:, :, :, None] - cs[:, :, None, :]
            fg_matrix = fg_matrix[:, :, 1:, 1:]
            causal = jnp.tril(jnp.ones((s, s), dtype=bool))
            log_fg_matrix = jnp.where(causal, fg_matrix, -jnp.inf)
            log_D = log_fg_matrix + jnp.swapaxes(igate_preact, -2, -1)
            max_log_D = jnp.max(log_D, axis=-1, keepdims=True)
            D = jnp.exp(log_D - max_log_D)
            qk = jnp.einsum('bhsd,bhtd->bhst', q, k) / jnp.sqrt(jnp.asarray(dh, q.dtype))
            C = qk * D
            normalizer = jnp.maximum(jnp.abs(jnp.sum(C, axis=-1, keepdims=True)), jnp.exp(-max_log_D))
            C_norm = C / (normalizer + EPS_BACKEND)
            return jnp.einsum('bhst,bhtd->bhsd', C_norm, v)

        def _multihead_layernorm(x, scale):
            mean = jnp.mean(x, axis=-1, keepdims=True)
            var = jnp.var(x, axis=-1, keepdims=True)
            xn = (x - mean) * jax.lax.rsqrt(var + EPS_LN)
            return xn * scale.reshape(NH, 1, DH)
        b, s, h = q.shape
        gate_in = jnp.concatenate([q, k, v], axis=-1)
        ig = gate_in @ igate_kernel + igate_bias
        fg = gate_in @ fgate_kernel + fgate_bias
        ig = jnp.transpose(ig, (0, 2, 1))[..., None]
        fg = jnp.transpose(fg, (0, 2, 1))[..., None]
        qh = jnp.transpose(q.reshape(b, s, NH, DH), (0, 2, 1, 3))
        kh = jnp.transpose(k.reshape(b, s, NH, DH), (0, 2, 1, 3))
        vh = jnp.transpose(v.reshape(b, s, NH, DH), (0, 2, 1, 3))
        hs = _mlstm_parallel_stabilized(qh, kh, vh, ig, fg)
        hn = _multihead_layernorm(hs, outnorm_scale)
        return jnp.transpose(hn, (0, 2, 1, 3)).reshape(b, s, h)

    def _L1_ffn_ref(x, W, Wp, bp, sim, temp, Wd0, Wu0, Wd1, Wu1, Wd2, Wu2, Wd3, Wu3):
        import jax, jax.numpy as jnp
        import numpy as np
        B, C, D, O = (4, 1024, 256, 256)
        PROJ = 64
        RANKS = [1, 2, 4, 8]
        E = len(RANKS)
        CLAMP_MAX = float(np.log(1.0 / 0.01))

        def _l2norm(v, axis):
            return v / jnp.maximum(jnp.linalg.norm(v, axis=axis, keepdims=True), 1e-12)
        base = jnp.einsum('bcd,od->bco', x, W)
        xf = x.reshape(-1, x.shape[-1])
        proj = _l2norm(xf @ Wp.T + bp, axis=1)
        simn = _l2norm(sim, axis=0)
        scale = jnp.exp(jnp.minimum(temp, CLAMP_MAX))
        logits = proj @ simn * scale
        lw = jax.nn.softmax(logits, axis=1)
        top1 = jnp.argmax(lw, axis=1)
        ret = jnp.where(jnp.arange(E)[None, :] == top1[:, None], lw, 0.0)
        ret = ret.reshape(x.shape[0], x.shape[1], E)
        downs = (Wd0, Wd1, Wd2, Wd3)
        ups = (Wu0, Wu1, Wu2, Wu3)
        l = jnp.stack([jnp.einsum('bcr,or->bco', jnp.einsum('bcd,rd->bcr', x, d), u) for d, u in zip(downs, ups)], axis=2)
        res = jnp.sum(ret[..., None] * l, axis=2)
        return base + res

    def _L2_xattn_ref(x, context, ln_gamma, ln_beta, w_q, w_kv, w_out, b_out, gate):
        import jax, jax.numpy as jnp
        import numpy as np
        DIM = 256
        NUM_HEADS = 16
        DIM_HEAD = 64
        INNER = NUM_HEADS * DIM_HEAD
        SCALE = DIM_HEAD ** (-0.5)

        def _layernorm(x, gamma, beta, eps=1e-05):
            mu = jnp.mean(x, axis=-1, keepdims=True)
            var = jnp.mean(jnp.square(x - mu), axis=-1, keepdims=True)
            return (x - mu) * jax.lax.rsqrt(var + eps) * gamma + beta
        B, SQ, _ = x.shape
        SK = context.shape[1]
        xn = _layernorm(x, ln_gamma, ln_beta)
        q = (xn @ w_q).reshape(B, SQ, NUM_HEADS, DIM_HEAD)
        kv = context @ w_kv
        k, v = jnp.split(kv, 2, axis=-1)
        k = k.reshape(B, SK, NUM_HEADS, DIM_HEAD)
        v = v.reshape(B, SK, NUM_HEADS, DIM_HEAD)
        scores = jnp.einsum('bqhd,bkhd->bhqk', q * SCALE, k)
        attn = jax.nn.softmax(scores, axis=-1)
        out = jnp.einsum('bhqk,bkhd->bqhd', attn, v).reshape(B, SQ, INNER)
        out = out @ w_out + b_out
        return out * jnp.tanh(gate[0])

    def _L2_ffn_ref(x, clip_x, clip_down, w_gate, w_up, w_down):
        import jax, jax.numpy as jnp
        import numpy as np
        QMAX = 127.0

        def _ste_round(v):
            return v + jax.lax.stop_gradient(jnp.round(v) - v)

        def _act_fake_quant(x, clip_factor):
            scale = jax.nn.sigmoid(clip_factor) * jnp.max(jnp.abs(x)) / QMAX
            return jnp.clip(_ste_round(x / scale), -QMAX - 1.0, QMAX) * scale

        def _weight_fake_quant(w):
            scale = jnp.max(jnp.abs(w), axis=1, keepdims=True) / QMAX
            return jnp.clip(_ste_round(w / scale), -QMAX - 1.0, QMAX) * scale
        xq = _act_fake_quant(x, clip_x[0])
        gate = jnp.einsum('bsh,ih->bsi', xq, _weight_fake_quant(w_gate))
        up = jnp.einsum('bsh,ih->bsi', xq, _weight_fake_quant(w_up))
        h = _act_fake_quant(jax.nn.silu(gate) * up, clip_down[0])
        return jnp.einsum('bsi,hi->bsh', h, _weight_fake_quant(w_down))

    def _L3_xattn_ref(q, k, v, Wq, Wk, Wv, Wo):
        import jax, jax.numpy as jnp
        import numpy as np
        DIM = 256
        N_HEADS = 16
        HEAD_DIM = DIM // N_HEADS
        B, L, M = (2, 512, 512)
        b, l, _ = q.shape
        m = k.shape[1]
        qp = q @ Wq.T
        kp = k @ Wk.T
        vp = v @ Wv.T
        qh = qp.reshape(b, l, HEAD_DIM, N_HEADS)
        kh = kp.reshape(b, m, HEAD_DIM, N_HEADS)
        score = jnp.einsum('bldn,bmdn->blmn', qh, kh) / jnp.sqrt(jnp.float32(HEAD_DIM))
        attn = jax.nn.softmax(score, axis=2)
        x = jnp.einsum('blmn,bmdn->bldn', attn, kh)
        x = x.reshape(b, l, DIM)
        return x @ Wo.T

    def _L3_ffn_ref(x, W1, b1, W2, b2, Wg, bg):
        import jax, jax.numpy as jnp
        import numpy as np
        N_EMBD = 256
        N_EXPERTS = 8
        TOP_K = 2
        B, T = (4, 512)
        gate_scores = jax.nn.softmax(jnp.einsum('btc,ce->bte', x, Wg) + bg, axis=-1)
        h = jax.nn.relu(jnp.einsum('btc,ech->bteh', x, W1) + b1)
        expert_out = jnp.einsum('bteh,ehc->btec', h, W2) + b2
        topk_scores, topk_idx = jax.lax.top_k(gate_scores, TOP_K)
        top_probs = jax.nn.softmax(topk_scores, axis=-1)
        sel = jnp.take_along_axis(expert_out, topk_idx[..., None], axis=2)
        out = jnp.sum(sel * top_probs[..., None], axis=2)
        return out
    x = x + _L0_xattn_ref(_layernorm(x, axis=-1), ctx_1024, ctx_1024, L0_xattn_w_q, L0_xattn_w_k, L0_xattn_w_v, L0_xattn_w_o, L0_xattn_b_q, L0_xattn_b_k, L0_xattn_b_v, L0_xattn_b_o)
    x = x + _L0_ffn_ref(_layernorm(x, axis=-1), L0_ffn_w_gate, L0_ffn_w_up, L0_ffn_w_down)
    x = x + _L1_xattn_ref(_layernorm(x, axis=-1), ctx_1024, ctx_1024, L1_xattn_igate_kernel, L1_xattn_igate_bias, L1_xattn_fgate_kernel, L1_xattn_fgate_bias, L1_xattn_outnorm_scale)
    x = x + _L1_ffn_ref(_layernorm(x, axis=-1), L1_ffn_W, L1_ffn_Wp, L1_ffn_bp, L1_ffn_sim, L1_ffn_temp, L1_ffn_Wd0, L1_ffn_Wu0, L1_ffn_Wd1, L1_ffn_Wu1, L1_ffn_Wd2, L1_ffn_Wu2, L1_ffn_Wd3, L1_ffn_Wu3)
    x = x + _L2_xattn_ref(_layernorm(x, axis=-1), ctx_1024, L2_xattn_ln_gamma, L2_xattn_ln_beta, L2_xattn_w_q, L2_xattn_w_kv, L2_xattn_w_out, L2_xattn_b_out, L2_xattn_gate)
    x = x + _L2_ffn_ref(_layernorm(x, axis=-1), L2_ffn_clip_x, L2_ffn_clip_down, L2_ffn_w_gate, L2_ffn_w_up, L2_ffn_w_down)
    x = x + _L3_xattn_ref(_layernorm(x, axis=-1), ctx_1024, ctx_1024, L3_xattn_Wq, L3_xattn_Wk, L3_xattn_Wv, L3_xattn_Wo)
    x = x + _L3_ffn_ref(_layernorm(x, axis=-1), L3_ffn_W1, L3_ffn_b1, L3_ffn_W2, L3_ffn_b2, L3_ffn_Wg, L3_ffn_bg)
    return x

_drawn_inputs = setup_inputs


def setup_inputs(seed=0):
    import zlib

    import numpy as np

    out = dict(_drawn_inputs(seed))
    spreads = {'L0_xattn_b_q': (0.0, 0.1),
     'L0_xattn_b_k': (0.0, 2.0),
     'L0_xattn_b_v': (0.0, 0.1),
     'L0_xattn_b_o': (0.0, 0.1),
     'L1_xattn_igate_kernel': (0.0, 0.1),
     'L1_xattn_fgate_kernel': (0.0, 0.1),
     'L1_xattn_outnorm_scale': (1.0, 0.2),
     'L1_ffn_bp': (0.0, 0.8),
     'L2_xattn_ln_gamma': (1.0, 0.6),
     'L2_xattn_ln_beta': (0.0, 0.8),
     'L2_xattn_b_out': (0.0, 0.297)}
    factors = {'L1_xattn_igate_bias': 64.0,
     'L1_ffn_Wp': 3.651,
     'L1_ffn_sim': 3.521,
     'L1_ffn_Wd0': 4.996,
     'L1_ffn_Wu0': 4.961,
     'L1_ffn_Wd1': 6.022,
     'L1_ffn_Wu1': 5.835,
     'L1_ffn_Wd2': 7.359,
     'L1_ffn_Wu2': 7.641,
     'L1_ffn_Wd3': 8.0,
     'L1_ffn_Wu3': 8.0,
     'L2_ffn_w_gate': 3.444,
     'L2_ffn_w_up': 3.545,
     'L2_ffn_w_down': 3.463,
     'L3_ffn_b1': 8.0,
     'L3_ffn_b2': 8.0,
     'L3_ffn_bg': 2.992}
    for name, (base, spread) in spreads.items():
        noise = np.random.default_rng([zlib.crc32(name.encode()), seed]).standard_normal(out[name].shape)
        drawn = base * np.exp(spread * noise) if base else spread * noise
        out[name] = jnp.asarray(drawn.astype(out[name].dtype))
    for name, factor in factors.items():
        out[name] = (out[name] * factor).astype(out[name].dtype)
    return out
```

```python
from contextlib import ExitStack

import numpy as np

import concourse.bass as bass
from concourse import mybir

P = 128
B = 16
S = 256
D = 256
TB = S // P
NT = B * TB
KC = D // P
H = 16

F32 = mybir.dt.float32
BF16 = mybir.dt.bfloat16
NB_TEST = B
EXPERTS = 8
TILE = 256
MAX_TILES = 2 * B * S // TILE + EXPERTS
I32 = mybir.dt.int32
ALU = mybir.AluOpType
ACT = mybir.ActivationFunctionType
AX = mybir.AxisListType
ROUND = 12582912.0


class Core:

    def __init__(self, nc, ctx, dram):
        self.nc, self.dram = nc, dram
        self.X = ctx.enter_context(nc.sbuf_tensor("X", [P, NT, D], F32))
        self.stats = ctx.enter_context(nc.sbuf_tensor("stats", [P, NT, 6], F32))
        self.mean = ctx.enter_context(nc.sbuf_tensor("mean", [P, NT], F32))
        self.rstd = ctx.enter_context(nc.sbuf_tensor("rstd", [P, NT], F32))
        self.ident = ctx.enter_context(nc.sbuf_tensor("ident", [P, P], F32))
        self.ident_b = ctx.enter_context(nc.sbuf_tensor("ident_b", [P, P], BF16))
        self.gathered = nc.dram_tensor("tokens_by_expert", [(MAX_TILES + 1) * TILE, D], F32, kind="Internal").ap()
        self.expert_out = nc.dram_tensor("expert_outputs", [MAX_TILES * TILE, D], F32, kind="Internal").ap()
        self.cleared = ctx.enter_context(nc.semaphore("cleared"))
        self.zeros = ctx.enter_context(nc.sbuf_tensor("zero_row", [P, D], F32))

    def clear(self, eng):
        def zero(dst):
            eng.dma_start(dst.rearrange("(r p) d -> p r d", p=P),
                          self.zeros[:, :].unsqueeze(1).to_broadcast([P, dst.shape[0] // P, D]))\
               .then_inc(self.cleared, 16)
        zero(self.gathered)
        zero(self.expert_out[2 * NB_TEST * S // TILE * TILE:, :])


def load_residual(core):
    nc, X, stats = core.nc, core.X, core.stats
    with ExitStack() as ctx:
        x_in = [ctx.enter_context(nc.semaphore(f"x_in{q}")) for q in range(4)]
        ident_in = ctx.enter_context(nc.semaphore("ident_in"))
        x_view = core.dram["x"].rearrange("b (j p) d -> p (b j) d", p=P)
        quarter = NT // 4
        with nc.Block() as block:
            @block.sync
            def _(sp):
                for q in range(4):
                    part = slice(q * quarter, (q + 1) * quarter)
                    sp.dma_start(X[:, part, :], x_view[:, part, :]).then_inc(x_in[q], 16)
                sp.dma_start(core.ident[:, :], core.dram["ident"]).then_inc(ident_in, 16)

            @block.vector
            def _(dve):
                nc.vector.memset(core.zeros[:, :], 0.0)
                dve.wait_ge(ident_in, 16)
                nc.vector.tensor_copy(core.ident_b[:, :], core.ident[:, :])
                for q in range(4):
                    dve.wait_ge(x_in[q], 16)
                    for t in range(q * quarter, (q + 1) * quarter):
                        nc.vector.bn_stats(stats[:, t, :], X[:, t, :])


def norm_params(core, tag, eps=1e-5, second_eps=None):
    nc, stats, mean, rstd = core.nc, core.stats, core.mean, core.rstd
    with ExitStack() as ctx:
        def sb(name):
            return ctx.enter_context(nc.sbuf_tensor(f"{tag}_{name}", [P, NT], F32))
        half_diff, var, root, tmp, first = sb("half_diff"), sb("norm_var"), sb("root"), sb("tmp"), sb("first_rstd")
        step = ctx.enter_context(nc.semaphore(f"{tag}_step"))
        var_ready = ctx.enter_context(nc.semaphore(f"{tag}_var_ready"))
        root_ready = ctx.enter_context(nc.semaphore(f"{tag}_root_ready"))
        rounds = [(eps, rstd)] if second_eps is None else [(eps, first), (second_eps, rstd)]
        with nc.Block() as block:
            @block.scalar
            def _(act):
                for r in range(len(rounds)):
                    act.wait_ge(var_ready, r + 1)
                    nc.scalar.activation(root[:, :], var[:, :], ACT.Sqrt).then_inc(root_ready, 1)

            @block.vector
            def _(dve):
                done = [0]

                def then_wait(ins):
                    done[0] += 1
                    ins.then_inc(step, 1)
                    dve.wait_ge(step, done[0])

                mean_e, m2_e, mean_o, m2_o = stats[:, :, 1], stats[:, :, 2], stats[:, :, 4], stats[:, :, 5]
                then_wait(nc.vector.tensor_tensor(mean[:, :], mean_e, mean_o, ALU.add))
                then_wait(nc.vector.tensor_scalar(mean[:, :], mean[:, :], 0.5, None, ALU.mult))
                then_wait(nc.vector.tensor_tensor(half_diff[:, :], mean_e, mean_o, ALU.subtract))
                then_wait(nc.vector.scalar_tensor_tensor(half_diff[:, :], half_diff[:, :], 0.25, half_diff[:, :],
                                                         ALU.mult, ALU.mult))
                then_wait(nc.vector.tensor_tensor(var[:, :], m2_e, m2_o, ALU.add))
                then_wait(nc.vector.scalar_tensor_tensor(var[:, :], var[:, :], 1.0 / D, half_diff[:, :],
                                                         ALU.mult, ALU.add))
                for r, (add, result) in enumerate(rounds):
                    if r:
                        then_wait(nc.vector.tensor_tensor(var[:, :], half_diff[:, :], first[:, :], ALU.mult))
                        then_wait(nc.vector.tensor_tensor(var[:, :], var[:, :], first[:, :], ALU.mult))
                    else:
                        then_wait(nc.vector.tensor_copy(half_diff[:, :], var[:, :]))
                    then_wait(nc.vector.tensor_scalar(var[:, :], var[:, :], add, None, ALU.add))
                    nc.vector.tensor_copy(tmp[:, :], var[:, :]).then_inc(var_ready, 1)
                    dve.wait_ge(root_ready, r + 1)
                    then_wait(nc.vector.reciprocal(result[:, :], root[:, :]))
                    then_wait(nc.vector.tensor_tensor(tmp[:, :], result[:, :], result[:, :], ALU.mult))
                    then_wait(nc.vector.tensor_tensor(tmp[:, :], tmp[:, :], var[:, :], ALU.mult))
                    then_wait(nc.vector.tensor_scalar(tmp[:, :], tmp[:, :], -0.5, 1.5, ALU.mult, ALU.add))
                    then_wait(nc.vector.tensor_tensor(result[:, :], result[:, :], tmp[:, :], ALU.mult))
                if second_eps is not None:
                    then_wait(nc.vector.tensor_tensor(rstd[:, :], rstd[:, :], first[:, :], ALU.mult))


def reuse_semaphores(core):
    ended = sorted(core.nc.released_uncleared_semaphores)
    with core.nc.Block() as block:
        @block.sync
        def _(sp):
            first = 0
            for i in range(1, len(ended) + 1):
                if i == len(ended) or ended[i] != ended[i - 1] + 1:
                    sp.sem_clear(range(ended[first], ended[i - 1] + 1))
                    first = i


def store_residual(core):
    nc, X = core.nc, core.X
    with nc.semaphore("out_stored") as out_stored, nc.Block() as block:
        @block.sync
        def _(sp):
            sp.dma_start(core.dram["out"].rearrange("b (j p) d -> p (b j) d", p=P), X[:, :, :])\
              .then_inc(out_stored, 16)
            sp.wait_ge(out_stored, 16)


def attention(core, tag, dh, w_q, w_k, w_v, w_o, scale, b_q=None, b_k=None, b_v=None, b_o=None,
              gamma=None, beta=None, gate=None, clear=False, batches=B):
    nc, X, dram = core.nc, core.X, core.dram
    DI = H * dh
    CH = DI // P
    HPC = P // dh
    ROWS = 32 if dh == 16 else dh
    HG = 16 if dh == 16 else 4
    W1 = dh + 1
    masked = dh == 16
    NPAIR = CH // 2
    VH = max(1, DI // 512)

    finish_fills = [f"oT{c}" for c in range(NPAIR)] + ["out0", "out1"]
    v_fills = ["v"] if masked else [f"v{j}{n}" for j in range(TB) for n in range(VH)]
    begin_fills = ["xnT"] + [f"q{c}" for c in range(NPAIR)] + [f"k{c}" for c in range(NPAIR)] + v_fills + ["mT"]
    nF, nP = len(finish_fills), len(begin_fills)
    assert (nF + nP) % 2 == 0
    slot_of = {}
    for n, f in enumerate(finish_fills):
        slot_of[f] = 2 + n * 3 // nF
    for n, f in enumerate(begin_fills[:-1]):
        slot_of[f] = 5 + n * 5 // (nP - 1)
    S_SLOTS = range(10, 16)
    heads_at = {s: [h for h in range(H) if 10 + h * 6 // 16 == s] for s in S_SLOTS}

    with ExitStack() as ctx:
        def sb(name, shape, dt=F32):
            return ctx.enter_context(nc.sbuf_tensor(f"{tag}_{name}", shape, dt))

        def ps(name, shape=(P, 512)):
            return ctx.enter_context(nc.psum_tensor(f"{tag}_{name}", list(shape), F32))

        def sem(name):
            return ctx.enter_context(nc.semaphore(f"{tag}_{name}"))

        wq, wk, wv = (sb(n, [P, KC, DI]) for n in ("wq", "wk", "wv"))
        wo = sb("wo", [P, CH, D])
        vec = sb("vec", [P, 3 * CH + 2 * KC + 2 + 1])
        bq_col, bk_col = vec[:, 0:CH], vec[:, CH:2 * CH]
        gam, bet = vec[:, 3 * CH:3 * CH + KC], vec[:, 3 * CH + KC:3 * CH + 2 * KC]
        masks = vec[:, 3 * CH + 2 * KC:3 * CH + 2 * KC + 2]
        gate_col = vec[:, 3 * CH + 2 * KC + 2:3 * CH + 2 * KC + 3]
        bq_masked = sb("bq_masked", [P, 2, CH])
        bv_row = sb("bv_row", [P, DI])
        bo_row = sb("bo_row", [P, D])
        sel32 = sb("sel32", [P, H])
        sel = sb("sel", [P, H, P], BF16)
        ctxT = [sb(f"ctxT{i}", [P, KC, S]) for i in range(2)]
        xn = sb("xn", [P, TB, D])
        xnT = sb("xnT", [P, KC, S])
        NQ = 2 if masked else 1
        qT = [sb(f"qT{i}", [P, NQ, CH, S]) for i in range(2)]
        kT = [sb(f"kT{i}", [P, CH, S]) for i in range(2)]
        v = [sb(f"v{i}", [P, TB, H, W1]) for i in range(2)]
        mx = sb("mx", [P, TB, H])
        nm = sb("nm", [P, TB, 2 * H], BF16)
        nm4 = sb("nm4", [P, TB, 4, 2 * H], BF16)
        mT = [sb(f"mT{i}", [P, S], BF16) for i in range(2)]
        probs = [sb(f"probs{i}", [P, TB, S]) for i in range(4)]
        inv = sb("inv", [P, TB, H])
        o = sb("o", [P, TB, H, dh])
        oT = sb("oT", [P, CH, S])
        out_t = sb("out_t", [P, TB, D])
        pS = [ps(f"pS{i}") for i in range(2)]
        pT = [ps(f"pT{i}") for i in range(2)]
        pO = [ps(f"pO{i}") for i in range(2)]
        pM = [ps(f"pM{i}") for i in range(2)]

        weights_in = sem("weights_in")
        small_in = sem("small_in")
        ctx_in = [sem(f"ctx_in{i}") for i in range(2)]
        setup = sem("setup")
        gate_ready = sem("gate_ready")
        xn_ready = sem("xn_ready")
        full = [sem(f"full{i}") for i in range(2)]
        free = [sem(f"free{i}") for i in range(2)]
        s_ready = sem("s_ready")
        max_done = sem("max_done")
        m_hi, m_lo, m_four = sem("m_hi"), sem("m_lo"), sem("m_four")
        t_ready = sem("t_ready")
        p_ready = sem("p_ready")
        pv_done = sem("pv_done")
        inv_ready = sem("inv_ready")
        o_ready = sem("o_ready")
        x_new = sem("x_new")
        NG = H // HG

        half = (nF + nP) // 2

        def fill(k, name):
            if isinstance(k, int) and k == -1:
                n = begin_fills.index(name)
            elif isinstance(k, int) and k == batches:
                n = 2 * nP + (batches - 2) * (nF + nP) + nF + finish_fills.index(name)
            else:
                i = finish_fills.index(name) if name in finish_fills else nF + begin_fills.index(name)
                return (nP - nF + i) % 2, k * half + (nP - nF + i) // 2
            return n % 2, n // 2

        def head_of(h):
            return h // 8 * 8 + h % 4 * 2 + h % 8 // 4 if masked else h

        def rows(h):
            c, r = h // HPC, (h % HPC) * dh
            return c, slice(r // ROWS * ROWS, r // ROWS * ROWS + ROWS)

        def q_of(h):
            return (h % 2) if masked else 0

        def run_rounds(eng, round_):
            round_(0, 0, 0, prev=False)
            if batches > 2:
                with eng.Fori(0, (batches - 2) // 2) as i:
                    round_(2 * i + 1, 1, i + 1)
                    round_(2 * i + 2, 0, i + 1)
            round_(batches - 1, (batches - 1) % 2, None, nxt=False)

        block = ctx.enter_context(nc.Block())

        @block.sync
        def _(sp):
            for w, src in ((wq, w_q), (wk, w_k), (wv, w_v), (wo, w_o)):
                sp.dma_start(w[:, :, :], dram[src].rearrange("(c p) n -> p c n", p=P)).then_inc(weights_in, 16)

            def column(dst, name):
                sp.dma_start(dst, dram[name].rearrange("(c p) -> p c", p=P),
                             allow_slow_non_contiguous=True).then_inc(small_in, 16)
            if b_q:
                column(bq_col, b_q)
            if b_k:
                column(bk_col, b_k)
            if gamma:
                column(gam, gamma)
                column(bet, beta)
            sp.dma_start(masks, dram["head_masks"]).then_inc(small_in, 16)
            sp.dma_start(sel32[:, :], dram[f"head_select{dh}"]).then_inc(small_in, 16)
            if b_v:
                sp.dma_start(bv_row[:, :], dram[b_v].partition_broadcast(P)).then_inc(small_in, 16)
            if b_o:
                sp.dma_start(bo_row[:, :], dram[b_o].partition_broadcast(P)).then_inc(small_in, 16)
            if gate:
                sp.dma_start(gate_col, dram[gate].partition_broadcast(P)).then_inc(small_in, 16)

            def load_ctx(b, par):
                bank, n = fill(b - 3, v_fills[-1])
                sp.wait_ge(full[bank], n + 1)
                sp.dma_start(ctxT[par][:, :, :], ctx_view[bass.ds(b, 1)].rearrange("o p c s -> p (o c) s"))\
                  .then_inc(ctx_in[par], 16)
            ctx_view = dram["ctxT"].rearrange("b (c p) s -> b p c s", p=P)
            sp.dma_start(ctxT[0][:, :, :], ctx_view[0]).then_inc(ctx_in[0], 16)
            sp.dma_start(ctxT[1][:, :, :], ctx_view[1]).then_inc(ctx_in[1], 16)
            if batches > 2:
                load_ctx(2, 0)
                with sp.Fori(0, (batches - 4) // 2) as i:
                    load_ctx(2 * i + 3, 1)
                    load_ctx(2 * i + 4, 0)
                load_ctx(batches - 1, 1)
            if clear:
                core.clear(sp)
        n_small = 16 * (2 + sum(1 for x in (b_q, b_k, b_v, b_o, gate) if x) + (2 if gamma else 0))

        @block.scalar
        def _(act):
            act.wait_ge(small_in, n_small)
            if gate:
                nc.scalar.activation(gate_col, gate_col, ACT.Tanh).then_inc(gate_ready, 1)
            act.wait_ge(setup, 1)

            def exp(k, h):
                act.wait_ge(t_ready, k * H + h + 1)
                if not (isinstance(k, int) and k == 0 and h < 4):
                    act.wait_ge(pv_done, k * H + h - 3)
                nc.scalar.activation(probs[h % 4][:, :, :], pT[h % 2][:, :], ACT.Exp, scale=scale).then_inc(p_ready, 1)

            def read_out(k, name, par):
                bank, n = fill(k, name)
                src = pM[bank][:, :].rearrange("p (c s) -> p c s", c=2)
                act.wait_ge(full[bank], n + 1)
                if name == "xnT" and gamma:
                    for c in range(KC):
                        ins = nc.scalar.activation(xnT[:, c, :], src[:, c, :], ACT.Identity, bias=bet[:, c:c + 1],
                                             scale=gam[:, c:c + 1])
                    ins.then_inc(free[bank], 1)
                elif name == "xnT":
                    nc.scalar.activation(xnT[:, :, :], src, ACT.Copy).then_inc(free[bank], 1)
                elif name[0] == "q":
                    c0 = 2 * int(name[1:])
                    if masked:
                        for e in range(2):
                            for c in range(2):
                                ins = nc.scalar.activation(qT[par][:, e, c0 + c, :], src[:, c, :], ACT.Identity,
                                                           bias=bq_masked[:, e, c0 + c:c0 + c + 1],
                                                           scale=masks[:, e:e + 1])
                        ins.then_inc(free[bank], 1)
                    else:
                        nc.scalar.activation(qT[par][:, 0, c0:c0 + 2, :], src, ACT.Copy).then_inc(free[bank], 1)
                elif name[:2] == "oT":
                    c0 = 2 * int(name[2:])
                    nc.scalar.activation(oT[:, c0:c0 + 2, :], src, ACT.Copy).then_inc(free[bank], 1)
                elif name == "mT":
                    nc.scalar.activation(mT[par][:, :], pM[bank][:, 0:S], ACT.Copy).then_inc(free[bank], 1)

            mine = lambda name: name == "xnT" or name[0] == "q" or name[:2] == "oT"

            for name in begin_fills:
                if mine(name) or name == "mT":
                    read_out(-1, name, 0)

            def round_(k, par, half_b, prev=True, nxt=True):
                for h in range(H):
                    exp(k, h)
                    for name in finish_fills:
                        if prev and slot_of[name] == h and mine(name):
                            read_out(k, name, 1 - par)
                    for name in begin_fills[:-1]:
                        if nxt and slot_of[name] == h and mine(name):
                            read_out(k, name, 1 - par)
                if nxt:
                    read_out(k, "mT", 1 - par)
            run_rounds(act, round_)
            for name in finish_fills:
                if mine(name):
                    read_out(batches, name, (batches - 1) % 2)

        @block.vector
        def _(dve):
            dve.wait_ge(small_in, n_small)
            for e in range(2):
                if b_q:
                    nc.vector.tensor_scalar(bq_masked[:, e, :], bq_col, masks[:, e:e + 1], None, ALU.mult)
                else:
                    nc.vector.memset(bq_masked[:, e, :], 0.0)
            for i in range(2):
                nc.vector.memset(v[i][:, :, :, dh:dh + 1], 1.0)
            nc.vector.tensor_copy(sel[:, :, :], sel32[:, :].unsqueeze(2).to_broadcast([P, H, P])).then_inc(setup, 1)

            def normalize(b):
                for j in range(TB):
                    t = TB * b + j
                    nc.vector.tensor_scalar(xn[:, j, :], X[:, bass.ds(t, 1), :].rearrange("p o d -> p (o d)"),
                                            core.mean[:, bass.ds(t, 1)], core.rstd[:, bass.ds(t, 1)],
                                            ALU.subtract, ALU.mult).then_inc(xn_ready, 1)

            def read_out(k, name, par):
                bank, n = fill(k, name)
                dve.wait_ge(full[bank], n + 1)
                src = pM[bank][:, :]
                if name[0] == "k":
                    c0 = 2 * int(name[1:])
                    if b_k:
                        for c in range(2):
                            ins = nc.vector.tensor_scalar(kT[par][:, c0 + c, :], src[:, c * S:(c + 1) * S],
                                                          bk_col[:, c0 + c:c0 + c + 1], None, ALU.add)
                    else:
                        ins = nc.vector.tensor_copy(kT[par][:, c0:c0 + 2, :], src.rearrange("p (c s) -> p c s", c=2))
                elif name == "v":
                    for j in range(TB):
                        part = src[:, j * DI:(j + 1) * DI].rearrange("p (h d) -> p h d", h=H)
                        if b_v:
                            ins = nc.vector.tensor_tensor(v[par][:, j, :, 0:dh], part,
                                                          bv_row[:, :].rearrange("p (h d) -> p h d", h=H), ALU.add)
                        else:
                            ins = nc.vector.tensor_copy(v[par][:, j, :, 0:dh], part)
                else:
                    j, n = int(name[1]), int(name[2])
                    hh = 512 // dh
                    ins = nc.vector.tensor_copy(v[par][:, j, n * hh:(n + 1) * hh, 0:dh],
                                                src.rearrange("p (h d) -> p h d", h=hh))
                ins.then_inc(free[bank], 1)

            def maximum(b, h):
                dve.wait_ge(s_ready, b * H + h + 1)
                nc.vector.tensor_reduce(mx[:, :, h], pS[h % 2][:, :].rearrange("p (j s) -> p j s", j=TB),
                                        AX.X, ALU.max).then_inc(max_done, 1)

            def split_max(b):
                dve.wait_ge(max_done, (b + 1) * H)
                nc.vector.tensor_scalar(nm[:, :, 0:H], mx[:, :, :], -1.0, None, ALU.mult).then_inc(m_hi, 1)
                dve.wait_ge(m_hi, b + 1)
                nc.vector.scalar_tensor_tensor(nm[:, :, H:2 * H], mx[:, :, :], -1.0, nm[:, :, 0:H],
                                               ALU.mult, ALU.subtract).then_inc(m_lo, 1)
                dve.wait_ge(m_lo, b + 1)
                nc.vector.tensor_copy(nm4[:, :, :, :], nm[:, :, :].unsqueeze(2).to_broadcast([P, TB, 4, 2 * H]))\
                  .then_inc(m_four, 1)

            def divide(b, g):
                dve.wait_ge(pv_done, b * H + (g + 1) * HG)
                for j in range(TB):
                    sums = pO[j][:, 0:HG * W1].rearrange("p (h w) -> p h w", h=HG)[:, :, dh]
                    nc.vector.reciprocal(inv[:, j, g * HG:(g + 1) * HG], sums).then_inc(inv_ready, 1)
                for j in range(TB):
                    part = pO[j][:, 0:HG * W1].rearrange("p (h w) -> p h w", h=HG)[:, :, 0:dh]
                    dve.wait_ge(inv_ready, TB * (b * NG + g) + j + 1)
                    nc.vector.tensor_tensor(o[:, j, g * HG:(g + 1) * HG, :], part,
                                            inv[:, j, g * HG:(g + 1) * HG].unsqueeze(2).to_broadcast([P, HG, dh]),
                                            ALU.mult).then_inc(o_ready, 1)

            def residual(k, j):
                bank, n = fill(k, f"out{j}")
                t = TB * (k - 1) + j
                x_t = X[:, bass.ds(t, 1), :].rearrange("p o d -> p (o d)")
                dve.wait_ge(full[bank], n + 1)
                if b_o:
                    nc.vector.tensor_tensor(out_t[:, j, :], pM[bank][:, 0:D], bo_row[:, :], ALU.add)\
                      .then_inc(free[bank], 1)
                    dve.wait_ge(free[bank], n + 1)
                    if gate:
                        ins = nc.vector.scalar_tensor_tensor(x_t, out_t[:, j, :], gate_col, x_t, ALU.mult, ALU.add)
                    else:
                        ins = nc.vector.tensor_tensor(x_t, out_t[:, j, :], x_t, ALU.add)
                    ins.then_inc(x_new, 1)
                    dve.wait_ge(x_new, t + 1)
                else:
                    nc.vector.tensor_tensor(x_t, pM[bank][:, 0:D], x_t, ALU.add).then_inc(free[bank], 1)
                    dve.wait_ge(free[bank], n + 1)
                nc.vector.bn_stats(core.stats[:, bass.ds(t, 1), :].rearrange("p o d -> p (o d)"), x_t)

            mine = lambda name: name[0] in "kv"
            if gate:
                dve.wait_ge(gate_ready, 1)
            normalize(0)
            for name in begin_fills:
                if mine(name):
                    read_out(-1, name, 0)
            for h in range(H):
                maximum(0, h)
            split_max(0)

            def round_(k, par, half_b, prev=True, nxt=True):
                if nxt:
                    normalize(k + 1)
                for h in range(H):
                    if h >= 2 and (h - 2) % HG == HG - 1:
                        divide(k, (h - 2) // HG)
                    for name in finish_fills:
                        if prev and slot_of[name] == h and name[:3] == "out":
                            residual(k, int(name[3]))
                    for name in begin_fills[:-1]:
                        if nxt and slot_of[name] == h and mine(name):
                            read_out(k, name, 1 - par)
                    if nxt:
                        for hs in heads_at.get(h, ()):
                            maximum(k + 1, hs)
                divide(k, NG - 1)
                if nxt:
                    split_max(k + 1)
            run_rounds(dve, round_)
            for j in range(TB):
                residual(batches, j)

        @block.tensor
        def _(pe):
            def project(dst, w, c0, src):
                for c in range(2):
                    for kc in range(KC):
                        ins = nc.tensor.matmul(dst[:, c * S:(c + 1) * S], w[:, kc, (c0 + c) * P:(c0 + c + 1) * P],
                                               src[:, kc, :], start=kc == 0, stop=kc == KC - 1)
                return ins

            def issue(k, name, par, b, i):
                bank, n = fill(k, name)
                dst = pM[bank]
                if not (isinstance(k, int) and k < 0 and n == 0):
                    pe.wait_ge(free[bank], n)
                if name == "xnT":
                    pe.wait_ge(xn_ready, TB * (b + 1))
                    for c in range(KC):
                        for j in range(TB):
                            ins = nc.tensor.transpose(dst[:, c * S + j * P:c * S + (j + 1) * P],
                                                      xn[:, j, c * P:(c + 1) * P], core.ident[:, :])
                elif name[0] == "q":
                    if name == "q0":
                        pe.wait_ge(free[fill(k, "xnT")[0]], fill(k, "xnT")[1] + 1)
                    ins = project(dst, wq, 2 * int(name[1:]), xnT)
                elif name[0] == "k":
                    if name == "k0":
                        pe.wait_ge(ctx_in[par], 16 * (i + 1))
                    ins = project(dst, wk, 2 * int(name[1:]), ctxT[par])
                elif name == "v":
                    for j in range(TB):
                        for kc in range(KC):
                            ins = nc.tensor.matmul(dst[:, j * DI:(j + 1) * DI], ctxT[par][:, kc, j * P:(j + 1) * P],
                                                   wv[:, kc, :], start=kc == 0, stop=kc == KC - 1)
                elif name[0] == "v":
                    j, hf = int(name[1]), int(name[2])
                    for kc in range(KC):
                        ins = nc.tensor.matmul(dst[:, :], ctxT[par][:, kc, j * P:(j + 1) * P],
                                               wv[:, kc, hf * 512:(hf + 1) * 512], start=kc == 0, stop=kc == KC - 1)
                elif name == "mT":
                    pe.wait_ge(m_four, b + 1)
                    for j in range(TB):
                        ins = nc.tensor.matmul(dst[:, j * P:(j + 1) * P],
                                               nm4[:, j, :, :].rearrange("p r h -> p (r h)"), core.ident_b[:, :],
                                               start=True, stop=True)
                elif name[:2] == "oT":
                    if name == "oT0":
                        pe.wait_ge(o_ready, TB * NG * (b + 1))
                    c0 = 2 * int(name[2:])
                    for c in range(2):
                        for j in range(TB):
                            flat = o[:, j, :, :].rearrange("p h d -> p (h d)")
                            ins = nc.tensor.transpose(dst[:, c * S + j * P:c * S + (j + 1) * P],
                                                      flat[:, (c0 + c) * P:(c0 + c + 1) * P], core.ident[:, :])
                else:
                    j = int(name[3])
                    if j == 0:
                        for c in range(NPAIR):
                            bk, m = fill(k, f"oT{c}")
                            if c >= NPAIR - 2:
                                pe.wait_ge(free[bk], m + 1)
                    for c in range(CH):
                        ins = nc.tensor.matmul(dst[:, 0:D], oT[:, c, j * P:(j + 1) * P], wo[:, c, :],
                                               start=c == 0, stop=c == CH - 1)
                ins.then_inc(full[bank], 1)

            def score(b, h, par):
                if not (isinstance(b, int) and b == 0 and h < 2):
                    pe.wait_ge(max_done, b * H + h - 1)
                hd = head_of(h)
                c, r = rows(hd)
                for j in range(TB):
                    ins = nc.tensor.matmul(pS[h % 2][:, j * S:(j + 1) * S], qT[par][r, q_of(hd), c, j * P:(j + 1) * P],
                                           kT[par][r, c, :], start=True, stop=True)
                ins.then_inc(s_ready, 1)

            def score_T(b, h, par):
                if not (isinstance(b, int) and b == 0 and h < 2):
                    pe.wait_ge(p_ready, b * H + h - 1)
                hd = head_of(h)
                c, r = rows(hd)
                for j in range(TB):
                    out = pT[h % 2][:, j * S:(j + 1) * S]
                    nc.tensor.matmul(out, kT[par][r, c, j * P:(j + 1) * P], qT[par][r, q_of(hd), c, :],
                                     start=True, stop=False)
                    ins = nc.tensor.matmul(out, sel[r, h, :], mT[par][r, :], start=False, stop=True)
                ins.then_inc(t_ready, 1)

            def times_v(b, h, par):
                pe.wait_ge(p_ready, b * H + h + 1)
                if h % HG == 0 and not (isinstance(b, int) and b == 0 and h == 0):
                    pe.wait_ge(o_ready, TB * (b * NG + h // HG))
                hd = head_of(h)
                for j in range(TB):
                    for kt in range(TB):
                        ins = nc.tensor.matmul(pO[j][:, (hd % HG) * W1:(hd % HG + 1) * W1],
                                               probs[h % 4][:, kt, j * P:(j + 1) * P], v[par][:, kt, hd, :],
                                               start=kt == 0, stop=kt == TB - 1)
                ins.then_inc(pv_done, 1)

            def wait_qkv(k):
                for name in begin_fills[-3:-1]:
                    bk, m = fill(k, name)
                    pe.wait_ge(free[bk], m + 1)

            pe.wait_ge(weights_in, 64)
            pe.wait_ge(setup, 1)
            for name in begin_fills[:-1]:
                issue(-1, name, 0, 0, 0)
            wait_qkv(-1)
            for h in range(H):
                score(0, h, 0)
            issue(-1, "mT", 0, 0, 0)

            def round_(k, par, half_b, prev=True, nxt=True):
                bank, n = fill(k - 1, "mT")
                pe.wait_ge(free[bank], n + 1)
                for h in range(H):
                    score_T(k, h, par)
                    if h >= 2:
                        times_v(k, h - 2, par)
                    for name in finish_fills:
                        if prev and slot_of[name] == h:
                            issue(k, name, 1 - par, k - 1, None)
                    for name in begin_fills[:-1]:
                        if nxt and slot_of[name] == h:
                            issue(k, name, 1 - par, k + 1, half_b)
                    if nxt and h == S_SLOTS[0]:
                        wait_qkv(k)
                    if nxt:
                        for hs in heads_at.get(h, ()):
                            score(k + 1, hs, 1 - par)
                for h in (H - 2, H - 1):
                    times_v(k, h, par)
                if nxt:
                    issue(k, "mT", 1 - par, k + 1, half_b)

            run_rounds(pe, round_)
            for name in finish_fills:
                issue(batches, name, (batches - 1) % 2, batches - 1, None)


def staggered(eng, n, round_):
    def flags(k):
        return {d: 0 <= k + d < n for d in range(-2, 4)}
    round_(0, 0, 0, flags(0))
    pairs = (n - 4) // 2
    with eng.Fori(0, pairs) as i:
        round_(2 * i + 1, 1, i, dict.fromkeys(range(-2, 4), True) | {-2: None})
        round_(2 * i + 2, 0, i + 1, dict.fromkeys(range(-2, 4), True) | {-2: None})
    for k in range(2 * pairs + 1, n):
        round_(k, k % 2, k // 2, flags(k))


def flat(ap):
    return ap.rearrange("p o d -> p (o d)")


def ternary_ffn(core):
    nc, X, dram = core.nc, core.X, core.dram
    F = 1024
    FC = F // P
    n = TB * NB_TEST
    with ExitStack() as ctx:
        def sb(name, shape, dt=F32):
            return ctx.enter_context(nc.sbuf_tensor(f"L0f_{name}", shape, dt))

        def ps(name, cols=512):
            return ctx.enter_context(nc.psum_tensor(f"L0f_{name}", [P, cols], F32))

        def sem(name):
            return ctx.enter_context(nc.semaphore(f"L0f_{name}"))

        w32 = [sb(f"w32_{i}", [P, KC * F]) for i in range(3)]
        wint = [sb(f"wint{i}", [P, KC * F], BF16) for i in range(3)]
        ones = sb("ones", [P, P])
        wsum, wmean, wscale = sb("wsum", [P, 3]), sb("wmean", [P, 3]), sb("wscale", [P, 3])
        xn = sb("xn", [P, D])
        amax, qs = sb("amax", [P, 2]), sb("qs", [P, 2])
        dqg, dqu = sb("dqg", [P, 2]), sb("dqu", [P, 2])
        xr = sb("xr", [P, D])
        a = sb("a", [P, 2, D], BF16)
        aT = sb("aT", [P, 2, KC * P], BF16)
        sg = sb("sg", [P, 2, F])
        h = sb("h", [P, F])
        hmax, hqs, hdq = sb("hmax", [P, 2]), sb("hqs", [P, 2]), sb("hdq", [P, 2])
        hr = sb("hr", [P, F])
        hq = sb("hq", [P, F], BF16)
        hT = sb("hT", [P, F], BF16)
        pG = [ps(f"pG{i}") for i in range(2)]
        pU = [ps(f"pU{i}") for i in range(2)]
        pA = ps("pA")
        pH = [ps(f"pH{i}") for i in range(2)]
        pY = ps("pY")

        w_in = [sem(f"w_in{i}") for i in range(3)]
        setup, sums_ready, w_ready = sem("setup"), sem("sums_ready"), sem("w_ready")
        wstep = sem("wstep")
        a_ready = sem("a_ready")
        astep = sem("astep")
        aT_full = sem("aT_full")
        aT_ready = sem("aT_ready")
        g_ready, u_ready = sem("g_ready"), sem("u_ready")
        sg_ready = sem("sg_ready")
        h_ready = sem("h_ready")
        hs_ready = sem("hs_ready")
        hstep = sem("hstep")
        hr_ready = sem("hr_ready")
        hq_ready = sem("hq_ready")
        hT_full = sem("hT_full")
        hT_ready = sem("hT_ready")
        y_ready = sem("y_ready")
        x_new = sem("x_new")

        with nc.Block() as block:
            @block.sync
            def _(sp):
                for i, name in enumerate(("L0f_wg", "L0f_wu")):
                    sp.dma_start(w32[i][:, :].rearrange("p (c n) -> p c n", c=KC),
                                 dram[name].rearrange("(c p) n -> p c n", p=P)).then_inc(w_in[i], 16)
                sp.dma_start(w32[2][:, :].rearrange("p (c n) -> p c n", c=FC),
                             dram["L0f_wd"].rearrange("(c p) n -> p c n", p=P)).then_inc(w_in[2], 16)

            @block.scalar
            def _(act):
                def silu(k, par):
                    for f in range(2):
                        act.wait_ge(g_ready, 2 * k + f + 1)
                        nc.scalar.activation(sg[:, par, f * 512:(f + 1) * 512], pG[f][:, :], ACT.Silu,
                                             scale=dqg[:, par:par + 1]).then_inc(sg_ready, 1)

                def take_aT(k, par):
                    act.wait_ge(aT_full, k + 1)
                    nc.scalar.activation(aT[:, par, :], pA[:, 0:KC * P], ACT.Copy).then_inc(aT_ready, 1)

                def round_(k, par, half, has):
                    act.wait_ge(hs_ready, k + 1)
                    nc.scalar.activation(hr[:, :], h[:, :], ACT.Copy, bias=ROUND, scale=hqs[:, par:par + 1])\
                      .then_inc(hr_ready, 1)
                    if has[1]:
                        silu(k + 1, 1 - par)
                    for f in range(2):
                        act.wait_ge(hT_full, 2 * k + f + 1)
                        nc.scalar.activation(hT[:, f * 512:(f + 1) * 512], pH[f][:, :], ACT.Copy).then_inc(hT_ready, 1)
                    if has[2]:
                        take_aT(k + 2, par)
                take_aT(0, 0)
                take_aT(1, 1)
                silu(0, 0)
                staggered(act, n, round_)

            @block.vector
            def _(dve):
                steps = [0]

                def then_wait(ins):
                    steps[0] += 1
                    ins.then_inc(wstep, 1)
                    dve.wait_ge(wstep, steps[0])

                nc.vector.memset(ones[:, :], 1.0)
                for i in range(3):
                    dve.wait_ge(w_in[i], 16)
                    ins = nc.vector.tensor_reduce(wsum[:, i:i + 1], w32[i][:, :], AX.X, ALU.add,
                                                  apply_absolute_value=True)
                ins.then_inc(setup, 1)
                dve.wait_ge(sums_ready, 1)
                then_wait(nc.vector.tensor_scalar(wmean[:, :], pY[:, 0:3], 1.0 / (D * F), 1e-5, ALU.mult, ALU.max))
                then_wait(nc.vector.reciprocal(wscale[:, :], wmean[:, :]))
                for i in range(3):
                    then_wait(nc.vector.tensor_scalar(w32[i][:, :], w32[i][:, :], wscale[:, i:i + 1], 1.0,
                                                      ALU.mult, ALU.min))
                    then_wait(nc.vector.tensor_scalar(w32[i][:, :], w32[i][:, :], -1.0, ROUND, ALU.max, ALU.add))
                    nc.vector.tensor_scalar(wint[i][:, :], w32[i][:, :], ROUND, None, ALU.subtract).then_inc(w_ready, 1)

                A_STEPS = 7

                def integers(k, par):
                    done = [0]

                    def step(ins):
                        done[0] += 1
                        ins.then_inc(astep, 1)
                        dve.wait_ge(astep, k * A_STEPS + done[0])
                    one = slice(par, par + 1)
                    step(nc.vector.tensor_scalar(xn[:, :], flat(X[:, bass.ds(k, 1), :]), core.mean[:, bass.ds(k, 1)],
                                                 core.rstd[:, bass.ds(k, 1)], ALU.subtract, ALU.mult))
                    step(nc.vector.tensor_reduce(amax[:, one], xn[:, :], AX.X, ALU.max, apply_absolute_value=True))
                    step(nc.vector.tensor_scalar(amax[:, one], amax[:, one], 1e-5, 1.0 / 127.0, ALU.max, ALU.mult))
                    nc.vector.tensor_scalar(dqg[:, one], amax[:, one], wmean[:, 0:1], None, ALU.mult)
                    nc.vector.tensor_scalar(dqu[:, one], amax[:, one], wmean[:, 1:2], None, ALU.mult)
                    step(nc.vector.reciprocal(qs[:, one], amax[:, one]))
                    step(nc.vector.tensor_scalar(xr[:, :], xn[:, :], qs[:, one], ROUND, ALU.mult, ALU.add))
                    nc.vector.tensor_scalar(a[:, par, :], xr[:, :], ROUND, None, ALU.subtract).then_inc(a_ready, 1)
                    assert done[0] == 5
                A_STEPS = 5

                def output(k, par):
                    x_t = flat(X[:, bass.ds(k, 1), :])
                    dve.wait_ge(y_ready, k + 1)
                    nc.vector.scalar_tensor_tensor(x_t, pY[:, 0:D], hdq[:, par:par + 1], x_t, ALU.mult, ALU.add)\
                      .then_inc(x_new, 1)
                    dve.wait_ge(x_new, k + 1)
                    nc.vector.bn_stats(flat(core.stats[:, bass.ds(k, 1), :]), x_t)

                def round_(k, par, half, has):
                    one = slice(par, par + 1)
                    for f in range(2):
                        dve.wait_ge(sg_ready, 2 * k + f + 1)
                        dve.wait_ge(u_ready, 2 * k + f + 1)
                        nc.vector.scalar_tensor_tensor(h[:, f * 512:(f + 1) * 512], pU[f][:, :], dqu[:, one],
                                                       sg[:, par, f * 512:(f + 1) * 512], ALU.mult, ALU.mult)\
                          .then_inc(h_ready, 1)
                    dve.wait_ge(h_ready, 2 * k + 2)
                    nc.vector.tensor_reduce(hmax[:, one], h[:, :], AX.X, ALU.max, apply_absolute_value=True)\
                      .then_inc(hstep, 1)
                    dve.wait_ge(hstep, 2 * k + 1)
                    nc.vector.tensor_scalar(hmax[:, one], hmax[:, one], 1e-5, 1.0 / 127.0, ALU.max, ALU.mult)\
                      .then_inc(hstep, 1)
                    dve.wait_ge(hstep, 2 * k + 2)
                    nc.vector.reciprocal(hqs[:, one], hmax[:, one]).then_inc(hs_ready, 1)
                    nc.vector.tensor_scalar(hdq[:, one], hmax[:, one], wmean[:, 2:3], None, ALU.mult)
                    if has[-1]:
                        output(k - 1, 1 - par)
                    if has[2]:
                        integers(k + 2, par)
                    dve.wait_ge(hr_ready, k + 1)
                    nc.vector.tensor_scalar(hq[:, :], hr[:, :], ROUND, None, ALU.subtract).then_inc(hq_ready, 1)
                integers(0, 0)
                integers(1, 1)
                staggered(dve, n, round_)
                output(n - 1, (n - 1) % 2)

            @block.tensor
            def _(pe):
                def transpose_a(k, par):
                    pe.wait_ge(a_ready, k + 1)
                    if not (isinstance(k, int) and k == 0):
                        pe.wait_ge(aT_ready, k)
                    for c in range(KC):
                        ins = nc.tensor.matmul(pA[:, c * P:(c + 1) * P], a[:, par, c * P:(c + 1) * P],
                                               core.ident_b[:, :], start=True, stop=True)
                    ins.then_inc(aT_full, 1)

                def gate_up(k, par):
                    pe.wait_ge(aT_ready, k + 1)
                    for f in range(2):
                        if not (isinstance(k, int) and k == 0):
                            pe.wait_ge(sg_ready, 2 * k + f - 1)
                            pe.wait_ge(h_ready, 2 * k + f - 1)
                        for w, bank, ready in ((wint[0], pG[f], g_ready), (wint[1], pU[f], u_ready)):
                            for c in range(KC):
                                ins = nc.tensor.matmul(bank[:, :], aT[:, par, c * P:(c + 1) * P],
                                                       w[:, c * F + f * 512:c * F + (f + 1) * 512],
                                                       start=c == 0, stop=c == KC - 1)
                            ins.then_inc(ready, 1)

                def round_(k, par, half, has):
                    if has[1]:
                        gate_up(k + 1, 1 - par)
                    if has[2]:
                        transpose_a(k + 2, par)
                    pe.wait_ge(hq_ready, k + 1)
                    for f in range(2):
                        if not (isinstance(k, int) and k == 0):
                            pe.wait_ge(hT_ready, 2 * k + f - 1)
                        for c in range(4):
                            cc = 4 * f + c
                            ins = nc.tensor.matmul(pH[f][:, c * P:(c + 1) * P], hq[:, cc * P:(cc + 1) * P],
                                                   core.ident_b[:, :], start=True, stop=True)
                        ins.then_inc(hT_full, 1)
                    if not (isinstance(k, int) and k == 0):
                        pe.wait_ge(x_new, k)
                    for cc in range(FC):
                        if cc % 4 == 0:
                            pe.wait_ge(hT_ready, 2 * k + cc // 4 + 1)
                        ins = nc.tensor.matmul(pY[:, 0:D], hT[:, cc * P:(cc + 1) * P], wint[2][:, cc * D:(cc + 1) * D],
                                               start=cc == 0, stop=cc == FC - 1)
                    ins.then_inc(y_ready, 1)
                pe.wait_ge(setup, 1)
                nc.tensor.matmul(pY[:, 0:3], ones[:, :], wsum[:, :], start=True, stop=True).then_inc(sums_ready, 1)
                transpose_a(0, 0)
                transpose_a(1, 1)
                pe.wait_ge(w_ready, 3)
                gate_up(0, 0)
                staggered(pe, n, round_)


def mlstm(core):
    nc, X, dram = core.nc, core.X, core.dram
    NH = 4
    DH = D // NH
    W1 = DH + 1
    HC = S + P
    n = NB_TEST
    FORGET, INPUT = slice(0, NH), slice(32, 32 + NH)
    with ExitStack() as ctx:
        def sb(name, shape, dt=F32):
            return ctx.enter_context(nc.sbuf_tensor(f"L1x_{name}", shape, dt))

        def ps(name):
            return ctx.enter_context(nc.psum_tensor(f"L1x_{name}", [P, 512], F32))

        def sem(name):
            return ctx.enter_context(nc.semaphore(f"L1x_{name}"))

        gk = sb("gk", [P, 3 * KC, 64])
        bias = sb("bias", [NH, 2])
        neg_ib = sb("neg_ib", [NH, 1])
        scale_row = sb("scale_row", [P, D])
        mask32 = sb("mask32", [P, S])
        mask = sb("mask", [P, S], BF16)
        sel = sb("sel", [P, NH, P])
        one4 = sb("one4", [NH, S])
        ctxT = [sb(f"ctxT{i}", [P, KC, S]) for i in range(2)]
        v = [sb(f"v{i}", [P, TB, NH, W1]) for i in range(2)]
        xn = sb("xn", [P, TB, D])
        xnT = [sb(f"xnT{i}", [P, KC, S]) for i in range(2)]
        f_pre, f_abs, f_exp, f_log, lf, F, a_row, FM, E_row = (sb(s, [NH, S]) for s in (
            "f_pre", "f_abs", "f_exp", "f_log", "lf", "F", "a_row", "FM", "E_row"))
        M = [sb(f"M{i}", [P, S]) for i in range(2)]
        tok = [sb(f"tok{i}", [P, TB, 2 * NH]) for i in range(2)]
        decay = sb("decay", [P, 2, HC])
        c_T = sb("c_T", [P, 2, HC])
        norm, inv = sb("norm", [P, TB, NH]), sb("inv", [P, TB, NH])
        hs, hc, sq = (sb(s, [P, TB, NH, DH]) for s in ("hs", "hc", "sq"))
        hsum, var, lnv, r, tmp = (sb(s, [P, TB, NH]) for s in ("hsum", "var", "lnv", "r", "tmp"))
        eps_col = sb("eps_col", [P, 1])
        hy, hz = sb("hy", [P, TB, D]), sb("hz", [P, TB, D])
        pQ = [ps(f"pQ{i}") for i in range(2)]
        pD = [ps(f"pD{i}") for i in range(2)]
        pO = [ps(f"pO{i}") for i in range(TB)]
        pX, pG = ps("pX"), ps("pG")

        small_in, setup = sem("small_in"), sem("setup")
        ctx_in = [sem(f"ctx_in{i}") for i in range(2)]
        v_in = [sem(f"v_in{i}") for i in range(2)]
        xn_ready, xnT_full, xnT_ready = sem("xn_ready"), sem("xnT_full"), sem("xnT_ready")
        gates_full, f_ready, f_abs_ready, f_exp_ready, f_log_ready = (sem(s) for s in (
            "gates_full", "f_ready", "f_abs_ready", "f_exp_ready", "f_log_ready"))
        row_step = sem("row_step")
        E_ready = sem("E_ready")
        tok_full, tok_ready = sem("tok_full"), sem("tok_ready")
        qk_ready, d_ready = sem("qk_ready"), sem("d_ready")
        decay_ready, c_ready, pv_done = sem("decay_ready"), sem("c_ready"), sem("pv_done")
        end_step = sem("end_step")
        sq_ready, ln_ready, r_ready = sem("sq_ready"), sem("ln_ready"), sem("r_ready")
        o_taken, var_sum, newton = sem("o_taken"), sem("var_sum"), sem("newton")
        hy_ready, hz_ready = sem("hy_ready"), sem("hz_ready")
        x_new = sem("x_new")

        with nc.Block() as block:
            @block.sync
            def _(sp):
                sp.dma_start(gk[:, :, :], dram["L1x_gates"].rearrange("(c p) n -> p c n", p=P)).then_inc(small_in, 16)
                for i, name in enumerate(("L1x_fb", "L1x_ib")):
                    sp.dma_start(bias[:, i:i + 1], dram[name].rearrange("(p o) -> p o", o=1),
                                 allow_slow_non_contiguous=True).then_inc(small_in, 16)
                sp.dma_start(scale_row[:, :], dram["L1x_scale"].partition_broadcast(P)).then_inc(small_in, 16)
                sp.dma_start(mask32[:, :], dram["L1x_mask"]).then_inc(small_in, 16)
                sp.dma_start(sel[:, :, :], dram["L1x_sel"]).then_inc(small_in, 16)

                def load(b, par):
                    sp.dma_start(ctxT[par][:, :, :],
                                 dram["ctxT"].rearrange("b (c p) s -> b p c s", p=P)[bass.ds(b, 1)]
                                 .rearrange("o p c s -> p (o c) s")).then_inc(ctx_in[par], 16)
                    for j in range(TB):
                        sp.dma_start(v[par][:, j, :, 0:DH],
                                     dram["ctx"].rearrange("b (j p) (h d) -> b j p h d", p=P, h=NH)[bass.ds(b, 1), j]
                                     .rearrange("o p h d -> p (o h) d")).then_inc(v_in[par], 16)
                sp.wait_ge(setup, 1)
                load(0, 0)
                load(1, 1)

                def round_(k, par, half, has):
                    if has[2]:
                        sp.wait_ge(pv_done, NH * (k + 1))
                        load(k + 2, par)
                staggered(sp, n, round_)

            @block.scalar
            def _(act):
                def begin1(k, par):
                    act.wait_ge(xnT_full, k + 1)
                    nc.scalar.activation(xnT[par][:, :, :], pX[:, :].rearrange("p (c s) -> p c s", c=KC), ACT.Copy)\
                      .then_inc(xnT_ready, 1)

                def begin2(k, par):
                    act.wait_ge(f_ready, k + 1)
                    nc.scalar.activation(f_abs[:, :], f_pre[:, :], ACT.Abs).then_inc(f_abs_ready, 1)
                    act.wait_ge(f_abs_ready, k + 1)
                    nc.scalar.activation(f_exp[:, :], f_abs[:, :], ACT.Exp, scale=-1.0).then_inc(f_exp_ready, 1)
                    act.wait_ge(f_exp_ready, k + 1)
                    nc.scalar.activation(f_log[:, :], f_exp[:, :], ACT.Ln, bias=1.0).then_inc(f_log_ready, 1)

                def begin3(k, par):
                    act.wait_ge(row_step, 5 * k + 5)
                    nc.scalar.activation(E_row[:, :], FM[:, :], ACT.Exp, scale=-1.0, bias=neg_ib[:, :]).then_inc(E_ready, 1)
                    act.wait_ge(tok_full, k + 1)
                    nc.scalar.activation(tok[par][:, :, :],
                                         pG[:, S:S + TB * 2 * NH].rearrange("p (j g) -> p j g", j=TB), ACT.Copy)\
                      .then_inc(tok_ready, 1)

                def head(k, par, h):
                    act.wait_ge(d_ready, k * NH + h + 1)
                    if not (isinstance(k, int) and k == 0 and h < 2):
                        act.wait_ge(c_ready, k * NH + h - 1)
                    nc.scalar.activation(decay[:, h % 2, 0:S], pD[h % 2][:, 0:S], ACT.Exp, bias=tok[par][:, 0, h:h + 1])
                    nc.scalar.activation(decay[:, h % 2, S:HC], pD[h % 2][:, S:HC], ACT.Exp,
                                         bias=tok[par][:, 1, h:h + 1]).then_inc(decay_ready, 1)

                def end(k, par):
                    act.wait_ge(end_step, 6 * k + 6)
                    nc.scalar.activation(sq[:, :, :, :], hc[:, :, :, :], ACT.Square).then_inc(sq_ready, 1)
                    act.wait_ge(ln_ready, k + 1)
                    nc.scalar.activation(lnv[:, :, :], var[:, :, :], ACT.Ln, bias=eps_col[:, :]).then_inc(r_ready, 1)
                    act.wait_ge(r_ready, 2 * k + 1)
                    nc.scalar.activation(r[:, :, :], lnv[:, :, :], ACT.Exp, scale=-0.5).then_inc(r_ready, 1)

                def round_(k, par, half, has):
                    head(k, par, 0)
                    if has[1]:
                        begin1(k + 1, 1 - par)
                    head(k, par, 1)
                    if has[1]:
                        begin2(k + 1, 1 - par)
                    head(k, par, 2)
                    head(k, par, 3)
                    if has[1]:
                        begin3(k + 1, 1 - par)
                    end(k, par)
                act.wait_ge(setup, 1)
                begin1(0, 0)
                begin2(0, 0)
                begin3(0, 0)
                staggered(act, n, round_)

            @block.vector
            def _(dve):
                for i in range(2):
                    nc.vector.memset(M[i][:, :], 0.0)
                    nc.vector.memset(v[i][:, :, :, DH:W1], 1.0)
                nc.vector.memset(one4[:, :], 1.0)
                nc.vector.memset(eps_col[:, :], 1e-6)
                dve.wait_ge(small_in, 16 * 6)
                nc.vector.tensor_copy(mask[:, :], mask32[:, :])
                nc.vector.tensor_scalar(neg_ib[:, :], bias[:, 1:2], -1.0, None, ALU.mult).then_inc(setup, 1)
                dve.wait_ge(setup, 1)

                def begin1(k, par):
                    for j in range(TB):
                        t = TB * k + j
                        ins = nc.vector.tensor_scalar(xn[:, j, :], flat(X[:, bass.ds(t, 1), :]),
                                                      core.mean[:, bass.ds(t, 1)], core.rstd[:, bass.ds(t, 1)],
                                                      ALU.subtract, ALU.mult)
                    ins.then_inc(xn_ready, 1)

                def begin2(k, par):
                    dve.wait_ge(gates_full, k + 1)
                    nc.vector.tensor_scalar(f_pre[:, :], pG[FORGET, 0:S], bias[:, 0:1], None, ALU.add).then_inc(f_ready, 1)

                def begin3(k, par):
                    m = M[par][0:NH, :]
                    dve.wait_ge(f_log_ready, k + 1)
                    nc.vector.scalar_tensor_tensor(lf[:, :], f_pre[:, :], 0.0, f_log[:, :], ALU.min, ALU.subtract)\
                      .then_inc(row_step, 1)
                    dve.wait_ge(row_step, 5 * k + 1)
                    nc.vector.tensor_tensor_scan(F[:, :], one4[:, :], lf[:, :], neg_ib[:, :], ALU.mult, ALU.add)\
                      .then_inc(row_step, 1)
                    dve.wait_ge(row_step, 5 * k + 2)
                    nc.vector.tensor_tensor(a_row[:, :], pG[INPUT, 0:S], F[:, :], ALU.subtract).then_inc(row_step, 1)
                    dve.wait_ge(row_step, 5 * k + 3)
                    nc.vector.tensor_tensor_scan(m, a_row[:, :], a_row[:, :], -3.0e38, ALU.max, ALU.max)\
                      .then_inc(row_step, 1)
                    dve.wait_ge(row_step, 5 * k + 4)
                    nc.vector.tensor_tensor(FM[:, :], F[:, :], m, ALU.add).then_inc(row_step, 1)

                def head(k, par, h):
                    dve.wait_ge(qk_ready, k * NH + h + 1)
                    dve.wait_ge(decay_ready, k * NH + h + 1)
                    if not (isinstance(k, int) and k == 0 and h < 2):
                        dve.wait_ge(pv_done, k * NH + h - 1)
                    nc.vector.scalar_tensor_tensor(c_T[:, h % 2, :], pQ[h % 2][:, 0:HC], DH ** -0.5, decay[:, h % 2, :],
                                                   ALU.mult, ALU.mult).then_inc(c_ready, 1)

                def end(k, par):
                    base = [0]

                    def step(ins):
                        base[0] += 1
                        ins.then_inc(end_step, 1)
                        dve.wait_ge(end_step, 6 * k + base[0])
                    dve.wait_ge(pv_done, NH * (k + 1))
                    for j in range(TB):
                        sums = pO[j][:, 0:NH * W1].rearrange("p (h w) -> p h w", h=NH)[:, :, DH:W1]
                        ins = nc.vector.tensor_reduce(norm[:, j, :], sums, AX.X, ALU.max, apply_absolute_value=True)
                    step(ins)
                    step(nc.vector.tensor_tensor(norm[:, :, :], norm[:, :, :], tok[par][:, :, NH:2 * NH], ALU.max))
                    step(nc.vector.tensor_scalar(norm[:, :, :], norm[:, :, :], 1e-6, None, ALU.add))
                    step(nc.vector.reciprocal(inv[:, :, :], norm[:, :, :]))
                    for j in range(TB):
                        part = pO[j][:, 0:NH * W1].rearrange("p (h w) -> p h w", h=NH)[:, :, 0:DH]
                        ins = nc.vector.tensor_tensor(hs[:, j, :, :], part,
                                                      inv[:, j, :].unsqueeze(2).to_broadcast([P, NH, DH]), ALU.mult)
                    ins.then_inc(o_taken, 1)
                    dve.wait_ge(o_taken, k + 1)
                    step(nc.vector.tensor_reduce(hsum[:, :, :], hs[:, :, :, :], AX.X, ALU.add))
                    nc.vector.scalar_tensor_tensor(
                        hc[:, :, :, :].rearrange("p j h d -> p (j h) d"),
                        hsum[:, :, :].rearrange("p j h -> p (j h)").unsqueeze(2).to_broadcast([P, TB * NH, DH]),
                        -1.0 / DH, hs[:, :, :, :].rearrange("p j h d -> p (j h) d"), ALU.mult, ALU.add)\
                        .then_inc(end_step, 1)
                    dve.wait_ge(sq_ready, k + 1)
                    nc.vector.tensor_reduce(var[:, :, :], sq[:, :, :, :], AX.X, ALU.add).then_inc(var_sum, 1)
                    dve.wait_ge(var_sum, k + 1)
                    nc.vector.tensor_scalar(var[:, :, :], var[:, :, :], 1.0 / DH, None, ALU.mult).then_inc(ln_ready, 1)
                    dve.wait_ge(r_ready, 2 * k + 2)
                    nc.vector.tensor_tensor(tmp[:, :, :], r[:, :, :], r[:, :, :], ALU.mult).then_inc(newton, 1)
                    dve.wait_ge(newton, 4 * k + 1)
                    nc.vector.scalar_tensor_tensor(tmp[:, :, :], var[:, :, :], 1e-6, tmp[:, :, :], ALU.add, ALU.mult)\
                      .then_inc(newton, 1)
                    dve.wait_ge(newton, 4 * k + 2)
                    nc.vector.tensor_scalar(tmp[:, :, :], tmp[:, :, :], -0.5, 1.5, ALU.mult, ALU.add).then_inc(newton, 1)
                    dve.wait_ge(newton, 4 * k + 3)
                    nc.vector.tensor_tensor(r[:, :, :], r[:, :, :], tmp[:, :, :], ALU.mult).then_inc(newton, 1)
                    dve.wait_ge(newton, 4 * k + 4)
                    nc.vector.tensor_tensor(hy[:, :, :].rearrange("p j (h d) -> p (j h) d", h=NH),
                                            hc[:, :, :, :].rearrange("p j h d -> p (j h) d"),
                                            r[:, :, :].rearrange("p j h -> p (j h)").unsqueeze(2)
                                            .to_broadcast([P, TB * NH, DH]), ALU.mult).then_inc(hy_ready, 1)
                    dve.wait_ge(hy_ready, k + 1)
                    nc.vector.tensor_tensor(hz[:, :, :], hy[:, :, :],
                                            scale_row[:, :].unsqueeze(1).to_broadcast([P, TB, D]), ALU.mult)\
                      .then_inc(hz_ready, 1)
                    x_b = X[:, bass.ds(TB * k, TB), :]
                    dve.wait_ge(hz_ready, k + 1)
                    nc.vector.tensor_tensor(x_b, hz[:, :, :], x_b, ALU.add).then_inc(x_new, 1)
                    dve.wait_ge(x_new, k + 1)
                    for j in range(TB):
                        t = TB * k + j
                        nc.vector.bn_stats(flat(core.stats[:, bass.ds(t, 1), :]), flat(X[:, bass.ds(t, 1), :]))

                def round_(k, par, half, has):
                    if has[1]:
                        begin1(k + 1, 1 - par)
                    head(k, par, 0)
                    head(k, par, 1)
                    if has[1]:
                        begin2(k + 1, 1 - par)
                    head(k, par, 2)
                    head(k, par, 3)
                    if has[1]:
                        begin3(k + 1, 1 - par)
                    end(k, par)
                begin1(0, 0)
                begin2(0, 0)
                begin3(0, 0)
                staggered(dve, n, round_)

            @block.tensor
            def _(pe):
                def begin1(k, par):
                    pe.wait_ge(xn_ready, k + 1)
                    for c in range(KC):
                        for j in range(TB):
                            ins = nc.tensor.transpose(pX[:, c * S + j * P:c * S + (j + 1) * P],
                                                      xn[:, j, c * P:(c + 1) * P], core.ident[:, :])
                    ins.then_inc(xnT_full, 1)

                def begin2(k, par, half):
                    pe.wait_ge(xnT_ready, k + 1)
                    pe.wait_ge(ctx_in[par], 16 * (half + 1))
                    if not (isinstance(k, int) and k == 0):
                        pe.wait_ge(tok_ready, k)
                    parts = [xnT[par], ctxT[par], ctxT[par]]
                    for i in range(3 * KC):
                        ins = nc.tensor.matmul(pG[0:64, 0:S], gk[:, i, :], parts[i // KC][:, i % KC, :],
                                               start=i == 0, stop=i == 3 * KC - 1)
                    ins.then_inc(gates_full, 1)

                def begin3(k, par):
                    pe.wait_ge(E_ready, k + 1)
                    for j in range(TB):
                        for g, row in enumerate((a_row, E_row)):
                            at = S + (2 * j + g) * NH
                            ins = nc.tensor.matmul(pG[:, at:at + NH], row[:, j * P:(j + 1) * P], core.ident[0:NH, 0:NH],
                                                   start=True, stop=True)
                    ins.then_inc(tok_full, 1)

                def scores(k, par, h):
                    c, r_ = h // 2, slice((h % 2) * DH, (h % 2 + 1) * DH)
                    if not (isinstance(k, int) and k == 0 and h < 2):
                        pe.wait_ge(c_ready, k * NH + h - 1)
                    nc.tensor.matmul(pQ[h % 2][:, 0:S], ctxT[par][r_, c, 0:P], xnT[par][r_, c, :], start=True, stop=True)
                    nc.tensor.matmul(pQ[h % 2][:, S:HC], ctxT[par][r_, c, P:S], xnT[par][r_, c, P:S],
                                     start=True, stop=True).then_inc(qk_ready, 1)
                    if not (isinstance(k, int) and k == 0 and h < 2):
                        pe.wait_ge(decay_ready, k * NH + h - 1)
                    for cols, queries in ((slice(0, S), slice(0, S)), (slice(S, HC), slice(P, S))):
                        nc.tensor.matmul(pD[h % 2][:, cols], sel[:, h, :], M[par][:, queries], start=True, stop=False)
                        ins = nc.tensor.matmul(pD[h % 2][:, cols], core.ident_b[:, :], mask[:, 0:cols.stop - cols.start],
                                               start=False, stop=True)
                    ins.then_inc(d_ready, 1)

                def times_v(k, par, h):
                    pe.wait_ge(c_ready, k * NH + h + 1)
                    if h == 0 and not (isinstance(k, int) and k == 0):
                        pe.wait_ge(o_taken, k)
                    out = slice(h * W1, (h + 1) * W1)
                    nc.tensor.matmul(pO[0][:, out], c_T[:, h % 2, 0:P], v[par][:, 0, h, :], start=True, stop=True)
                    nc.tensor.matmul(pO[1][:, out], c_T[:, h % 2, P:S], v[par][:, 0, h, :], start=True, stop=False)
                    nc.tensor.matmul(pO[1][:, out], c_T[:, h % 2, S:HC], v[par][:, 1, h, :], start=False, stop=True)\
                      .then_inc(pv_done, 1)

                def round_(k, par, half, has):
                    pe.wait_ge(v_in[par], 32 * (half + 1))
                    scores(k, par, 0)
                    if has[1]:
                        begin1(k + 1, 1 - par)
                    scores(k, par, 1)
                    times_v(k, par, 0)
                    if has[1]:
                        begin2(k + 1, 1 - par, half + par)
                    scores(k, par, 2)
                    times_v(k, par, 1)
                    scores(k, par, 3)
                    times_v(k, par, 2)
                    times_v(k, par, 3)
                    if has[1]:
                        begin3(k + 1, 1 - par)
                pe.wait_ge(setup, 1)
                begin1(0, 0)
                begin2(0, 0, 0)
                begin3(0, 0)
                pe.wait_ge(tok_ready, 1)
                staggered(pe, n, round_)


def routed_low_rank(core):
    nc, X, dram = core.nc, core.X, core.dram
    E, R, PROJ = 4, 8, 64
    TEMP_MAX = float(np.log(1.0 / 0.01))
    n = NB_TEST
    nt = TB * n
    with ExitStack() as ctx:
        def sb(name, shape, dt=F32):
            return ctx.enter_context(nc.sbuf_tensor(f"L1f_{name}", shape, dt))

        xnT = sb("xnT", [P, KC, NT * P])
        zT = sb("zT", [E * R, NT * P])
        logit = sb("logit", [P, NT, E + 1])
        weight = sb("weight", [P, NT, E])
        WT = sb("WT", [P, KC, D])
        WuT = sb("WuT", [P, D])

        first = ExitStack()
        with first:
            def sb1(name, shape, dt=F32):
                return first.enter_context(nc.sbuf_tensor(f"L1f_{name}", shape, dt))

            def sem1(name):
                return first.enter_context(nc.semaphore(f"L1f_{name}"))

            def ps1(name):
                return first.enter_context(nc.psum_tensor(f"L1f_{name}", [P, 512], F32))
            WpdT = sb1("WpdT", [P, KC, PROJ + E * R])
            bp = sb1("bp", [PROJ, 1])
            sim = sb1("sim", [PROJ, E])
            sim_sq, sim_n = sb1("sim_sq", [PROJ, E]), sb1("sim_n", [PROJ, E])
            ones = sb1("ones", [PROJ, PROJ])
            gate_w = sb1("gate_w", [P, E + 1])
            temp = sb1("temp", [P, 1])
            prefer = sb1("prefer", [P, E])
            xn = sb1("xn", [P, TB, D])
            proj = [sb1(f"proj{i}", [P, S]) for i in range(2)]
            root, fac = sb1("root", [P, NT]), sb1("fac", [P, NT])
            top, total = sb1("top", [P, NT]), sb1("total", [P, NT])
            l4, e4, m4 = (sb1(s, [P, NT, E]) for s in ("l4", "e4", "m4"))
            pX, pP, pL = ([ps1(f"{s}{i}") for i in range(2)] for s in ("pX", "pP", "pL"))
            w_in, xn_ready, xT_full, xT_ready = (sem1(s) for s in ("w_in", "xn_ready", "xT_full", "xT_ready"))
            p_full, p_ready, sq_ready, l_full, l_ready, z_ready = (sem1(s) for s in (
                "p_full", "p_ready", "sq_ready", "l_full", "l_ready", "z_ready"))
            ones_ready, sim_sum, sim_root, gate_ready, step, wu_zero = (sem1(s) for s in (
                "ones_ready", "sim_sum", "sim_root", "gate_ready", "step", "wu_zero"))
            root_ready, temp_ready, d_ready, e_ready, n_ready = (sem1(s) for s in (
                "root_ready", "temp_ready", "d_ready", "e_ready", "n_ready"))
            with nc.Block() as block:
                @block.sync
                def _(sp):
                    sp.dma_start(WpdT[:, :, :], dram["L1f_WpdT"].rearrange("(c p) n -> p c n", p=P)).then_inc(w_in, 16)
                    sp.dma_start(bp[:, :], dram["L1f_bp"].rearrange("(p o) -> p o", o=1),
                                 allow_slow_non_contiguous=True).then_inc(w_in, 16)
                    sp.dma_start(sim[:, :], dram["L1f_sim"]).then_inc(w_in, 16)
                    sp.dma_start(temp[:, :], dram["L1f_temp"].partition_broadcast(P)).then_inc(w_in, 16)
                    sp.dma_start(prefer[:, :], dram["L1f_prefer"].partition_broadcast(P)).then_inc(w_in, 16)
                    sp.dma_start(WT[:, :, :], dram["L1f_WT"].rearrange("(c p) n -> p c n", p=P)).then_inc(w_in, 16)
                    sp.wait_ge(wu_zero, 1)
                    sp.dma_start(WuT[0:E * R, :], dram["L1f_WuT"]).then_inc(w_in, 16)
                    sp.wait_ge(w_in, 16 * 7)

                @block.scalar
                def _(act):
                    act.wait_ge(sim_sum, 1)
                    nc.scalar.activation(sim_n[:, :], pP[0][0:PROJ, 0:E], ACT.Sqrt).then_inc(sim_root, 1)

                    def take_xT(k, par):
                        act.wait_ge(xT_full, k + 1)
                        nc.scalar.activation(xnT[:, :, bass.ds(k * S, S)],
                                             pX[par][:, :].rearrange("p (c s) -> p c s", c=KC), ACT.Copy)\
                          .then_inc(xT_ready, 1)

                    def round_(k, par, half, has):
                        if has[1]:
                            take_xT(k + 1, 1 - par)
                        act.wait_ge(p_full, k + 1)
                        if not (isinstance(k, int) and k < 2):
                            act.wait_ge(l_full, k - 1)
                        nc.scalar.activation(proj[par][0:PROJ, :], pP[par][0:PROJ, 0:S], ACT.Identity, bias=bp[:, :])\
                          .then_inc(p_ready, 1)
                        nc.scalar.activation(proj[par][PROJ:P, :], pP[par][0:PROJ, 0:S], ACT.Square, bias=bp[:, :])\
                          .then_inc(sq_ready, 1)
                        nc.scalar.activation(zT[:, bass.ds(k * S, S)], pP[par][PROJ:PROJ + E * R, 0:S], ACT.Copy)\
                          .then_inc(z_ready, 1)
                    take_xT(0, 0)
                    act.wait_ge(w_in, 16 * 7)
                    staggered(act, n, round_)
                    act.wait_ge(n_ready, 1)
                    nc.scalar.activation(root[:, 0:nt], fac[:, 0:nt], ACT.Sqrt).then_inc(root_ready, 1)
                    act.wait_ge(temp_ready, 1)
                    nc.scalar.activation(temp[:, :], temp[:, :], ACT.Exp).then_inc(e_ready, 1)
                    act.wait_ge(d_ready, 1)
                    nc.scalar.activation(e4[:, 0:nt, :], l4[:, 0:nt, :], ACT.Exp).then_inc(e_ready, 1)

                @block.vector
                def _(dve):
                    done = [0]

                    def then_wait(ins):
                        done[0] += 1
                        ins.then_inc(step, 1)
                        dve.wait_ge(step, done[0])

                    nc.vector.memset(ones[:, :], 1.0)
                    nc.vector.memset(WuT[:, :], 0.0).then_inc(wu_zero, 1)
                    nc.vector.memset(gate_w[:, :], 0.0)
                    dve.wait_ge(w_in, 16 * 7)
                    nc.vector.tensor_tensor(sim_sq[:, :], sim[:, :], sim[:, :], ALU.mult).then_inc(ones_ready, 1)
                    nc.vector.tensor_scalar(temp[:, :], temp[:, :], TEMP_MAX, None, ALU.min).then_inc(temp_ready, 1)
                    dve.wait_ge(sim_root, 1)
                    then_wait(nc.vector.tensor_scalar(sim_n[:, :], sim_n[:, :], 1e-12, None, ALU.max))
                    then_wait(nc.vector.reciprocal(sim_sq[:, :], sim_n[:, :]))
                    nc.vector.tensor_tensor(gate_w[0:PROJ, 0:E], sim[:, :], sim_sq[:, :], ALU.mult)
                    nc.vector.memset(gate_w[PROJ:P, E:E + 1], 1.0).then_inc(gate_ready, 1)

                    def normalize(k, par):
                        for j in range(TB):
                            t = TB * k + j
                            ins = nc.vector.tensor_scalar(xn[:, j, :], flat(X[:, bass.ds(t, 1), :]),
                                                          core.mean[:, bass.ds(t, 1)], core.rstd[:, bass.ds(t, 1)],
                                                          ALU.subtract, ALU.mult)
                        ins.then_inc(xn_ready, 1)

                    def round_(k, par, half, has):
                        if has[2]:
                            dve.wait_ge(xT_full, k + 2)
                            normalize(k + 2, par)
                        dve.wait_ge(l_full, k + 1)
                        nc.vector.tensor_copy(logit[:, bass.ds(TB * k, TB), :],
                                              pL[par][:, 0:TB * (E + 1)].rearrange("p (j e) -> p j e", j=TB))\
                          .then_inc(l_ready, 1)
                    normalize(0, 0)
                    dve.wait_ge(xT_full, 1)
                    normalize(1, 1)
                    staggered(dve, n, round_)
                    dve.wait_ge(l_ready, n)
                    nc.vector.tensor_copy(fac[:, 0:nt], logit[:, 0:nt, E]).then_inc(n_ready, 1)
                    dve.wait_ge(root_ready, 1)
                    dve.wait_ge(e_ready, 1)
                    then_wait(nc.vector.tensor_scalar(root[:, 0:nt], root[:, 0:nt], 1e-12, None, ALU.max))
                    then_wait(nc.vector.reciprocal(fac[:, 0:nt], root[:, 0:nt]))
                    then_wait(nc.vector.tensor_scalar(fac[:, 0:nt], fac[:, 0:nt], temp[:, :], None, ALU.mult))
                    wide = lambda ap: ap.unsqueeze(2).to_broadcast([P, nt, E])
                    then_wait(nc.vector.tensor_tensor(l4[:, 0:nt, :], logit[:, 0:nt, 0:E], wide(fac[:, 0:nt]), ALU.mult))
                    then_wait(nc.vector.tensor_reduce(top[:, 0:nt], l4[:, 0:nt, :], AX.X, ALU.max))
                    nc.vector.tensor_tensor(l4[:, 0:nt, :], l4[:, 0:nt, :], wide(top[:, 0:nt]), ALU.subtract)\
                      .then_inc(d_ready, 1)
                    dve.wait_ge(d_ready, 1)
                    then_wait(nc.vector.tensor_scalar(m4[:, 0:nt, :], l4[:, 0:nt, :], 0.0, None, ALU.is_ge))
                    then_wait(nc.vector.tensor_tensor(m4[:, 0:nt, :], m4[:, 0:nt, :],
                                                      prefer[:, :].unsqueeze(1).to_broadcast([P, nt, E]), ALU.mult))
                    then_wait(nc.vector.tensor_reduce(top[:, 0:nt], m4[:, 0:nt, :], AX.X, ALU.max))
                    then_wait(nc.vector.tensor_tensor(m4[:, 0:nt, :], m4[:, 0:nt, :], wide(top[:, 0:nt]), ALU.is_equal))
                    dve.wait_ge(e_ready, 2)
                    then_wait(nc.vector.tensor_reduce(total[:, 0:nt], e4[:, 0:nt, :], AX.X, ALU.add))
                    then_wait(nc.vector.reciprocal(top[:, 0:nt], total[:, 0:nt]))
                    nc.vector.tensor_tensor(weight[:, 0:nt, :], m4[:, 0:nt, :], wide(top[:, 0:nt]), ALU.mult)

                @block.tensor
                def _(pe):
                    pe.wait_ge(ones_ready, 1)
                    nc.tensor.matmul(pP[0][0:PROJ, 0:E], ones[:, :], sim_sq[:, :], start=True, stop=True)\
                      .then_inc(sim_sum, 1)

                    def transpose_x(k, par):
                        pe.wait_ge(xn_ready, k + 1)
                        if not (isinstance(k, int) and k < 2):
                            pe.wait_ge(xT_ready, k - 1)
                        for c in range(KC):
                            for j in range(TB):
                                ins = nc.tensor.transpose(pX[par][:, c * S + j * P:c * S + (j + 1) * P],
                                                          xn[:, j, c * P:(c + 1) * P], core.ident[:, :])
                        ins.then_inc(xT_full, 1)

                    def project(k, par):
                        pe.wait_ge(xT_ready, k + 1)
                        if not (isinstance(k, int) and k < 2):
                            pe.wait_ge(p_ready, k - 1)
                            pe.wait_ge(z_ready, k - 1)
                        for c in range(KC):
                            ins = nc.tensor.matmul(pP[par][0:PROJ + E * R, 0:S], WpdT[:, c, :],
                                                   xnT[:, c, bass.ds(k * S, S)], start=c == 0, stop=c == KC - 1)
                        ins.then_inc(p_full, 1)

                    def gate(k, par):
                        pe.wait_ge(p_ready, k + 1)
                        pe.wait_ge(sq_ready, k + 1)
                        if not (isinstance(k, int) and k < 2):
                            pe.wait_ge(l_ready, k - 1)
                        for j in range(TB):
                            ins = nc.tensor.matmul(pL[par][:, j * (E + 1):(j + 1) * (E + 1)],
                                                   proj[par][:, j * P:(j + 1) * P], gate_w[:, :], start=True, stop=True)
                        ins.then_inc(l_full, 1)

                    def round_(k, par, half, has):
                        if has[1]:
                            transpose_x(k + 1, 1 - par)
                            project(k + 1, 1 - par)
                        gate(k, par)
                    pe.wait_ge(w_in, 16 * 7)
                    pe.wait_ge(sim_root, 1)
                    transpose_x(0, 0)
                    project(0, 0)
                    pe.wait_ge(gate_ready, 1)
                    staggered(pe, n, round_)

        second = ExitStack()
        with second:
            def sb2(name, shape, dt=F32):
                return second.enter_context(nc.sbuf_tensor(f"L1f_{name}", shape, dt))

            def sem2(name):
                return second.enter_context(nc.semaphore(f"L1f_{name}"))

            def ps2(name):
                return second.enter_context(nc.psum_tensor(f"L1f_{name}", [P, 512], F32))
            wide8 = [sb2(f"wide8{i}", [P, TB, E, R]) for i in range(2)]
            zw = [sb2(f"zw{i}", [P, S]) for i in range(2)]
            xTs = [sb2(f"xTs{i}", [P, KC, S]) for i in range(2)]
            pW = [ps2(f"pW{i}") for i in range(2)]
            pY = [ps2(f"pY{i}") for i in range(2)]
            wide_ready, w_full, zw_ready, xs_ready, y_ready, x_new, zero = (sem2(s) for s in (
                "wide_ready", "w_full", "zw_ready", "xs_ready", "y_ready", "x_new", "zero"))
            with nc.Block() as block:
                @block.scalar
                def _(act):
                    def bring(k, par):
                        nc.scalar.activation(xTs[par][:, :, :], xnT[:, :, bass.ds(k * S, S)], ACT.Copy)\
                          .then_inc(xs_ready, 1)

                    def round_(k, par, half, has):
                        if has[2]:
                            act.wait_ge(y_ready, k + 1)
                            bring(k + 2, par)
                    bring(0, 0)
                    bring(1, 1)
                    staggered(act, n, round_)

                @block.vector
                def _(dve):
                    for i in range(2):
                        ins = nc.vector.memset(zw[i][:, :], 0.0)
                    ins.then_inc(zero, 1)
                    dve.wait_ge(zero, 1)

                    def widen(k, par):
                        nc.vector.tensor_copy(wide8[par][:, :, :, :].rearrange("p j e r -> p (j e) r"),
                                              weight[:, bass.ds(TB * k, TB), :].rearrange("p j e -> p (j e)")
                                              .unsqueeze(2).to_broadcast([P, TB * E, R])).then_inc(wide_ready, 1)

                    def round_(k, par, half, has):
                        dve.wait_ge(w_full, k + 1)
                        nc.vector.tensor_tensor(zw[par][0:E * R, :], pW[par][0:E * R, 0:S], zT[:, bass.ds(k * S, S)],
                                                ALU.mult).then_inc(zw_ready, 1)
                        if has[2]:
                            widen(k + 2, par)
                        dve.wait_ge(y_ready, k + 1)
                        x_b = X[:, bass.ds(TB * k, TB), :]
                        nc.vector.tensor_tensor(x_b, pY[par][:, :].rearrange("p (j d) -> p j d", j=TB), x_b, ALU.add)\
                          .then_inc(x_new, 1)
                        dve.wait_ge(x_new, k + 1)
                        for j in range(TB):
                            t = TB * k + j
                            nc.vector.bn_stats(flat(core.stats[:, bass.ds(t, 1), :]), flat(X[:, bass.ds(t, 1), :]))
                    widen(0, 0)
                    widen(1, 1)
                    staggered(dve, n, round_)

                @block.tensor
                def _(pe):
                    def weights(k, par):
                        pe.wait_ge(wide_ready, k + 1)
                        if not (isinstance(k, int) and k < 2):
                            pe.wait_ge(zw_ready, k - 1)
                        for j in range(TB):
                            ins = nc.tensor.transpose(pW[par][0:E * R, j * P:(j + 1) * P],
                                                      wide8[par][:, j, :, :].rearrange("p e r -> p (e r)"),
                                                      core.ident[:, :])
                        ins.then_inc(w_full, 1)

                    def round_(k, par, half, has):
                        if has[1]:
                            weights(k + 1, 1 - par)
                        pe.wait_ge(xs_ready, k + 1)
                        if not (isinstance(k, int) and k < 2):
                            pe.wait_ge(x_new, k - 1)
                        pe.wait_ge(zw_ready, k + 1)
                        for j in range(TB):
                            out = pY[par][:, j * D:(j + 1) * D]
                            for c in range(KC):
                                nc.tensor.matmul(out, xTs[par][:, c, j * P:(j + 1) * P], WT[:, c, :],
                                                 start=c == 0, stop=False)
                            ins = nc.tensor.matmul(out, zw[par][:, j * P:(j + 1) * P], WuT[:, :], start=False, stop=True)
                        ins.then_inc(y_ready, 1)
                    pe.wait_ge(zero, 1)
                    weights(0, 0)
                    staggered(pe, n, round_)


def int8_ffn(core):
    nc, X, dram = core.nc, core.X, core.dram
    F = 704
    FC = -(-F // P)
    n = NB_TEST
    with ExitStack() as ctx:
        def sb(name, shape, dt=F32):
            return ctx.enter_context(nc.sbuf_tensor(f"L2f_{name}", shape, dt))

        def ps(name):
            return ctx.enter_context(nc.psum_tensor(f"L2f_{name}", [P, 512], F32))

        def sem(name):
            return ctx.enter_context(nc.semaphore(f"L2f_{name}"))

        hT = sb("hT", [P, FC, NT * P])
        wg, wu = (sb(n_, [P, KC, FC * P], BF16) for n_ in ("wg", "wu"))
        wd = sb("wd", [P, FC, D], BF16)
        sg_col, su_col = sb("sg_col", [P, FC]), sb("su_col", [P, FC])
        gate_scale, up_scale = sb("gate_scale", [P, FC]), sb("up_scale", [P, FC])
        down_row = sb("down_row", [P, D])
        ones = sb("ones", [P, P])
        xabs = sb("xabs", [P, NT])
        habs = sb("habs", [P, n])
        top = sb("top", [P, 2])
        top_row = sb("top_row", [1, P])
        top_one = sb("top_one", [1, 2])
        clip = sb("clip", [P, 2])
        sx, inv_sx, sh, inv_sh = (sb(n_, [P, 1]) for n_ in ("sx", "inv_sx", "sh", "inv_sh"))

        block1 = ExitStack()
        with block1:
            def sb1(name, shape, dt=F32):
                return block1.enter_context(nc.sbuf_tensor(f"L2f_{name}", shape, dt))
            w32 = [sb1(f"w32_{i}", [P, FC, D]) for i in range(2)]
            wd32 = sb1("wd32", [P, KC, FC * P])
            wr = sb1("wr", [P, FC * D])
            wi = sb1("wi", [P, FC * D], BF16)
            wmax, winv = sb1("wmax", [P, FC]), sb1("winv", [P, FC])
            sd_col = sb1("sd_col", [P, KC])
            diag = sb1("diag", [P, KC, P])
            xt = sb1("xt", [P, TB, D])
            pW = [block1.enter_context(nc.psum_tensor(f"L2f_pW{i}", [P, 512], F32)) for i in range(2)]
            pR = block1.enter_context(nc.psum_tensor("L2f_pR", [P, 512], F32))
            w_in = [block1.enter_context(nc.semaphore(f"L2f_w_in{i}")) for i in range(3)]
            clip_in = block1.enter_context(nc.semaphore("L2f_clip_in"))
            sem1 = lambda name: block1.enter_context(nc.semaphore(f"L2f_{name}"))
            wstep, wi_ready, wT_full, wT_taken = sem1("wstep"), sem1("wi_ready"), sem1("wT_full"), sem1("wT_taken")
            x_step, diag_ready, row_ready, sig_ready = sem1("x_step"), sem1("diag_ready"), sem1("row_ready"), sem1("sig_ready")
            top_ready, topT_ready, one_ready, all_ready = (sem1(s) for s in ("top_ready", "topT_ready", "one_ready",
                                                                          "all_ready"))
            with nc.Block() as block:
                @block.sync
                def _(sp):
                    for i, name in enumerate(("L2f_wg", "L2f_wu")):
                        sp.dma_start(w32[i][:, :, :], dram[name].rearrange("(c p) n -> p c n", p=P)).then_inc(w_in[i], 16)
                    sp.dma_start(wd32[:, :, :], dram["L2f_wd"].rearrange("(c p) n -> p c n", p=P)).then_inc(w_in[2], 16)
                    for i, name in enumerate(("L2f_clip_x", "L2f_clip_down")):
                        sp.dma_start(clip[:, i:i + 1], dram[name].partition_broadcast(P)).then_inc(clip_in, 16)

                plans = [(w32[0], FC, KC, wg), (w32[1], FC, KC, wu), (wd32, KC, FC, wd)]
                blocks = [(i, c, m) for i, (_, rows_, cols_, _) in enumerate(plans)
                          for c in range(rows_) for m in range(cols_)]
                groups = [blocks[j:j + 4] for j in range(0, len(blocks), 4)]

                @block.scalar
                def _(act):
                    act.wait_ge(clip_in, 32)
                    nc.scalar.activation(clip[:, :], clip[:, :], ACT.Sigmoid).then_inc(sig_ready, 1)
                    for g, group in enumerate(groups):
                        act.wait_ge(wT_full, g + 1)
                        for q, (i, c, m) in enumerate(group):
                            ins = nc.scalar.activation(plans[i][3][:, m, c * P:(c + 1) * P],
                                                       pW[g % 2][:, q * P:(q + 1) * P], ACT.Copy)
                        ins.then_inc(wT_taken, 1)

                @block.vector
                def _(dve):
                    steps = [0]

                    def then_wait(ins):
                        steps[0] += 1
                        ins.then_inc(wstep, 1)
                        dve.wait_ge(wstep, steps[0])

                    nc.vector.memset(ones[:, :], 1.0)
                    for i, (w, rows_, cols_, _) in enumerate(plans):
                        width = cols_ * P
                        dve.wait_ge(w_in[i], 16)
                        then_wait(nc.vector.tensor_reduce(wmax[:, 0:rows_], w[:, :, :], AX.X, ALU.max,
                                                          apply_absolute_value=True))
                        scale = (sg_col, su_col, sd_col)[i]
                        then_wait(nc.vector.tensor_scalar(scale[:, 0:rows_], wmax[:, 0:rows_], 1e-30, 1.0 / 127.0,
                                                          ALU.max, ALU.mult))
                        then_wait(nc.vector.reciprocal(winv[:, 0:rows_], scale[:, 0:rows_]))
                        if i:
                            dve.wait_ge(wT_full, sum(1 for group in groups if group[0][0] < i))
                        for c in range(rows_):
                            ins = nc.vector.tensor_scalar(wr[:, c * width:(c + 1) * width], w[:, c, :],
                                                          winv[:, c:c + 1], ROUND, ALU.mult, ALU.add)
                        then_wait(ins)
                        nc.vector.tensor_scalar(wi[:, :], wr[:, :], ROUND, None, ALU.subtract).then_inc(wi_ready, 1)
                    for c in range(KC):
                        ins = nc.vector.tensor_scalar(diag[:, c, :], core.ident[:, :], sd_col[:, c:c + 1], None, ALU.mult)
                    ins.then_inc(diag_ready, 1)
                    dve.wait_ge(row_ready, 1)
                    nc.vector.tensor_copy(down_row[:, :], pR[:, 0:D])
                    with dve.Fori(0, n) as i:
                        for j in range(TB):
                            t = TB * i + j
                            nc.vector.tensor_scalar(xt[:, j, :], flat(X[:, bass.ds(t, 1), :]),
                                                    core.mean[:, bass.ds(t, 1)], core.rstd[:, bass.ds(t, 1)],
                                                    ALU.subtract, ALU.mult).then_inc(x_step, 1)
                            dve.wait_ge(x_step, 2 * t + 1)
                            nc.vector.tensor_reduce(xabs[:, bass.ds(t, 1)], xt[:, j, :], AX.X, ALU.max,
                                                    apply_absolute_value=True).then_inc(x_step, 1)
                    dve.wait_ge(x_step, 2 * TB * n)
                    nc.vector.tensor_reduce(top[:, 0:1], xabs[:, 0:TB * n], AX.X, ALU.max).then_inc(top_ready, 1)
                    dve.wait_ge(topT_ready, 1)
                    nc.vector.tensor_reduce(top_one[:, 0:1], pR[0:1, 256:256 + P], AX.X, ALU.max).then_inc(one_ready, 1)
                    dve.wait_ge(all_ready, 1)
                    dve.wait_ge(sig_ready, 1)
                    then_wait(nc.vector.tensor_scalar(sx[:, :], pR[:, 384:385], clip[:, 0:1], 1.0 / 127.0,
                                                      ALU.mult, ALU.mult))
                    then_wait(nc.vector.reciprocal(inv_sx[:, :], sx[:, :]))
                    nc.vector.tensor_scalar(gate_scale[:, :], sg_col[:, :], sx[:, :], None, ALU.mult)
                    nc.vector.tensor_scalar(up_scale[:, :], su_col[:, :], sx[:, :], None, ALU.mult)
                    nc.vector.tensor_scalar(core.rstd[:, :], core.rstd[:, :], inv_sx[:, :], None, ALU.mult)

                @block.tensor
                def _(pe):
                    seen = -1
                    for g, group in enumerate(groups):
                        if group[-1][0] != seen:
                            seen = group[-1][0]
                            pe.wait_ge(wi_ready, seen + 1)
                        if g >= 2:
                            pe.wait_ge(wT_taken, g - 1)
                        for q, (i, c, m) in enumerate(group):
                            at = (c * plans[i][2] + m) * P
                            ins = nc.tensor.matmul(pW[g % 2][:, q * P:(q + 1) * P], wi[:, at:at + P],
                                                   core.ident_b[:, :], start=True, stop=True)
                        ins.then_inc(wT_full, 1)
                    pe.wait_ge(diag_ready, 1)
                    for c in range(KC):
                        ins = nc.tensor.matmul(pR[:, c * P:(c + 1) * P], ones[:, :], diag[:, c, :],
                                               start=True, stop=True)
                    ins.then_inc(row_ready, 1)
                    pe.wait_ge(top_ready, 1)
                    nc.tensor.transpose(pR[0:1, 256:256 + P], top[:, 0:1], core.ident[:, :]).then_inc(topT_ready, 1)
                    pe.wait_ge(one_ready, 1)
                    nc.tensor.matmul(pR[:, 384:385], ones[0:1, :], top_one[:, 0:1], start=True, stop=True)\
                      .then_inc(all_ready, 1)

        block2 = ExitStack()
        with block2:
            def sb2(name, shape, dt=F32):
                return block2.enter_context(nc.sbuf_tensor(f"L2f_{name}", shape, dt))

            def sem2(name):
                return block2.enter_context(nc.semaphore(f"L2f_{name}"))
            xs = sb2("xs", [P, TB, D])
            xc = sb2("xc", [P, TB, D])
            a = sb2("a", [P, 2, TB, D], BF16)
            aT = sb2("aT", [P, 2, KC, S], BF16)
            sg = sb2("sg", [P, FC, S])
            NP2 = FC // 2
            pA = block2.enter_context(nc.psum_tensor("L2f_pA", [P, 512], F32))
            pG = [block2.enter_context(nc.psum_tensor(f"L2f_pG{i}", [P, 512], F32)) for i in range(NP2)]
            pU = [block2.enter_context(nc.psum_tensor(f"L2f_pU{i}", [P, 512], F32)) for i in range(NP2)]
            astep, a_ready, aT_full, aT_ready = sem2("astep"), sem2("a_ready"), sem2("aT_full"), sem2("aT_ready")
            g_ready, u_ready, sg_ready, h_ready = sem2("g_ready"), sem2("u_ready"), sem2("sg_ready"), sem2("h_ready")
            with nc.Block() as block:
                @block.scalar
                def _(act):
                    def take_aT(k, par):
                        act.wait_ge(aT_full, k + 1)
                        nc.scalar.activation(aT[:, par, :, :], pA[:, :].rearrange("p (c s) -> p c s", c=KC), ACT.Copy)\
                          .then_inc(aT_ready, 1)

                    def round_(k, par, half, has):
                        if has[1]:
                            take_aT(k + 1, 1 - par)
                        for g in range(NP2):
                            act.wait_ge(g_ready, NP2 * k + g + 1)
                            if not (isinstance(k, int) and k == 0):
                                act.wait_ge(h_ready, NP2 * k - NP2 + g + 1)
                            for c in range(2):
                                cc = 2 * g + c
                                ins = nc.scalar.activation(sg[:, cc, :], pG[g][:, c * S:(c + 1) * S], ACT.Silu,
                                                           scale=gate_scale[:, cc:cc + 1])
                            ins.then_inc(sg_ready, 1)
                    take_aT(0, 0)
                    staggered(act, n, round_)

                @block.vector
                def _(dve):
                    def integers(k, par):
                        for j in range(TB):
                            t = TB * k + j
                            nc.vector.tensor_scalar(xs[:, j, :], flat(X[:, bass.ds(t, 1), :]),
                                                    core.mean[:, bass.ds(t, 1)], core.rstd[:, bass.ds(t, 1)],
                                                    ALU.subtract, ALU.mult).then_inc(astep, 1)
                        dve.wait_ge(astep, 3 * k + 2)
                        nc.vector.tensor_scalar(xc[:, :, :], xs[:, :, :], 127.0, -128.0, ALU.min, ALU.max).then_inc(astep, 1)
                        dve.wait_ge(astep, 3 * k + 3)
                        nc.vector.tensor_scalar(a[:, par, :, :], xc[:, :, :], ROUND, ROUND, ALU.add, ALU.subtract)\
                          .then_inc(a_ready, 1)

                    def round_(k, par, half, has):
                        if has[1]:
                            integers(k + 1, 1 - par)
                        for g in range(NP2):
                            dve.wait_ge(sg_ready, NP2 * k + g + 1)
                            dve.wait_ge(u_ready, NP2 * k + g + 1)
                            for c in range(2):
                                cc = 2 * g + c
                                ins = nc.vector.scalar_tensor_tensor(
                                    hT[:, cc, bass.ds(k * S, S)], pU[g][:, c * S:(c + 1) * S],
                                    up_scale[:, cc:cc + 1], sg[:, cc, :], ALU.mult, ALU.mult)
                            ins.then_inc(h_ready, 1)
                        dve.wait_ge(h_ready, NP2 * k + NP2)
                        nc.vector.tensor_reduce(habs[:, bass.ds(k, 1)], hT[:, :, bass.ds(k * S, S)], AX.XY, ALU.max,
                                                apply_absolute_value=True)
                    integers(0, 0)
                    staggered(dve, n, round_)

                @block.tensor
                def _(pe):
                    def transpose_a(k, par):
                        pe.wait_ge(a_ready, k + 1)
                        if not (isinstance(k, int) and k == 0):
                            pe.wait_ge(aT_ready, k)
                        for c in range(KC):
                            for j in range(TB):
                                ins = nc.tensor.matmul(pA[:, c * S + j * P:c * S + (j + 1) * P],
                                                       a[:, par, j, c * P:(c + 1) * P], core.ident_b[:, :],
                                                       start=True, stop=True)
                        ins.then_inc(aT_full, 1)

                    def round_(k, par, half, has):
                        if has[1]:
                            transpose_a(k + 1, 1 - par)
                        pe.wait_ge(aT_ready, k + 1)
                        for g in range(NP2):
                            if not (isinstance(k, int) and k == 0):
                                pe.wait_ge(h_ready, NP2 * k - NP2 + g + 1)
                            for w, bank, ready in ((wg, pG[g], g_ready), (wu, pU[g], u_ready)):
                                for c in range(2):
                                    for kc in range(KC):
                                        cc = 2 * g + c
                                        ins = nc.tensor.matmul(bank[:, c * S:(c + 1) * S],
                                                               w[:, kc, cc * P:(cc + 1) * P], aT[:, par, kc, :],
                                                               start=kc == 0, stop=kc == KC - 1)
                                ins.then_inc(ready, 1)
                    transpose_a(0, 0)
                    staggered(pe, n, round_)

        block3 = ExitStack()
        with block3:
            def sb3(name, shape, dt=F32):
                return block3.enter_context(nc.sbuf_tensor(f"L2f_{name}", shape, dt))

            def sem3(name):
                return block3.enter_context(nc.semaphore(f"L2f_{name}"))
            hr = sb3("hr", [P, 2, FC * S])
            hq = sb3("hq", [P, 2, FC, S], BF16)
            out_scale = sb3("out_scale", [P, D])
            yt = sb3("yt", [P, TB, D])
            pY = [block3.enter_context(nc.psum_tensor(f"L2f_pY{i}", [P, 512], F32)) for i in range(2)]
            pR = block3.enter_context(nc.psum_tensor("L2f_pR3", [P, 512], F32))
            top_ready, topT_ready, one_ready, all_ready = (sem3(s) for s in ("top3", "topT3", "one3", "all3"))
            step3, scales_ready = sem3("step3"), sem3("scales_ready")
            hr_ready, clipped, hq_ready, y_ready, y_taken, x_new = (sem3(s) for s in ("hr_ready", "clipped",
                                                                    "hq_ready", "y_ready", "y_taken", "x_new3"))
            with nc.Block() as block:
                @block.scalar
                def _(act):
                    act.wait_ge(scales_ready, 1)
                    def scale_h(k, par):
                        nc.scalar.activation(hr[:, par, :].rearrange("p (c s) -> p c s", c=FC),
                                             hT[:, :, bass.ds(k * S, S)], ACT.Copy, bias=ROUND, scale=inv_sh[:, :])\
                          .then_inc(hr_ready, 1)

                    def round_(k, par, half, has):
                        if has[2]:
                            act.wait_ge(hq_ready, k + 1)
                            scale_h(k + 2, par)
                    scale_h(0, 0)
                    scale_h(1, 1)
                    staggered(act, n, round_)

                @block.vector
                def _(dve):
                    steps = [0]

                    def then_wait(ins):
                        steps[0] += 1
                        ins.then_inc(step3, 1)
                        dve.wait_ge(step3, steps[0])
                    nc.vector.tensor_reduce(top[:, 1:2], habs[:, :], AX.X, ALU.max).then_inc(top_ready, 1)
                    dve.wait_ge(topT_ready, 1)
                    nc.vector.tensor_reduce(top_one[:, 1:2], pR[0:1, 256:256 + P], AX.X, ALU.max).then_inc(one_ready, 1)
                    dve.wait_ge(all_ready, 1)
                    then_wait(nc.vector.tensor_scalar(sh[:, :], pR[:, 384:385], clip[:, 1:2], 1.0 / 127.0,
                                                      ALU.mult, ALU.mult))
                    nc.vector.reciprocal(inv_sh[:, :], sh[:, :]).then_inc(scales_ready, 1)
                    then_wait(nc.vector.tensor_scalar(out_scale[:, :], down_row[:, :], sh[:, :], None, ALU.mult))

                    def integers(k, par):
                        dve.wait_ge(hr_ready, k + 1)
                        nc.vector.tensor_scalar(hr[:, par, :], hr[:, par, :], ROUND + 127.0, ROUND - 128.0,
                                                ALU.min, ALU.max).then_inc(clipped, 1)
                        dve.wait_ge(clipped, k + 1)
                        nc.vector.tensor_scalar(hq[:, par, :, :].rearrange("p c s -> p (c s)"), hr[:, par, :],
                                                ROUND, None, ALU.subtract).then_inc(hq_ready, 1)

                    def round_(k, par, half, has):
                        if has[1]:
                            integers(k + 1, 1 - par)
                        dve.wait_ge(y_ready, k + 1)
                        for j in range(TB):
                            nc.vector.tensor_tensor(yt[:, j, :], pY[par][:, j * D:(j + 1) * D], out_scale[:, :],
                                                    ALU.mult).then_inc(y_taken, 1)
                        for j in range(TB):
                            x_t = flat(X[:, bass.ds(TB * k + j, 1), :])
                            dve.wait_ge(y_taken, TB * k + j + 1)
                            nc.vector.tensor_tensor(x_t, yt[:, j, :], x_t, ALU.add).then_inc(x_new, 1)
                        for j in range(TB):
                            x_t = flat(X[:, bass.ds(TB * k + j, 1), :])
                            dve.wait_ge(x_new, TB * k + j + 1)
                            nc.vector.bn_stats(flat(core.stats[:, bass.ds(TB * k + j, 1), :]), x_t)
                    integers(0, 0)
                    staggered(dve, n, round_)

                @block.tensor
                def _(pe):
                    pe.wait_ge(top_ready, 1)
                    nc.tensor.transpose(pR[0:1, 256:256 + P], top[:, 1:2], core.ident[:, :]).then_inc(topT_ready, 1)
                    pe.wait_ge(one_ready, 1)
                    nc.tensor.matmul(pR[:, 384:385], ones[0:1, :], top_one[:, 1:2], start=True, stop=True)\
                      .then_inc(all_ready, 1)

                    def round_(k, par, half, has):
                        pe.wait_ge(hq_ready, k + 1)
                        if not (isinstance(k, int) and k < 2):
                            pe.wait_ge(y_taken, TB * k - TB)
                        for j in range(TB):
                            for cc in range(FC):
                                ins = nc.tensor.matmul(pY[par][:, j * D:(j + 1) * D], hq[:, par, cc, j * P:(j + 1) * P],
                                                       wd[:, cc, :], start=cc == 0, stop=cc == FC - 1)
                        ins.then_inc(y_ready, 1)
                    staggered(pe, n, round_)


EXPERTS = 8
TILE = 256
MAX_TILES = 2 * B * S // TILE + EXPERTS


def routed_experts(core):
    nc, X, dram = core.nc, core.X, core.dram
    E, HID = EXPERTS, 1024
    HCH = HID // P
    n = NB_TEST
    nt = TB * n
    gathered, expert_out = core.gathered, core.expert_out
    with ExitStack() as ctx:
        def sb(name, shape, dt=F32):
            return ctx.enter_context(nc.sbuf_tensor(f"L3f_{name}", shape, dt))

        slot = [sb(f"slot{i}", [P, NT], I32) for i in range(2)]
        weight = [sb(f"weight{i}", [P, NT]) for i in range(2)]
        bounds = sb("bounds", [1, 2 * E], I32)
        W1 = [sb(f"W1_{i}", [P, KC, HID]) for i in range(2)]
        W2 = [sb(f"W2_{i}", [P, HCH, D]) for i in range(2)]
        b1 = sb("b1", [P, E, HCH])
        b2 = [sb(f"b2_{i}", [P, D]) for i in range(2)]
        w_in = [ctx.enter_context(nc.semaphore(f"L3f_w_in{i}")) for i in range(2)]
        b1_in = ctx.enter_context(nc.semaphore("L3f_b1_in"))
        y_stored = ctx.enter_context(nc.semaphore("L3f_y_stored"))

        def load_expert(eng, e):
            par = e % 2
            eng.dma_start(W1[par][:, :, :], dram["L3f_W1"][e].rearrange("(c p) n -> p c n", p=P)).then_inc(w_in[par], 16)
            eng.dma_start(W2[par][:, :, :], dram["L3f_W2"][e].rearrange("(c p) n -> p c n", p=P)).then_inc(w_in[par], 16)
            eng.dma_start(b2[par][:, :], dram["L3f_b2"][e].partition_broadcast(P)).then_inc(w_in[par], 16)

        first = ExitStack()
        with first:
            def sb1(name, shape, dt=F32):
                return first.enter_context(nc.sbuf_tensor(f"L3f_{name}", shape, dt))

            def sem1(name):
                return first.enter_context(nc.semaphore(f"L3f_{name}"))

            def ps1(name):
                return first.enter_context(nc.psum_tensor(f"L3f_{name}", [P, 512], F32))
            XN = sb1("XN", [P, NT, D])
            xs = [sb1(f"xs{i}", [P, TB, D]) for i in range(2)]
            xT = [sb1(f"xT{i}", [P, KC, S]) for i in range(2)]
            Wg, bg, prefer = sb1("Wg", [P, KC, E]), sb1("bg", [P, E]), sb1("prefer", [P, E])
            tri, ones = sb1("tri", [P, P]), sb1("ones", [P, P])
            g, p8, hot1, hot2, both, pos = (sb1(s, [P, NT, E]) for s in ("g", "p8", "hot1", "hot2", "both", "pos"))
            top, total, p1, p2 = (sb1(s, [P, NT]) for s in ("top", "total", "p1", "p2"))
            per, cum, cex = (sb1(s, [P, E, NT]) for s in ("per", "cum", "cex"))
            onesT = sb1("onesT", [P, E * NT])
            cnt, tiles, tile_end, tile_start, base = (sb1(s, [P, E]) for s in ("cnt", "tiles", "tile_end",
                                                                               "tile_start", "base"))
            pX, pL = ([ps1(f"{s}{i}") for i in range(2)] for s in ("pX", "pL"))
            pW, pT = ps1("pW"), ps1("pT")
            c_in, xn_ready, xT_full, xT_ready, l_full, l_ready = (sem1(s) for s in (
                "c_in", "xn_ready", "xT_full", "xT_ready", "l_full", "l_ready"))
            step, d_ready, e_ready, counted, slots_ready, ones_ready, scattered = (sem1(s) for s in (
                "step", "d_ready", "e_ready", "counted", "slots_ready", "ones_ready", "scattered"))
            with nc.Block() as block:
                @block.sync
                def _(sp):
                    sp.dma_start(Wg[:, :, :], dram["L3f_Wg"].rearrange("(c p) n -> p c n", p=P)).then_inc(c_in, 16)
                    sp.dma_start(bg[:, :], dram["L3f_bg"].partition_broadcast(P)).then_inc(c_in, 16)
                    sp.dma_start(prefer[:, :], dram["L3f_prefer"].partition_broadcast(P)).then_inc(c_in, 16)
                    sp.dma_start(tri[:, :], dram["L3f_tri"]).then_inc(c_in, 16)
                    sp.dma_start(b1[:, :, :], dram["L3f_b1"].rearrange("e (c p) -> p e c", p=P),
                                 allow_slow_non_contiguous=True).then_inc(b1_in, 16)
                    load_expert(sp, 0)
                    load_expert(sp, 1)

                @block.scalar
                def _(act):
                    def round_(k, par, half, has):
                        act.wait_ge(xT_full, k + 1)
                        if not (isinstance(k, int) and k < 2):
                            act.wait_ge(l_full, k - 1)
                        nc.scalar.activation(xT[par][:, :, :], pX[par][:, :].rearrange("p (c s) -> p c s", c=KC),
                                             ACT.Copy).then_inc(xT_ready, 1)
                    staggered(act, n, round_)
                    act.wait_ge(d_ready, 1)
                    nc.scalar.activation(p8[:, 0:nt, :], g[:, 0:nt, :], ACT.Exp).then_inc(e_ready, 1)
                    act.wait_ge(d_ready, 2)
                    nc.scalar.activation(p2[:, 0:nt], p2[:, 0:nt], ACT.Exp).then_inc(e_ready, 1)

                @block.vector
                def _(dve):
                    nc.vector.memset(ones[:, :], 1.0)
                    nc.vector.memset(onesT[:, :], 1.0).then_inc(ones_ready, 1)

                    def normalize(k, par):
                        for j in range(TB):
                            t = TB * k + j
                            ins = nc.vector.tensor_scalar(xs[par][:, j, :], flat(X[:, bass.ds(t, 1), :]),
                                                          core.mean[:, bass.ds(t, 1)], core.rstd[:, bass.ds(t, 1)],
                                                          ALU.subtract, ALU.mult)
                        ins.then_inc(xn_ready, 1)
                        dve.wait_ge(xn_ready, k + 1)
                        nc.vector.tensor_copy(XN[:, bass.ds(TB * k, TB), :], xs[par][:, :, :])

                    def round_(k, par, half, has):
                        if has[1]:
                            if not (isinstance(k, int) and k < 1):
                                dve.wait_ge(xT_full, k)
                            normalize(k + 1, 1 - par)
                        dve.wait_ge(l_full, k + 1)
                        nc.vector.tensor_tensor(g[:, bass.ds(TB * k, TB), :],
                                                pL[par][:, 0:TB * E].rearrange("p (j e) -> p j e", j=TB),
                                                bg[:, :].unsqueeze(1).to_broadcast([P, TB, E]), ALU.add)\
                          .then_inc(l_ready, 1)
                    normalize(0, 0)
                    dve.wait_ge(c_in, 64)
                    staggered(dve, n, round_)
                    done = [0]

                    def then_wait(ins):
                        done[0] += 1
                        ins.then_inc(step, 1)
                        dve.wait_ge(step, done[0])

                    G, P8, H1, H2, BO, PO = (a[:, 0:nt, :] for a in (g, p8, hot1, hot2, both, pos))
                    wide = lambda ap: ap[:, 0:nt].unsqueeze(2).to_broadcast([P, nt, E])
                    every = lambda ap: ap[:, :].unsqueeze(1).to_broadcast([P, nt, E])
                    tt, red = nc.vector.tensor_tensor, nc.vector.tensor_reduce
                    dve.wait_ge(l_ready, n)
                    then_wait(red(top[:, 0:nt], G, AX.X, ALU.max))
                    tt(G, G, wide(top), ALU.subtract).then_inc(d_ready, 1)
                    dve.wait_ge(e_ready, 1)
                    then_wait(red(total[:, 0:nt], P8, AX.X, ALU.add))
                    then_wait(nc.vector.reciprocal(top[:, 0:nt], total[:, 0:nt]))
                    then_wait(tt(P8, P8, wide(top), ALU.mult))
                    for hot, best in ((H1, p1), (H2, p2)):
                        then_wait(red(best[:, 0:nt], P8, AX.X, ALU.max))
                        then_wait(tt(hot, P8, wide(best), ALU.is_equal))
                        then_wait(tt(hot, hot, every(prefer), ALU.mult))
                        then_wait(red(top[:, 0:nt], hot, AX.X, ALU.max))
                        then_wait(tt(hot, wide(top), every(prefer), ALU.is_equal))
                        if best is p1:
                            then_wait(nc.vector.scalar_tensor_tensor(
                                P8.rearrange("p t e -> p (t e)"), H1.rearrange("p t e -> p (t e)"), -2.0,
                                P8.rearrange("p t e -> p (t e)"), ALU.mult, ALU.add))
                    then_wait(tt(BO, H1, H2, ALU.add))
                    tt(p2[:, 0:nt], p2[:, 0:nt], p1[:, 0:nt], ALU.subtract).then_inc(d_ready, 1)
                    dve.wait_ge(e_ready, 2)
                    then_wait(nc.vector.tensor_scalar(total[:, 0:nt], p2[:, 0:nt], 1.0, None, ALU.add))
                    then_wait(nc.vector.reciprocal(weight[0][:, 0:nt], total[:, 0:nt]))
                    then_wait(tt(weight[1][:, 0:nt], weight[0][:, 0:nt], p2[:, 0:nt], ALU.mult))
                    dve.wait_ge(counted, 1)
                    then_wait(nc.vector.tensor_copy(per[:, :, 0:nt],
                                                    pT[:, 0:nt * E].rearrange("p (t e) -> p e t", e=E)))
                    if nt < NT:
                        then_wait(nc.vector.memset(per[:, :, nt:NT], 0.0))
                    lin = lambda ap: ap[:, :, :].rearrange("p e t -> p (e t)")
                    then_wait(nc.vector.tensor_tensor_scan(lin(cum), onesT[:, :], lin(per), 0.0, ALU.mult, ALU.add))
                    then_wait(tt(cex[:, :, :], cum[:, :, :], per[:, :, :], ALU.subtract))
                    then_wait(tt(cnt[:, :], cum[:, :, NT - 1], cex[:, :, 0], ALU.subtract))
                    then_wait(nc.vector.tensor_scalar(tiles[:, :], cnt[:, :], TILE / 2 - 0.5, 1.0 / TILE, ALU.add, ALU.mult))
                    then_wait(nc.vector.tensor_scalar(tiles[:, :], tiles[:, :], ROUND, ROUND, ALU.add, ALU.subtract))
                    then_wait(nc.vector.tensor_scalar(tiles[:, :], tiles[:, :], 1.0, None, ALU.max))
                    then_wait(nc.vector.tensor_tensor_scan(tile_end[:, :], onesT[:, 0:E], tiles[:, :], 0.0,
                                                           ALU.mult, ALU.add))
                    then_wait(tt(tile_start[:, :], tile_end[:, :], tiles[:, :], ALU.subtract))
                    nc.vector.tensor_copy(bounds[:, 0:E], tile_start[0:1, :])
                    nc.vector.tensor_copy(bounds[:, E:2 * E], tile_end[0:1, :])
                    then_wait(nc.vector.scalar_tensor_tensor(base[:, :], tile_start[:, :], float(TILE), cex[:, :, 0],
                                                             ALU.mult, ALU.subtract))
                    then_wait(tt(PO, pW[:, 0:nt * E].rearrange("p (t e) -> p t e", e=E),
                                 cex[:, :, 0:nt].rearrange("p e t -> p t e"), ALU.add))
                    then_wait(tt(PO, PO, every(base), ALU.add))
                    for i, hot in enumerate((H1, H2)):
                        then_wait(tt(hot, hot, PO, ALU.mult))
                        then_wait(red(top[:, 0:nt], hot, AX.X, ALU.add))
                        nc.vector.tensor_copy(slot[i][:, 0:nt], top[:, 0:nt]).then_inc(slots_ready, 1)
                        dve.wait_ge(slots_ready, i + 1)

                @block.tensor
                def _(pe):
                    pe.wait_ge(c_in, 64)

                    def transpose_x(k, par):
                        pe.wait_ge(xn_ready, k + 1)
                        if not (isinstance(k, int) and k < 2):
                            pe.wait_ge(xT_ready, k - 1)
                        for c in range(KC):
                            for j in range(TB):
                                ins = nc.tensor.transpose(pX[par][:, c * S + j * P:c * S + (j + 1) * P],
                                                          xs[par][:, j, c * P:(c + 1) * P], core.ident[:, :])
                        ins.then_inc(xT_full, 1)

                    def round_(k, par, half, has):
                        if has[1]:
                            transpose_x(k + 1, 1 - par)
                        pe.wait_ge(xT_ready, k + 1)
                        if not (isinstance(k, int) and k < 2):
                            pe.wait_ge(l_ready, k - 1)
                        for j in range(TB):
                            for c in range(KC):
                                ins = nc.tensor.matmul(pL[par][:, j * E:(j + 1) * E], xT[par][:, c, j * P:(j + 1) * P],
                                                       Wg[:, c, :], start=c == 0, stop=c == KC - 1)
                        ins.then_inc(l_full, 1)
                    transpose_x(0, 0)
                    staggered(pe, n, round_)
                    pe.wait_ge(ones_ready, 1)
                    pe.wait_ge(d_ready, 2)
                    chosen = both[:, 0:nt, :].rearrange("p t e -> p (t e)")
                    nc.tensor.matmul(pW[:, 0:nt * E], tri[:, :], chosen, start=True, stop=True)
                    nc.tensor.matmul(pT[:, 0:nt * E], ones[:, :], chosen, start=True, stop=True).then_inc(counted, 1)

                @block.gpsimd
                def _(pool):
                    pool.wait_ge(core.cleared, 32)
                    pool.wait_ge(slots_ready, 2)
                    for t in range(nt):
                        for i in range(2):
                            pool.indirect_dma_start(gathered, bass.IndirectOffsetOnAxis(ap=slot[i][:, t:t + 1], axis=0),
                                                    XN[:, t, :], None).then_inc(scattered, 16)
                    pool.wait_ge(scattered, 16 * 2 * nt)

        second = ExitStack()
        with second:
            def sb2(name, shape, dt=F32):
                return second.enter_context(nc.sbuf_tensor(f"L3f_{name}", shape, dt))

            def sem2(name):
                return second.enter_context(nc.semaphore(f"L3f_{name}"))

            def ps2(name):
                return second.enter_context(nc.psum_tensor(f"L3f_{name}", [P, 512], F32))
            xg = sb2("xg", [P, TB, D])
            xgT = sb2("xgT", [P, KC, TILE])
            hT = sb2("hT", [P, HCH, TILE])
            y = sb2("y", [P, TB, D])
            pX2 = ps2("pX2")
            pH = [ps2(f"pH{i}") for i in range(4)]
            pY = [ps2(f"pY{i}") for i in range(TB)]
            xg_in, T_full, T_ready, y_full, y_ready = (sem2(s) for s in (
                "xg_in", "T_full", "T_ready", "y_full", "y_ready"))
            h_full = [sem2(f"h_full{i}") for i in range(2)]
            h_ready = [sem2(f"h_ready{i}") for i in range(2)]
            HALF = HCH // 2
            with nc.Block() as block:
                def expert_range(eng, e):
                    lo = eng.value_load(bounds[0:1, e:e + 1], min_val=e, max_val=MAX_TILES - 1)
                    hi = eng.value_load(bounds[0:1, E + e:E + e + 1], min_val=e + 1, max_val=MAX_TILES)
                    return lo, hi

                @block.sync
                def _(sp):
                    def load_rows(s):
                        sp.dma_start(xg[:, :, :],
                                     gathered.rearrange("(t j p) d -> t p j d", p=P, j=TB)[bass.ds(s, 1)]
                                     .rearrange("o p j d -> p (o j) d")).then_inc(xg_in, 16)
                    load_rows(0)
                    for e in range(E):
                        lo, hi = expert_range(sp, e)
                        with sp.Fori(lo, hi) as s:
                            sp.wait_ge(T_full, s + 1)
                            load_rows(s + 1)
                            sp.wait_ge(y_ready, s + 1)
                            sp.dma_start(expert_out.rearrange("(t j p) d -> t p j d", p=P, j=TB)[bass.ds(s, 1)]
                                         .rearrange("o p j d -> p (o j) d"), y[:, :, :]).then_inc(y_stored, 16)
                        if e + 2 < E:
                            load_expert(sp, e + 2)

                @block.tensor
                def _(pe):
                    def transpose_rows(s):
                        pe.wait_ge(xg_in, s * 16 + 16)
                        for c in range(KC):
                            for j in range(TB):
                                ins = nc.tensor.transpose(pX2[:, c * TILE + j * P:c * TILE + (j + 1) * P],
                                                          xg[:, j, c * P:(c + 1) * P], core.ident[:, :])
                        ins.then_inc(T_full, 1)
                    transpose_rows(0)
                    for e in range(E):
                        par = e % 2
                        lo, hi = expert_range(pe, e)
                        pe.wait_ge(w_in[par], 48 * (e // 2 + 1))
                        with pe.Fori(lo, hi) as s:
                            pe.wait_ge(T_ready, s + 1)
                            for c in range(HCH):
                                who, m = c % 2, c // 2
                                if c >= 4:
                                    pe.wait_ge(h_ready[who], s * HALF + m - 1)
                                else:
                                    pe.wait_ge(h_ready[who], s * HALF)
                                for kc in range(KC):
                                    ins = nc.tensor.matmul(pH[c % 4][:, 0:TILE], W1[par][:, kc, c * P:(c + 1) * P],
                                                           xgT[:, kc, :], start=kc == 0, stop=kc == KC - 1)
                                ins.then_inc(h_full[who], 1)
                            transpose_rows(s + 1)
                            pe.wait_ge(y_ready, s)
                            for c in range(HCH):
                                pe.wait_ge(h_ready[c % 2], s * HALF + c // 2 + 1)
                                for j in range(TB):
                                    ins = nc.tensor.matmul(pY[j][:, 0:D], hT[:, c, j * P:(j + 1) * P],
                                                           W2[par][:, c, :], start=c == 0, stop=c == HCH - 1)
                            ins.then_inc(y_full, 1)

                @block.scalar
                def _(act):
                    act.wait_ge(b1_in, 16)

                    def take_T(s):
                        act.wait_ge(T_full, s + 1)
                        nc.scalar.activation(xgT[:, :, :], pX2[:, :].rearrange("p (c s) -> p c s", c=KC), ACT.Copy)\
                          .then_inc(T_ready, 1)
                    take_T(0)
                    for e in range(E):
                        lo, hi = expert_range(act, e)
                        with act.Fori(lo, hi) as s:
                            for m in range(HALF):
                                c = 2 * m
                                act.wait_ge(h_full[0], s * HALF + m + 1)
                                nc.scalar.activation(hT[:, c, :], pH[c % 4][:, 0:TILE], ACT.Relu, bias=b1[:, e, c:c + 1])\
                                  .then_inc(h_ready[0], 1)
                            take_T(s + 1)

                @block.vector
                def _(dve):
                    dve.wait_ge(b1_in, 16)
                    for e in range(E):
                        lo, hi = expert_range(dve, e)
                        dve.wait_ge(w_in[e % 2], 48 * (e // 2 + 1))
                        with dve.Fori(lo, hi) as s:
                            for m in range(HALF):
                                c = 2 * m + 1
                                dve.wait_ge(h_full[1], s * HALF + m + 1)
                                nc.vector.tensor_scalar(hT[:, c, :], pH[c % 4][:, 0:TILE], b1[:, e, c:c + 1], 0.0,
                                                        ALU.add, ALU.max).then_inc(h_ready[1], 1)
                            dve.wait_ge(y_full, s + 1)
                            dve.wait_ge(y_stored, s * 16)
                            for j in range(TB):
                                ins = nc.vector.tensor_tensor(y[:, j, :], pY[j][:, 0:D], b2[e % 2][:, :], ALU.add)
                            ins.then_inc(y_ready, 1)

        third = ExitStack()
        with third:
            RING = 4
            yg = third.enter_context(nc.sbuf_tensor("L3f_yg", [P, RING, 2, D], F32))
            part = third.enter_context(nc.sbuf_tensor("L3f_part", [P, 2, D], F32))
            yg_in = [third.enter_context(nc.semaphore(f"L3f_yg_in{i}")) for i in range(RING)]
            part_ready = third.enter_context(nc.semaphore("L3f_part_ready"))
            x_new = third.enter_context(nc.semaphore("L3f_x_new"))
            all_stored = third.enter_context(nc.semaphore("L3f_all_stored"))
            with nc.Block() as block:
                @block.gpsimd
                def _(pool):
                    pool.wait_ge(all_stored, 1)
                    for t in range(nt):
                        if t >= RING:
                            pool.wait_ge(x_new, t - RING + 1)
                        for i in range(2):
                            pool.indirect_dma_start(yg[:, t % RING, i, :], None, expert_out,
                                                    bass.IndirectOffsetOnAxis(ap=slot[i][:, t:t + 1], axis=0))\
                                .then_inc(yg_in[t % RING], 16)

                @block.vector
                def _(dve):
                    tiles_all = dve.value_load(bounds[0:1, 2 * E - 1:2 * E], min_val=E, max_val=MAX_TILES)
                    dve.wait_ge(y_stored, tiles_all * 16)
                    nc.vector.memset(part[:, 0, 0:1], 0.0).then_inc(all_stored, 1)
                    dve.wait_ge(all_stored, 1)
                    for t in range(nt):
                        dve.wait_ge(yg_in[t % RING], 32 * (t // RING + 1))
                        nc.vector.scalar_tensor_tensor(part[:, t % 2, :], yg[:, t % RING, 0, :], weight[0][:, t:t + 1],
                                                       X[:, t, :], ALU.mult, ALU.add).then_inc(part_ready, 1)
                        dve.wait_ge(part_ready, t + 1)
                        nc.vector.scalar_tensor_tensor(X[:, t, :], yg[:, t % RING, 1, :], weight[1][:, t:t + 1],
                                                       part[:, t % 2, :], ALU.mult, ALU.add).then_inc(x_new, 1)


def build(nc, dram, batches=B):
    with ExitStack() as ctx:
        core = Core(nc, ctx, dram)
        load_residual(core)
        norm_params(core, "NL0X")
        attention(core, "L0x", 16, "L0_wq", "L0_wk", "L0_wv", "L0_wo", 0.25, "L0_bq", "L0_bk", "L0_bv", "L0_bo", clear=True)
        norm_params(core, "NL0F")
        ternary_ffn(core)
        reuse_semaphores(core)
        norm_params(core, "NL1X")
        mlstm(core)
        norm_params(core, "NL1F")
        routed_low_rank(core)
        reuse_semaphores(core)
        norm_params(core, "NL2X", second_eps=1e-5)
        attention(core, "L2x", 64, "L2_wq", "L2_wk", "L2_wv", "L2_wo", 0.125, b_o="L2_bo",
                  gamma="L2_gamma", beta="L2_beta", gate="L2_gate")
        reuse_semaphores(core)
        norm_params(core, "NL2F")
        int8_ffn(core)
        reuse_semaphores(core)
        norm_params(core, "NL3X")
        attention(core, "L3x", 16, "L3_wq", "L3_wk", "L3_wk", "L3_wo", 0.25)
        norm_params(core, "NL3F")
        routed_experts(core)
        store_residual(core)


def kernel(**inputs):
    import concourse.bacc as bacc
    from concourse.bass_utils import run_bass_kernel_spmd as run

    a = {k: np.asarray(x) for k, x in inputs.items()}
    t = lambda w: np.ascontiguousarray(w.T)

    def head_major(w):
        return np.ascontiguousarray(w.reshape(w.shape[0], D // H, H).transpose(0, 2, 1).reshape(w.shape[0], D))

    arrays = {
        "x": a["x"], "ctx": a["ctx_1024"], "ctxT": np.ascontiguousarray(a["ctx_1024"].transpose(0, 2, 1)),
        "ident": np.eye(P, dtype=np.float32),
        "head_masks": np.stack([(np.arange(P) // 16 % 2 == e) for e in range(2)], 1).astype(np.float32),
        "head_select16": (np.arange(P)[:, None] % H == np.arange(H)).astype(np.float32),
        "head_select64": ((np.arange(P)[:, None] % H == np.arange(H)) & (np.arange(P)[:, None] % 64 < 32))
                         .astype(np.float32),
        "L0_wq": t(a["L0_xattn_w_q"]), "L0_wk": t(a["L0_xattn_w_k"]), "L0_wv": t(a["L0_xattn_w_v"]),
        "L0_wo": t(a["L0_xattn_w_o"]), "L0_bq": a["L0_xattn_b_q"], "L0_bk": a["L0_xattn_b_k"],
        "L0_bv": a["L0_xattn_b_v"], "L0_bo": a["L0_xattn_b_o"],
        "L2_wq": a["L2_xattn_w_q"], "L2_wk": np.ascontiguousarray(a["L2_xattn_w_kv"][:, :1024]),
        "L2_wv": np.ascontiguousarray(a["L2_xattn_w_kv"][:, 1024:]), "L2_wo": a["L2_xattn_w_out"],
        "L2_bo": a["L2_xattn_b_out"], "L2_gate": a["L2_xattn_gate"], "L2_gamma": a["L2_xattn_ln_gamma"],
        "L2_beta": a["L2_xattn_ln_beta"],
        "L3_wq": head_major(t(a["L3_xattn_Wq"])), "L3_wk": head_major(t(a["L3_xattn_Wk"])),
        "L3_wo": np.ascontiguousarray(head_major(a["L3_xattn_Wo"]).T),
        "L0f_wg": t(a["L0_ffn_w_gate"]), "L0f_wu": t(a["L0_ffn_w_up"]), "L0f_wd": t(a["L0_ffn_w_down"]),
        "L2f_wg": np.pad(a["L2_ffn_w_gate"], ((0, 64), (0, 0))), "L2f_wu": np.pad(a["L2_ffn_w_up"], ((0, 64), (0, 0))),
        "L2f_wd": np.pad(a["L2_ffn_w_down"], ((0, 0), (0, 64))),
        "L2f_clip_x": a["L2_ffn_clip_x"], "L2f_clip_down": a["L2_ffn_clip_down"],
        "L1x_gates": np.concatenate([np.pad(a["L1_xattn_fgate_kernel"], ((0, 0), (0, 28))),
                                     np.pad(a["L1_xattn_igate_kernel"], ((0, 0), (0, 28)))], 1),
        "L1x_fb": a["L1_xattn_fgate_bias"], "L1x_ib": a["L1_xattn_igate_bias"], "L1x_scale": a["L1_xattn_outnorm_scale"],
        "L1x_mask": np.where(np.arange(P)[:, None] > np.arange(S)[None, :], -1e30, 0.0).astype(np.float32),
        "L1x_sel": -np.repeat((np.arange(P)[:, None] == np.arange(4)[None, :])[:, :, None], P, 2).astype(np.float32),
        "L1f_WpdT": np.concatenate([t(a["L1_ffn_Wp"])] + [np.pad(t(a[f"L1_ffn_Wd{e}"]), ((0, 0), (0, 8 - 2 ** e)))
                                                          for e in range(4)], 1),
        "L1f_WuT": np.concatenate([np.pad(t(a[f"L1_ffn_Wu{e}"]), ((0, 8 - 2 ** e), (0, 0))) for e in range(4)], 0),
        "L1f_WT": t(a["L1_ffn_W"]), "L1f_bp": a["L1_ffn_bp"], "L1f_sim": a["L1_ffn_sim"], "L1f_temp": a["L1_ffn_temp"],
        "L1f_prefer": np.arange(4, 0, -1).astype(np.float32),
        "L3f_W1": a["L3_ffn_W1"], "L3f_b1": a["L3_ffn_b1"], "L3f_W2": a["L3_ffn_W2"], "L3f_b2": a["L3_ffn_b2"],
        "L3f_Wg": a["L3_ffn_Wg"], "L3f_bg": a["L3_ffn_bg"], "L3f_prefer": np.arange(8, 0, -1).astype(np.float32),
        "L3f_tri": (np.arange(P)[:, None] < np.arange(P)[None, :]).astype(np.float32),
    }
    nc = bacc.Bacc("TRN2", target_bir_lowering=False, num_devices=1)
    dram = {n: nc.dram_tensor(f"in_{n}", x.shape, mybir.dt.from_np(x.dtype), kind="ExternalInput").ap()
            for n, x in arrays.items()}
    dram["out"] = nc.dram_tensor("out", a["x"].shape, F32, kind="ExternalOutput").ap()
    build(nc, dram)
    r = run(nc, [{f"in_{n}": x for n, x in arrays.items()}], core_ids=[0])
    return r.results[0]["out"]
```

```python
from contextlib import ExitStack

import numpy as np

import concourse.bass as bass
from concourse import mybir

P = 128
B = 16
S = 256
D = 256
TB = S // P
NT = B * TB
KC = D // P
H = 16

F32 = mybir.dt.float32
BF16 = mybir.dt.bfloat16
EXPERTS = 8
TILE = 256
MAX_TILES = 2 * B * S // TILE + EXPERTS
I32 = mybir.dt.int32
ALU = mybir.AluOpType
ACT = mybir.ActivationFunctionType
AX = mybir.AxisListType
ROUND = 12582912.0


class Core:

    def __init__(self, nc, ctx, dram):
        self.nc, self.dram = nc, dram
        self.X = ctx.enter_context(nc.sbuf_tensor("X", [P, NT, D], F32))
        self.stats = ctx.enter_context(nc.sbuf_tensor("stats", [P, NT, 6], F32))
        self.mean = ctx.enter_context(nc.sbuf_tensor("mean", [P, NT], F32))
        self.rstd = ctx.enter_context(nc.sbuf_tensor("rstd", [P, NT], F32))
        self.ident = ctx.enter_context(nc.sbuf_tensor("ident", [P, P], F32))
        self.ident_b = ctx.enter_context(nc.sbuf_tensor("ident_b", [P, P], BF16))
        self.gathered = nc.dram_tensor("tokens_by_expert", [(MAX_TILES + 1) * TILE, D], F32, kind="Internal").ap()
        self.expert_out = nc.dram_tensor("expert_outputs", [MAX_TILES * TILE, D], F32, kind="Internal").ap()
        self.cleared = ctx.enter_context(nc.semaphore("cleared"))
        self.zeros = ctx.enter_context(nc.sbuf_tensor("zero_row", [P, D], F32))

    def clear(self, eng):
        def zero(dst):
            eng.dma_start(dst.rearrange("(r p) d -> p r d", p=P),
                          self.zeros[:, :].unsqueeze(1).to_broadcast([P, dst.shape[0] // P, D]))\
               .then_inc(self.cleared, 16)
        zero(self.gathered)
        zero(self.expert_out[2 * B * S // TILE * TILE:, :])


def load_residual(core):
    nc, X, stats = core.nc, core.X, core.stats
    with ExitStack() as ctx:
        x_in = [ctx.enter_context(nc.semaphore(f"x_in{q}")) for q in range(4)]
        ident_in = ctx.enter_context(nc.semaphore("ident_in"))
        x_view = core.dram["x"].rearrange("b (j p) d -> p (b j) d", p=P)
        quarter = NT // 4
        with nc.Block() as block:
            @block.sync
            def _(sp):
                for q in range(4):
                    part = slice(q * quarter, (q + 1) * quarter)
                    sp.dma_start(X[:, part, :], x_view[:, part, :]).then_inc(x_in[q], 16)
                sp.dma_start(core.ident[:, :], core.dram["ident"]).then_inc(ident_in, 16)

            @block.vector
            def _(dve):
                nc.vector.memset(core.zeros[:, :], 0.0)
                dve.wait_ge(ident_in, 16)
                nc.vector.tensor_copy(core.ident_b[:, :], core.ident[:, :])
                for q in range(4):
                    dve.wait_ge(x_in[q], 16)
                    for t in range(q * quarter, (q + 1) * quarter):
                        nc.vector.bn_stats(stats[:, t, :], X[:, t, :])


def norm_params(core, tag, eps=1e-5, second_eps=None):
    nc, stats, mean, rstd = core.nc, core.stats, core.mean, core.rstd
    with ExitStack() as ctx:
        def sb(name):
            return ctx.enter_context(nc.sbuf_tensor(f"{tag}_{name}", [P, NT], F32))
        half_diff, var, root, tmp, first = sb("half_diff"), sb("norm_var"), sb("root"), sb("tmp"), sb("first_rstd")
        step = ctx.enter_context(nc.semaphore(f"{tag}_step"))
        var_ready = ctx.enter_context(nc.semaphore(f"{tag}_var_ready"))
        root_ready = ctx.enter_context(nc.semaphore(f"{tag}_root_ready"))
        rounds = [(eps, rstd)] if second_eps is None else [(eps, first), (second_eps, rstd)]
        with nc.Block() as block:
            @block.scalar
            def _(act):
                for r in range(len(rounds)):
                    act.wait_ge(var_ready, r + 1)
                    nc.scalar.activation(root[:, :], var[:, :], ACT.Sqrt).then_inc(root_ready, 1)

            @block.vector
            def _(dve):
                done = [0]

                def then_wait(ins):
                    done[0] += 1
                    ins.then_inc(step, 1)
                    dve.wait_ge(step, done[0])

                mean_e, m2_e, mean_o, m2_o = stats[:, :, 1], stats[:, :, 2], stats[:, :, 4], stats[:, :, 5]
                then_wait(nc.vector.tensor_tensor(mean[:, :], mean_e, mean_o, ALU.add))
                then_wait(nc.vector.tensor_scalar(mean[:, :], mean[:, :], 0.5, None, ALU.mult))
                then_wait(nc.vector.tensor_tensor(half_diff[:, :], mean_e, mean_o, ALU.subtract))
                then_wait(nc.vector.scalar_tensor_tensor(half_diff[:, :], half_diff[:, :], 0.25, half_diff[:, :],
                                                         ALU.mult, ALU.mult))
                then_wait(nc.vector.tensor_tensor(var[:, :], m2_e, m2_o, ALU.add))
                then_wait(nc.vector.scalar_tensor_tensor(var[:, :], var[:, :], 1.0 / D, half_diff[:, :],
                                                         ALU.mult, ALU.add))
                for r, (add, result) in enumerate(rounds):
                    if r:
                        then_wait(nc.vector.tensor_tensor(var[:, :], half_diff[:, :], first[:, :], ALU.mult))
                        then_wait(nc.vector.tensor_tensor(var[:, :], var[:, :], first[:, :], ALU.mult))
                    else:
                        then_wait(nc.vector.tensor_copy(half_diff[:, :], var[:, :]))
                    then_wait(nc.vector.tensor_scalar(var[:, :], var[:, :], add, None, ALU.add))
                    nc.vector.tensor_copy(tmp[:, :], var[:, :]).then_inc(var_ready, 1)
                    dve.wait_ge(root_ready, r + 1)
                    then_wait(nc.vector.reciprocal(result[:, :], root[:, :]))
                    then_wait(nc.vector.tensor_tensor(tmp[:, :], result[:, :], result[:, :], ALU.mult))
                    then_wait(nc.vector.tensor_tensor(tmp[:, :], tmp[:, :], var[:, :], ALU.mult))
                    then_wait(nc.vector.tensor_scalar(tmp[:, :], tmp[:, :], -0.5, 1.5, ALU.mult, ALU.add))
                    then_wait(nc.vector.tensor_tensor(result[:, :], result[:, :], tmp[:, :], ALU.mult))
                if second_eps is not None:
                    then_wait(nc.vector.tensor_tensor(rstd[:, :], rstd[:, :], first[:, :], ALU.mult))


def reuse_semaphores(core):
    ended = sorted(core.nc.released_uncleared_semaphores)
    with core.nc.Block() as block:
        @block.sync
        def _(sp):
            first = 0
            for i in range(1, len(ended) + 1):
                if i == len(ended) or ended[i] != ended[i - 1] + 1:
                    sp.sem_clear(range(ended[first], ended[i - 1] + 1))
                    first = i


def store_residual(core):
    nc, X = core.nc, core.X
    with nc.semaphore("out_stored") as out_stored, nc.Block() as block:
        @block.sync
        def _(sp):
            sp.dma_start(core.dram["out"].rearrange("b (j p) d -> p (b j) d", p=P), X[:, :, :])\
              .then_inc(out_stored, 16)
            sp.wait_ge(out_stored, 16)


def attention(core, tag, dh, w_q, w_k, w_v, w_o, scale, b_q=None, b_k=None, b_v=None, b_o=None,
              gamma=None, beta=None, gate=None, clear=False):
    nc, X, dram = core.nc, core.X, core.dram
    DI = H * dh
    CH = DI // P
    HPC = P // dh
    HPG = 64 // dh
    GW = HPG * (P + dh) if HPG > 1 else P
    HG = 2 * HPG
    stacked = dh == 16
    NPAIR = CH // 2
    VH = max(1, DI // 512)

    finish_fills = ["out01"] if stacked else ["out0", "out1"]
    v_fills = ["v"] if stacked else [f"v{j}{n}" for j in range(TB) for n in range(VH)]
    qk_fills = ["k0", "q0"] if NPAIR == 1 else ["k0", "k1", "q0", "k2", "q1", "k3", "q2", "q3"]
    begin_fills = ["xnT"] + qk_fills + v_fills + ["mT"]
    nF, nP = len(finish_fills), len(begin_fills)
    assert (nF + nP) % 2 == 0
    ahead = 3 if stacked else 6
    round_fills = begin_fills[:ahead] + finish_fills + begin_fills[ahead:-1]
    slot_of = {f: (0 if stacked else 1) + n * 5 // len(round_fills) for n, f in enumerate(round_fills)}
    LAG_PV, LAG_DIVIDE = 2, 3
    S_SLOTS = range(8 if stacked else 6, 14)
    heads_at = {s: [h for h in range(H) if S_SLOTS[h * len(S_SLOTS) // H] == s] for s in S_SLOTS}

    with ExitStack() as ctx:
        def sb(name, shape, dt=F32):
            return ctx.enter_context(nc.sbuf_tensor(f"{tag}_{name}", shape, dt))

        def ps(name, shape=(P, 512)):
            return ctx.enter_context(nc.psum_tensor(f"{tag}_{name}", list(shape), F32))

        def sem(name):
            return ctx.enter_context(nc.semaphore(f"{tag}_{name}"))

        wq, wk, wv = (sb(n, [P, KC, DI]) for n in ("wq", "wk", "wv"))
        wo = sb("wo", [P, CH, D])
        vec = sb("vec", [P, 3 * CH + 2 * KC + 1])
        bq_col, bk_col = vec[:, 0:CH], vec[:, CH:2 * CH]
        gam, bet = vec[:, 3 * CH:3 * CH + KC], vec[:, 3 * CH + KC:3 * CH + 2 * KC]
        gate_col = vec[:, 3 * CH + 2 * KC:3 * CH + 2 * KC + 1]
        bv_row = sb("bv_row", [P, DI]) if b_v else None
        bo_row = sb("bo_row", [P, D])
        sel32 = sb("sel32", [P, H])
        Q_TERMS = ((0, 3, 0), (3, 3, 0), (6, 2, 0))
        K_TERMS = tuple((t, 1, part) for t, part in enumerate((0, 0, 0, 1, 1, 1, 2, 2)))
        STACK_DMAS = len(Q_TERMS) + len(K_TERMS)
        sel = sb("sel", [P, H, P], BF16)
        ctxT = [sb(f"ctxT{i}", [P, KC, S]) for i in range(2)]
        xn = sb("xn", [P, TB, D])
        xnT = sb("xnT", [P, KC, S])
        if stacked:
            qT, kT = ([sb(name, [P, CH, S])] * 2 for name in ("qT", "kT"))
            q_parts, k_parts = (sb(name, [P, CH, 3, S], BF16) for name in ("q_parts", "k_parts"))
            q_rest, k_rest = (sb(name, [P, CH, S]) for name in ("q_rest", "k_rest"))
            q_stack, k_stack = ([sb(f"{name}{i}", [P, H, S], BF16) for i in range(2)] for name in ("q_stack", "k_stack"))
            q_dram, k_dram = (nc.dram_tensor(f"{tag}_{name}", [CH, 3, P, S], BF16, kind="Internal").ap()
                              for name in ("q_parts_dram", "k_parts_dram"))
        else:
            qT, kT = ([sb(f"{name}{i}", [P, CH, S]) for i in range(2)] for name in ("qT", "kT"))
            q_b, kT_b = (sb(name, [P, CH, S], BF16) for name in ("q_b", "kT_b"))
        v = [sb(f"v{i}", [P, TB, H // HPG, GW]) for i in range(2)]
        mx = sb("mx", [P, TB, H])
        nm = sb("nm", [P, TB, 2 * H], BF16)
        mT = [sb(f"mT{i}", [P, S], BF16) for i in range(2)]
        probs = [sb(f"probs{i}", [P, TB, S]) for i in range(4)]
        ln_sum, inv = ([sb(f"{n}{i}", [64, 2, S]) for i in range(2)] for n in ("ln_sum", "inv"))
        oT = [sb(f"oT{i}", [P, CH, S]) for i in range(2)]
        out_t = sb("out_t", [P, TB, D])
        pS = [ps(f"pS{i}") for i in range(2)]
        pT = [ps(f"pT{i}") for i in range(2)]
        pO = [ps(f"pO{i}") for i in range(2)]
        pM = [ps(f"pM{i}") for i in range(2)]

        weights_in = {src: sem(f"{n}_in") for n, src in (("wq", w_q), ("wk", w_k), ("wv", w_v), ("wo", w_o))}
        small_in = sem("small_in")
        ctx_in = [sem(f"ctx_in{i}") for i in range(2)]
        setup = sem("setup")
        gate_ready = sem("gate_ready")
        xn_ready = sem("xn_ready")
        full = [sem(f"full{i}") for i in range(2)]
        free = [sem(f"free{i}") for i in range(2)]
        s_ready = sem("s_ready")
        max_done = sem("max_done")
        k_rest_ready, k_2, k_split = sem("k_rest_ready"), sem("k_2"), sem("k_split")
        q_rest_ready, q_2, q_split = sem("q_rest_ready"), sem("q_2"), sem("q_split")
        k_saved, q_saved = sem("k_saved"), sem("q_saved")
        stacks_in = [sem(f"stacks_in{i}") for i in range(2)]
        m_hi, m_lo = sem("m_hi"), sem("m_lo")
        t_ready = sem("t_ready")
        p_ready = sem("p_ready")
        pv_done = sem("pv_done")
        newton_1, newton_2 = sem("newton_1"), sem("newton_2")
        ln_ready, inv_ready = sem("ln_ready"), sem("inv_ready")
        o_ready = sem("o_ready")
        x_new = sem("x_new")
        v_zero = sem("v_zero")
        first_half = sem("first_half")
        NG = H // HG

        half = (nF + nP) // 2

        def fill(k, name):
            if isinstance(k, int) and k == -1:
                n = begin_fills.index(name)
            elif isinstance(k, int) and k == 0 and name in begin_fills[:ahead]:
                n = nP + begin_fills.index(name)
            elif isinstance(k, int) and k >= B - 1 and name in finish_fills:
                n = 2 * nP + (B - 2) * (nF + nP) + (k - B + 1) * nF + finish_fills.index(name)
            else:
                i = nF + nP - 1 if name == "mT" else round_fills.index(name)
                return (nP - nF + i) % 2, k * half + (nP - nF + i) // 2
            return n % 2, n // 2

        def head_of(h):
            bank, i = h // HG, h % HG
            group = 4 * (bank // 2) + bank % 2 + 2 * (i // HPG)
            return group * HPG + i % HPG

        def v_place(i, j, h0, h1, at=0):
            groups = v[i][:, j, h0 // HPG:h1 // HPG, :]
            return groups.rearrange("p g (e w) -> p g e w", e=HPG)[:, :, :, at:at + dh]

        def rows(h):
            return h // HPC, slice(h % HPC * dh, (h % HPC + 1) * dh)

        def run_rounds(eng, round_):
            round_(0, 0, 0, prev=False)
            if B > 2:
                with eng.Fori(0, (B - 2) // 2) as i:
                    round_(2 * i + 1, 1, i + 1)
                    round_(2 * i + 2, 0, i + 1)
            round_(B - 1, (B - 1) % 2, None, nxt=False)

        block = ctx.enter_context(nc.Block())

        @block.sync
        def _(sp):
            def load_weights(w, src):
                sp.dma_start(w[:, :, :], dram[src].rearrange("(c p) n -> p c n", p=P)).then_inc(weights_in[src], 16)

            def column(dst, name):
                sp.dma_start(dst, dram[name].rearrange("(c p) -> p c", p=P),
                             allow_slow_non_contiguous=True).then_inc(small_in, 16)
            if b_q:
                column(bq_col, b_q)
            if b_k:
                column(bk_col, b_k)
            if gamma:
                column(gam, gamma)
                column(bet, beta)
            sp.dma_start(sel32[:, :], dram["head_select"]).then_inc(small_in, 16)
            if b_v:
                sp.dma_start(bv_row[:, :], dram[b_v].partition_broadcast(P)).then_inc(small_in, 16)
            if b_o:
                sp.dma_start(bo_row[:, :], dram[b_o].partition_broadcast(P)).then_inc(small_in, 16)
            if gate:
                sp.dma_start(gate_col, dram[gate].partition_broadcast(P)).then_inc(small_in, 16)

            def load_ctx(b, par):
                bank, n = fill(b - 3, v_fills[-1])
                sp.wait_ge(full[bank], n + 1)
                sp.dma_start(ctxT[par][:, :, :], ctx_view[bass.ds(b, 1)].rearrange("o p c s -> p (o c) s"))\
                  .then_inc(ctx_in[par], 16)
            ctx_view = dram["ctxT"].rearrange("b (c p) s -> b p c s", p=P)
            load_weights(wk, w_k)
            sp.dma_start(ctxT[0][:, :, :], ctx_view[0]).then_inc(ctx_in[0], 16)
            for w, src in ((wq, w_q), (wv, w_v), (wo, w_o)):
                load_weights(w, src)
            sp.dma_start(ctxT[1][:, :, :], ctx_view[1]).then_inc(ctx_in[1], 16)

            def restack(b, par):
                if not stacked:
                    return
                def save(split, parts, saved_dram, saved):
                    sp.wait_ge(split, b + 1)
                    sp.dma_start(saved_dram.rearrange("c t p s -> p (c t) s"),
                                 parts[:, :, :, :].rearrange("p c t s -> p (c t) s")).then_inc(saved, 16)

                def load(stack, saved_dram, terms):
                    for first, count, part in terms:
                        src = saved_dram[:, part:part + count]
                        sp.dma_start(stack[first * dh:(first + count) * dh, :, :].rearrange("p (c e) s -> p c (e s)", c=CH),
                                     src.rearrange("c t (d e) s -> (t d) c (e s)", d=dh)).then_inc(stacks_in[par], 16)
                save(k_split, k_parts, k_dram, k_saved)
                sp.wait_ge(k_saved, 16 * (b + 1))
                load(k_stack[par], k_dram, K_TERMS[:5])
                save(q_split, q_parts, q_dram, q_saved)
                load(k_stack[par], k_dram, K_TERMS[5:])
                sp.wait_ge(q_saved, 16 * (b + 1))
                load(q_stack[par], q_dram, Q_TERMS)

            restack(0, 0)
            restack(1, 1)
            load_ctx(2, 0)
            with sp.Fori(0, (B - 4) // 2) as i:
                restack(2 * i + 2, 0)
                load_ctx(2 * i + 3, 1)
                restack(2 * i + 3, 1)
                load_ctx(2 * i + 4, 0)
            restack(B - 2, 0)
            load_ctx(B - 1, 1)
            restack(B - 1, 1)
            if clear:
                core.clear(sp)
        n_small = 16 * (1 + sum(1 for x in (b_q, b_k, b_v, b_o, gate) if x) + (2 if gamma else 0))

        @block.scalar
        def _(act):
            act.wait_ge(small_in, n_small)
            if gate:
                nc.scalar.activation(gate_col, gate_col, ACT.Tanh).then_inc(gate_ready, 1)
            nc.scalar.preload_act_table_set("natural_log_exp_and_others")

            def exp(k, h):
                act.wait_ge(t_ready, k * H + h + 1)
                if not (isinstance(k, int) and k == 0 and h < 4):
                    act.wait_ge(pv_done, k * H + h - 3)
                nc.scalar.activation(probs[h % 4][:, :, :], pT[h % 2][:, :], ACT.Exp, scale=scale).then_inc(p_ready, 1)

            def read_out(k, name, par):
                bank, n = fill(k, name)
                src = pM[bank][:, :].rearrange("p (c s) -> p c s", c=2)
                act.wait_ge(full[bank], n + 1)
                if name == "xnT" and gamma:
                    for c in range(KC):
                        ins = nc.scalar.activation(xnT[:, c, :], src[:, c, :], ACT.Identity, bias=bet[:, c:c + 1],
                                             scale=gam[:, c:c + 1])
                    ins.then_inc(free[bank], 1)
                elif name == "xnT":
                    nc.scalar.activation(xnT[:, :, :], src, ACT.Copy).then_inc(free[bank], 1)
                elif name[0] == "q":
                    c0 = 2 * int(name[1:])
                    if b_q:
                        for c in range(2):
                            ins = nc.scalar.activation(qT[par][:, c0 + c, :], src[:, c, :], ACT.Identity,
                                                       bias=bq_col[:, c0 + c:c0 + c + 1])
                    else:
                        ins = nc.scalar.activation(qT[par][:, c0:c0 + 2, :], src, ACT.Copy)
                    first = q_parts[:, :, 0, :] if stacked else q_b[:, c0:c0 + 2, :]
                    if b_q:
                        for c in range(2):
                            ins = nc.scalar.activation(first[:, c, :], src[:, c, :], ACT.Identity, bias=bq_col[:, c0 + c:c0 + c + 1])
                    else:
                        ins = nc.scalar.activation(first, src, ACT.Copy)
                    ins.then_inc(free[bank], 1)
                elif name == "mT":
                    nc.scalar.activation(mT[par][0:2 * H, :], pM[bank][0:2 * H, 0:S], ACT.Copy).then_inc(free[bank], 1)

            mine = lambda name: name == "xnT" or name[0] == "q"

            for name in begin_fills:
                if mine(name) or name == "mT":
                    read_out(-1, name, 0)

            def inverse(b, g):
                act.wait_ge(pv_done, b * H + (g + 1) * HG)
                nc.scalar.activation(ln_sum[g % 2][:, :, :], pO[g % 2][64:P, :].rearrange("p (c s) -> p c s", c=2), ACT.Ln)\
                  .then_inc(ln_ready, 1)
                act.wait_ge(ln_ready, b * NG + g + 1)
                nc.scalar.activation(inv[g % 2][:, :, :], ln_sum[g % 2][:, :, :], ACT.Exp, scale=-1.0)\
                  .then_inc(inv_ready, 1)

            def round_(k, par, half_b, prev=True, nxt=True):
                for h in range(H):
                    if nxt and h == H - 1:
                        read_out(k, "mT", 1 - par)
                    exp(k, h)
                    if (h - LAG_PV) % HG == HG - 1:
                        if h >= LAG_PV:
                            inverse(k, (h - LAG_PV) // HG)
                        elif prev:
                            inverse(k - 1, (H + h - LAG_PV) // HG)
                    for name in begin_fills[:-1]:
                        if nxt and slot_of[name] == h and mine(name):
                            read_out(k, name, 1 - par)
            run_rounds(act, round_)
            for h in range(H - LAG_PV, H):
                if h % HG == HG - 1:
                    inverse(B - 1, h // HG)

        @block.gpsimd
        def _(pool):
            def split_q(k):
                bank, n = fill(k, "q0")
                pool.wait_ge(free[bank], n + 1)
                nc.gpsimd.tensor_tensor(q_rest[:, :, :], qT[0][:, :, :], q_parts[:, :, 0, :], ALU.subtract)\
                  .then_inc(q_rest_ready, 1)
                pool.wait_ge(q_rest_ready, k + 2)
                nc.gpsimd.tensor_tensor(q_parts[:, :, 1, :], q_rest[:, :, :],
                                        core.zeros[:, 0:S].unsqueeze(1).to_broadcast([P, CH, S]), ALU.add).then_inc(q_2, 1)
                pool.wait_ge(q_2, k + 2)
                nc.gpsimd.tensor_tensor(q_parts[:, :, 2, :], q_rest[:, :, :], q_parts[:, :, 1, :], ALU.subtract)\
                  .then_inc(q_split, 1)

            def round_(k, par, half_b, prev=True, nxt=True):
                if nxt:
                    split_q(k)
            if stacked:
                split_q(-1)
                run_rounds(pool, round_)

        @block.vector
        def _(dve):
            dve.wait_ge(small_in, n_small)
            for i in range(2):
                nc.vector.memset(mT[i][:, :], 0.0)
                if stacked:
                    nc.vector.memset(v[i][:, :, :, :], 0.0).then_inc(v_zero, 1)
            for i in range(2):
                if stacked:
                    dve.wait_ge(v_zero, 2)
                for j in range(TB):
                    nc.vector.memset(v_place(i, j, 0, H, 64), 1.0)
            nc.vector.tensor_copy(sel[:, :, :], sel32[:, :].unsqueeze(2).to_broadcast([P, H, P])).then_inc(setup, 1)

            def normalize(b):
                for j in range(TB):
                    t = TB * b + j
                    nc.vector.tensor_scalar(xn[:, j, :], X[:, bass.ds(t, 1), :].rearrange("p o d -> p (o d)"),
                                            core.mean[:, bass.ds(t, 1)], core.rstd[:, bass.ds(t, 1)],
                                            ALU.subtract, ALU.mult).then_inc(xn_ready, 1)

            def read_out(k, name, par):
                bank, n = fill(k, name)
                dve.wait_ge(full[bank], n + 1)
                src = pM[bank][:, :]
                if name[0] == "k":
                    c0 = 2 * int(name[1:])
                    for dst in (kT[par][:, c0:c0 + 2, :], k_parts[:, :, 0, :] if stacked else kT_b[:, c0:c0 + 2, :]):
                        if b_k:
                            for c in range(2):
                                ins = nc.vector.tensor_scalar(dst[:, c, :], src[:, c * S:(c + 1) * S],
                                                              bk_col[:, c0 + c:c0 + c + 1], None, ALU.add)
                        else:
                            ins = nc.vector.tensor_copy(dst, src.rearrange("p (c s) -> p c s", c=2))
                elif name == "v":
                    by_head = lambda a: a.rearrange("p (g e d) -> p g e d", e=HPG, d=dh)
                    for j in range(TB):
                        part = by_head(src[:, j * DI:(j + 1) * DI])
                        if b_v:
                            ins = nc.vector.tensor_tensor(v_place(par, j, 0, H), part, by_head(bv_row[:, :]), ALU.add)
                        else:
                            ins = nc.vector.tensor_copy(v_place(par, j, 0, H), part)
                else:
                    j, n = int(name[1]), int(name[2])
                    hh = 512 // dh
                    ins = nc.vector.tensor_copy(v_place(par, j, n * hh, (n + 1) * hh),
                                                src.rearrange("p (h e d) -> p h e d", h=hh, e=1))
                ins.then_inc(free[bank], 1)
                if stacked and name == "k0":
                    dve.wait_ge(free[bank], n + 1)
                    nc.vector.tensor_tensor(k_rest[:, :, :], kT[0][:, :, :], k_parts[:, :, 0, :], ALU.subtract)\
                      .then_inc(k_rest_ready, 1)
                    dve.wait_ge(k_rest_ready, k + 2)
                    nc.vector.tensor_copy(k_parts[:, :, 1, :], k_rest[:, :, :]).then_inc(k_2, 1)
                    dve.wait_ge(k_2, k + 2)
                    nc.vector.tensor_tensor(k_parts[:, :, 2, :], k_rest[:, :, :], k_parts[:, :, 1, :], ALU.subtract)\
                      .then_inc(k_split, 1)

            def maximum(b, h):
                dve.wait_ge(s_ready, b * H + h + 1)
                nc.vector.tensor_reduce(mx[:, :, h], pS[h % 2][:, :].rearrange("p (j s) -> p j s", j=TB),
                                        AX.X, ALU.max).then_inc(max_done, 1)

            def split_max(b):
                dve.wait_ge(max_done, (b + 1) * H)
                nc.vector.tensor_scalar(nm[:, :, 0:H], mx[:, :, :], -1.0, None, ALU.mult).then_inc(m_hi, 1)
                dve.wait_ge(m_hi, b + 1)
                nc.vector.scalar_tensor_tensor(nm[:, :, H:2 * H], mx[:, :, :], -1.0, nm[:, :, 0:H],
                                               ALU.mult, ALU.subtract).then_inc(m_lo, 1)

            def divide(b, par, g, step):
                n = b * NG + g + 1
                outputs, sums = (pO[g % 2][rows_, :].rearrange("p (c s) -> p c s", c=2)
                                 for rows_ in (slice(0, 64), slice(64, P)))
                r, t = inv[g % 2][:, :, :], ln_sum[g % 2][:, :, :]
                if step == 0:
                    dve.wait_ge(inv_ready, n)
                    nc.vector.tensor_tensor(t, sums, r, ALU.mult).then_inc(newton_1, 1)
                elif step == 1:
                    dve.wait_ge(newton_1, n)
                    nc.vector.scalar_tensor_tensor(t, t, 2.0, r, ALU.subtract, ALU.mult).then_inc(newton_2, 1)
                else:
                    dve.wait_ge(newton_2, n)
                    c0, r0 = g // 2 * 2, g % 2 * 64
                    nc.vector.scalar_tensor_tensor(oT[par][r0:r0 + 64, c0:c0 + 2, :], outputs, -1.0, t,
                                                   ALU.mult, ALU.mult).then_inc(o_ready, 1)

            def residual(k, j, name):
                bank, n = fill(k, name)
                at = name.index(str(j)) - 3
                proj = pM[bank][:, at * D:(at + 1) * D]
                last = name[-1] == str(j)
                t = TB * (k - 1) + j
                x_t = X[:, bass.ds(t, 1), :].rearrange("p o d -> p (o d)")
                dve.wait_ge(full[bank], n + 1)
                if b_o:
                    ins = nc.vector.tensor_tensor(out_t[:, j, :], proj, bo_row[:, :], ALU.add)
                else:
                    ins = nc.vector.tensor_tensor(x_t, proj, x_t, ALU.add)
                if last:
                    ins.then_inc(free[bank], 1)
                    dve.wait_ge(free[bank], n + 1)
                else:
                    ins.then_inc(first_half, 1)
                    dve.wait_ge(first_half, k)
                if b_o:
                    if gate:
                        ins = nc.vector.scalar_tensor_tensor(x_t, out_t[:, j, :], gate_col, x_t, ALU.mult, ALU.add)
                    else:
                        ins = nc.vector.tensor_tensor(x_t, out_t[:, j, :], x_t, ALU.add)
                    ins.then_inc(x_new, 1)
                    dve.wait_ge(x_new, t + 1)
                nc.vector.bn_stats(core.stats[:, bass.ds(t, 1), :].rearrange("p o d -> p (o d)"), x_t)

            mine = lambda name: name[0] in "kv"
            if gate:
                dve.wait_ge(gate_ready, 1)
            normalize(0)
            for name in begin_fills:
                if mine(name):
                    read_out(-1, name, 0)
            for h in range(H):
                maximum(0, h)
            split_max(0)

            def round_(k, par, half_b, prev=True, nxt=True):
                if nxt:
                    normalize(k + 1)
                for h in range(H):
                    for name in round_fills:
                        if prev and slot_of[name] == h and name in finish_fills:
                            for j in name[3:]:
                                residual(k, int(j), name)
                        if nxt and slot_of[name] == h and mine(name):
                            read_out(k, name, 1 - par)
                    maxima = list(heads_at.get(h, ())) if nxt else []
                    if (h - LAG_DIVIDE) % HG == HG - 1 and (prev or h >= LAG_DIVIDE):
                        back = h < LAG_DIVIDE
                        for step in range(3):
                            for hs in maxima[step:step + 1]:
                                maximum(k + 1, hs)
                            divide(k - back, 1 - par if back else par, (back * H + h - LAG_DIVIDE) // HG, step)
                        maxima = maxima[3:]
                    for hs in maxima:
                        maximum(k + 1, hs)
                    if nxt and h == S_SLOTS[-1]:
                        split_max(k + 1)
            run_rounds(dve, round_)
            for h in range(H - LAG_DIVIDE, H):
                if h % HG == HG - 1:
                    for step in range(3):
                        divide(B - 1, (B - 1) % 2, h // HG, step)
            for name in finish_fills:
                for j in name[3:]:
                    residual(B, int(j), name)

        @block.tensor
        def _(pe):
            def project(dst, w, c0, src):
                for c in range(2):
                    for kc in range(KC):
                        ins = nc.tensor.matmul(dst[:, c * S:(c + 1) * S], w[:, kc, (c0 + c) * P:(c0 + c + 1) * P],
                                               src[:, kc, :], start=kc == 0, stop=kc == KC - 1)
                return ins

            def issue(k, name, par, b, i):
                bank, n = fill(k, name)
                dst = pM[bank]
                if not (isinstance(k, int) and k < 0 and n == 0):
                    pe.wait_ge(free[bank], n)
                if name == "xnT":
                    pe.wait_ge(xn_ready, TB * (b + 1))
                    for c in range(KC):
                        for j in range(TB):
                            ins = nc.tensor.transpose(dst[:, c * S + j * P:c * S + (j + 1) * P],
                                                      xn[:, j, c * P:(c + 1) * P], core.ident[:, :])
                elif name[0] == "q":
                    if name == "q0":
                        pe.wait_ge(free[fill(k, "xnT")[0]], fill(k, "xnT")[1] + 1)
                    ins = project(dst, wq, 2 * int(name[1:]), xnT)
                elif name[0] == "k":
                    if name == "k0":
                        pe.wait_ge(ctx_in[par], 16 * (i + 1))
                    ins = project(dst, wk, 2 * int(name[1:]), ctxT[par])
                elif name == "v":
                    for j in range(TB):
                        for kc in range(KC):
                            ins = nc.tensor.matmul(dst[:, j * DI:(j + 1) * DI], ctxT[par][:, kc, j * P:(j + 1) * P],
                                                   wv[:, kc, :], start=kc == 0, stop=kc == KC - 1)
                elif name[0] == "v":
                    j, hf = int(name[1]), int(name[2])
                    for kc in range(KC):
                        ins = nc.tensor.matmul(dst[:, :], ctxT[par][:, kc, j * P:(j + 1) * P],
                                               wv[:, kc, hf * 512:(hf + 1) * 512], start=kc == 0, stop=kc == KC - 1)
                elif name == "mT":
                    pe.wait_ge(m_lo, b + 1)
                    for j in range(TB):
                        ins = nc.tensor.matmul(dst[0:2 * H, j * P:(j + 1) * P], nm[:, j, :], core.ident_b[:, :],
                                               start=True, stop=True)
                else:
                    pe.wait_ge(o_ready, NG * (b + 1))
                    for at, j in enumerate(name[3:]):
                        for c in range(CH):
                            ins = nc.tensor.matmul(dst[:, at * D:(at + 1) * D], oT[par][:, c, int(j) * P:(int(j) + 1) * P],
                                                   wo[:, c, :], start=c == 0, stop=c == CH - 1)
                ins.then_inc(full[bank], 1)

            def score(b, h, par):
                if not (isinstance(b, int) and b == 0 and h < 2):
                    pe.wait_ge(max_done, b * H + h - 1)
                hd = head_of(h)
                c, r = rows(hd)
                q, key = (q_stack[par][:, hd, :], k_stack[par][:, hd, :]) if stacked else (q_b[r, c, :], kT_b[r, c, :])
                for j in range(TB):
                    ins = nc.tensor.matmul(pS[h % 2][:, j * S:(j + 1) * S], q[:, j * P:(j + 1) * P], key,
                                           start=True, stop=True)
                ins.then_inc(s_ready, 1)

            def score_T(b, h, par):
                if not (isinstance(b, int) and b == 0 and h < 2):
                    pe.wait_ge(p_ready, b * H + h - 1)
                hd = head_of(h)
                c, r = rows(hd)
                q, key = ((q_stack[par][:, hd, :], k_stack[par][:, hd, :]) if stacked
                          else (qT[par][r, c, :], kT[par][r, c, :]))
                for j in range(TB):
                    out = pT[h % 2][:, j * S:(j + 1) * S]
                    nc.tensor.matmul(out, key[:, j * P:(j + 1) * P], q, start=True, stop=False)
                    ins = nc.tensor.matmul(out, sel[:, h, :], mT[par][:, :], start=False, stop=True)
                ins.then_inc(t_ready, 1)

            def times_v(b, h, par):
                pe.wait_ge(p_ready, b * H + h + 1)
                g, hd = h // HG, head_of(h)
                if h % HG == 0 and not (isinstance(b, int) and b == 0 and g < 2):
                    pe.wait_ge(o_ready, b * NG + g - 1)
                e, half_bank = h % HPG, h % HG // HPG
                for kt in range(TB):
                    ins = nc.tensor.matmul(pO[g % 2][:, half_bank * S:(half_bank + 1) * S],
                                           v[par][:, kt, hd // HPG, e * P:(e + 1) * P], probs[h % 4][:, kt, :],
                                           start=e == 0 and kt == 0, stop=e == HPG - 1 and kt == TB - 1)
                ins.then_inc(pv_done, 1)

            def wait_qkv(k, par, half_b):
                for name in begin_fills[-3:-1]:
                    bk, m = fill(k, name)
                    pe.wait_ge(free[bk], m + 1)
                if stacked:
                    pe.wait_ge(stacks_in[par], 16 * STACK_DMAS * (half_b + 1))

            pe.wait_ge(setup, 1)
            first_use = {"k0": w_k, "q0": w_q, v_fills[0]: w_v}
            for name in begin_fills[:-1]:
                if name in first_use:
                    pe.wait_ge(weights_in[first_use[name]], 16)
                issue(-1, name, 0, 0, 0)
            wait_qkv(-1, 0, 0)
            for h in range(H):
                score(0, h, 0)
            issue(-1, "mT", 0, 0, 0)

            def round_(k, par, half_b, prev=True, nxt=True):
                bank, n = fill(k - 1, "mT")
                pe.wait_ge(free[bank], n + 1)
                for h in range(H):
                    if nxt and h == S_SLOTS[0]:
                        wait_qkv(k, 1 - par, half_b)
                    ahead_scores = heads_at.get(h, ()) if nxt else ()
                    for hs in ahead_scores[:1]:
                        score(k + 1, hs, 1 - par)
                    score_T(k, h, par)
                    for hs in ahead_scores[1:2]:
                        score(k + 1, hs, 1 - par)
                    if h >= LAG_PV:
                        times_v(k, h - LAG_PV, par)
                    elif prev:
                        times_v(k - 1, H + h - LAG_PV, 1 - par)
                    for name in round_fills:
                        if prev and slot_of[name] == h and name in finish_fills:
                            issue(k, name, 1 - par, k - 1, None)
                        if nxt and slot_of[name] == h and name in begin_fills:
                            issue(k, name, 1 - par, k + 1, half_b)
                    for hs in ahead_scores[2:]:
                        score(k + 1, hs, 1 - par)
                    if nxt and h == H - 2:
                        issue(k, "mT", 1 - par, k + 1, half_b)

            pe.wait_ge(weights_in[w_o], 16)
            run_rounds(pe, round_)
            for h in range(H - LAG_PV, H):
                times_v(B - 1, h, (B - 1) % 2)
            for name in finish_fills:
                issue(B, name, (B - 1) % 2, B - 1, None)


def staggered(eng, n, round_):
    def flags(k):
        return {d: 0 <= k + d < n for d in range(-2, 4)}
    for k in range(3):
        round_(k, k % 2, k // 2, flags(k))
    pairs = (n - 6) // 2
    with eng.Fori(0, pairs) as i:
        round_(2 * i + 3, 1, i + 1, dict.fromkeys(range(-2, 4), True))
        round_(2 * i + 4, 0, i + 2, dict.fromkeys(range(-2, 4), True))
    for k in range(2 * pairs + 3, n):
        round_(k, k % 2, k // 2, flags(k))


def flat(ap):
    return ap.rearrange("p o d -> p (o d)")


def ternary_ffn(core):
    nc, X, dram = core.nc, core.X, core.dram
    F = 1024
    FC = F // P
    n = TB * B
    with ExitStack() as ctx:
        def sb(name, shape, dt=F32):
            return ctx.enter_context(nc.sbuf_tensor(f"L0f_{name}", shape, dt))

        def ps(name, cols=512):
            return ctx.enter_context(nc.psum_tensor(f"L0f_{name}", [P, cols], F32))

        def sem(name):
            return ctx.enter_context(nc.semaphore(f"L0f_{name}"))

        w32 = [sb(f"w32_{i}", [P, KC * F]) for i in range(3)]
        wint = [sb(f"wint{i}", [P, KC * F], BF16) for i in range(3)]
        ones = sb("ones", [P, P])
        wsum, wmean, wscale = sb("wsum", [P, 3]), sb("wmean", [P, 3]), sb("wscale", [P, 3])
        xn = sb("xn", [P, D])
        amax, qs = sb("amax", [P, 2]), sb("qs", [P, 2])
        dqg, dqu = sb("dqg", [P, 2]), sb("dqu", [P, 2])
        xr = sb("xr", [P, D])
        a = sb("a", [P, 2, D], BF16)
        aT = sb("aT", [P, 2, KC * P], BF16)
        sg = sb("sg", [P, 2, F])
        h = sb("h", [P, F])
        hmax, hqs, hdq = sb("hmax", [P, 2]), sb("hqs", [P, 2]), sb("hdq", [P, 2])
        hr = sb("hr", [P, F])
        hq = sb("hq", [P, F], BF16)
        hT = sb("hT", [P, F], BF16)
        pG = [ps(f"pG{i}") for i in range(2)]
        pU = [ps(f"pU{i}") for i in range(2)]
        pA = ps("pA")
        pH = [ps(f"pH{i}") for i in range(2)]
        pY = ps("pY")

        w_in = [sem(f"w_in{i}") for i in range(3)]
        setup, sums_ready, w_ready = sem("setup"), sem("sums_ready"), sem("w_ready")
        wstep = sem("wstep")
        a_ready = sem("a_ready")
        astep = sem("astep")
        aT_full = sem("aT_full")
        aT_ready = sem("aT_ready")
        g_ready, u_ready = sem("g_ready"), sem("u_ready")
        sg_ready = sem("sg_ready")
        h_ready = sem("h_ready")
        hs_ready = sem("hs_ready")
        hstep = sem("hstep")
        hr_ready = sem("hr_ready")
        hq_ready = sem("hq_ready")
        hT_full = sem("hT_full")
        hT_ready = sem("hT_ready")
        y_ready = sem("y_ready")
        x_new = sem("x_new")

        with nc.Block() as block:
            @block.sync
            def _(sp):
                for i, name in enumerate(("L0f_wg", "L0f_wu")):
                    sp.dma_start(w32[i][:, :].rearrange("p (c n) -> p c n", c=KC),
                                 dram[name].rearrange("(c p) n -> p c n", p=P)).then_inc(w_in[i], 16)
                sp.dma_start(w32[2][:, :].rearrange("p (c n) -> p c n", c=FC),
                             dram["L0f_wd"].rearrange("(c p) n -> p c n", p=P)).then_inc(w_in[2], 16)

            @block.scalar
            def _(act):
                def silu(k, par):
                    for f in range(2):
                        act.wait_ge(g_ready, 2 * k + f + 1)
                        nc.scalar.activation(sg[:, par, f * 512:(f + 1) * 512], pG[f][:, :], ACT.Silu,
                                             scale=dqg[:, par:par + 1]).then_inc(sg_ready, 1)

                def take_aT(k, par):
                    act.wait_ge(aT_full, k + 1)
                    nc.scalar.activation(aT[:, par, :], pA[:, 0:KC * P], ACT.Copy).then_inc(aT_ready, 1)

                def round_(k, par, half, has):
                    act.wait_ge(hs_ready, k + 1)
                    nc.scalar.activation(hr[:, :], h[:, :], ACT.Copy, bias=ROUND, scale=hqs[:, par:par + 1])\
                      .then_inc(hr_ready, 1)
                    if has[1]:
                        silu(k + 1, 1 - par)
                    for f in range(2):
                        act.wait_ge(hT_full, 2 * k + f + 1)
                        nc.scalar.activation(hT[:, f * 512:(f + 1) * 512], pH[f][:, :], ACT.Copy).then_inc(hT_ready, 1)
                    if has[2]:
                        take_aT(k + 2, par)
                take_aT(0, 0)
                take_aT(1, 1)
                silu(0, 0)
                staggered(act, n, round_)

            @block.vector
            def _(dve):
                steps = [0]

                def then_wait(ins):
                    steps[0] += 1
                    ins.then_inc(wstep, 1)
                    dve.wait_ge(wstep, steps[0])

                nc.vector.memset(ones[:, :], 1.0)
                for i in range(3):
                    dve.wait_ge(w_in[i], 16)
                    ins = nc.vector.tensor_reduce(wsum[:, i:i + 1], w32[i][:, :], AX.X, ALU.add,
                                                  apply_absolute_value=True)
                ins.then_inc(setup, 1)
                dve.wait_ge(sums_ready, 1)
                then_wait(nc.vector.tensor_scalar(wmean[:, :], pY[:, 0:3], 1.0 / (D * F), 1e-5, ALU.mult, ALU.max))
                then_wait(nc.vector.reciprocal(wscale[:, :], wmean[:, :]))
                for i in range(3):
                    then_wait(nc.vector.tensor_scalar(w32[i][:, :], w32[i][:, :], wscale[:, i:i + 1], 1.0,
                                                      ALU.mult, ALU.min))
                    then_wait(nc.vector.tensor_scalar(w32[i][:, :], w32[i][:, :], -1.0, ROUND, ALU.max, ALU.add))
                    nc.vector.tensor_scalar(wint[i][:, :], w32[i][:, :], ROUND, None, ALU.subtract).then_inc(w_ready, 1)

                A_STEPS = 7

                def integers(k, par):
                    done = [0]

                    def step(ins):
                        done[0] += 1
                        ins.then_inc(astep, 1)
                        dve.wait_ge(astep, k * A_STEPS + done[0])
                    one = slice(par, par + 1)
                    step(nc.vector.tensor_scalar(xn[:, :], flat(X[:, bass.ds(k, 1), :]), core.mean[:, bass.ds(k, 1)],
                                                 core.rstd[:, bass.ds(k, 1)], ALU.subtract, ALU.mult))
                    step(nc.vector.tensor_reduce(amax[:, one], xn[:, :], AX.X, ALU.max, apply_absolute_value=True))
                    step(nc.vector.tensor_scalar(amax[:, one], amax[:, one], 1e-5, 1.0 / 127.0, ALU.max, ALU.mult))
                    nc.vector.tensor_scalar(dqg[:, one], amax[:, one], wmean[:, 0:1], None, ALU.mult)
                    nc.vector.tensor_scalar(dqu[:, one], amax[:, one], wmean[:, 1:2], None, ALU.mult)
                    step(nc.vector.reciprocal(qs[:, one], amax[:, one]))
                    step(nc.vector.tensor_scalar(xr[:, :], xn[:, :], qs[:, one], ROUND, ALU.mult, ALU.add))
                    nc.vector.tensor_scalar(a[:, par, :], xr[:, :], ROUND, None, ALU.subtract).then_inc(a_ready, 1)
                    assert done[0] == 5
                A_STEPS = 5

                def output(k, par):
                    x_t = flat(X[:, bass.ds(k, 1), :])
                    dve.wait_ge(y_ready, k + 1)
                    nc.vector.scalar_tensor_tensor(x_t, pY[:, 0:D], hdq[:, par:par + 1], x_t, ALU.mult, ALU.add)\
                      .then_inc(x_new, 1)
                    dve.wait_ge(x_new, k + 1)
                    nc.vector.bn_stats(flat(core.stats[:, bass.ds(k, 1), :]), x_t)

                def round_(k, par, half, has):
                    one = slice(par, par + 1)
                    for f in range(2):
                        dve.wait_ge(sg_ready, 2 * k + f + 1)
                        dve.wait_ge(u_ready, 2 * k + f + 1)
                        nc.vector.scalar_tensor_tensor(h[:, f * 512:(f + 1) * 512], pU[f][:, :], dqu[:, one],
                                                       sg[:, par, f * 512:(f + 1) * 512], ALU.mult, ALU.mult)\
                          .then_inc(h_ready, 1)
                    dve.wait_ge(h_ready, 2 * k + 2)
                    nc.vector.tensor_reduce(hmax[:, one], h[:, :], AX.X, ALU.max, apply_absolute_value=True)\
                      .then_inc(hstep, 1)
                    dve.wait_ge(hstep, 2 * k + 1)
                    nc.vector.tensor_scalar(hmax[:, one], hmax[:, one], 1e-5, 1.0 / 127.0, ALU.max, ALU.mult)\
                      .then_inc(hstep, 1)
                    dve.wait_ge(hstep, 2 * k + 2)
                    nc.vector.reciprocal(hqs[:, one], hmax[:, one]).then_inc(hs_ready, 1)
                    nc.vector.tensor_scalar(hdq[:, one], hmax[:, one], wmean[:, 2:3], None, ALU.mult)
                    if has[-1]:
                        output(k - 1, 1 - par)
                    if has[2]:
                        integers(k + 2, par)
                    dve.wait_ge(hr_ready, k + 1)
                    nc.vector.tensor_scalar(hq[:, :], hr[:, :], ROUND, None, ALU.subtract).then_inc(hq_ready, 1)
                integers(0, 0)
                integers(1, 1)
                staggered(dve, n, round_)
                output(n - 1, (n - 1) % 2)

            @block.tensor
            def _(pe):
                def transpose_a(k, par):
                    pe.wait_ge(a_ready, k + 1)
                    if not (isinstance(k, int) and k == 0):
                        pe.wait_ge(aT_ready, k)
                    for c in range(KC):
                        ins = nc.tensor.matmul(pA[:, c * P:(c + 1) * P], a[:, par, c * P:(c + 1) * P],
                                               core.ident_b[:, :], start=True, stop=True)
                    ins.then_inc(aT_full, 1)

                def gate_up(k, par):
                    pe.wait_ge(aT_ready, k + 1)
                    for f in range(2):
                        if not (isinstance(k, int) and k == 0):
                            pe.wait_ge(sg_ready, 2 * k + f - 1)
                            pe.wait_ge(h_ready, 2 * k + f - 1)
                        for w, bank, ready in ((wint[0], pG[f], g_ready), (wint[1], pU[f], u_ready)):
                            for c in range(KC):
                                ins = nc.tensor.matmul(bank[:, :], aT[:, par, c * P:(c + 1) * P],
                                                       w[:, c * F + f * 512:c * F + (f + 1) * 512],
                                                       start=c == 0, stop=c == KC - 1)
                            ins.then_inc(ready, 1)

                def round_(k, par, half, has):
                    if has[1]:
                        gate_up(k + 1, 1 - par)
                    if has[2]:
                        transpose_a(k + 2, par)
                    pe.wait_ge(hq_ready, k + 1)
                    for f in range(2):
                        if not (isinstance(k, int) and k == 0):
                            pe.wait_ge(hT_ready, 2 * k + f - 1)
                        for c in range(4):
                            cc = 4 * f + c
                            ins = nc.tensor.matmul(pH[f][:, c * P:(c + 1) * P], hq[:, cc * P:(cc + 1) * P],
                                                   core.ident_b[:, :], start=True, stop=True)
                        ins.then_inc(hT_full, 1)
                    if not (isinstance(k, int) and k == 0):
                        pe.wait_ge(x_new, k)
                    for cc in range(FC):
                        if cc % 4 == 0:
                            pe.wait_ge(hT_ready, 2 * k + cc // 4 + 1)
                        ins = nc.tensor.matmul(pY[:, 0:D], hT[:, cc * P:(cc + 1) * P], wint[2][:, cc * D:(cc + 1) * D],
                                               start=cc == 0, stop=cc == FC - 1)
                    ins.then_inc(y_ready, 1)
                pe.wait_ge(setup, 1)
                nc.tensor.matmul(pY[:, 0:3], ones[:, :], wsum[:, :], start=True, stop=True).then_inc(sums_ready, 1)
                transpose_a(0, 0)
                transpose_a(1, 1)
                pe.wait_ge(w_ready, 3)
                gate_up(0, 0)
                staggered(pe, n, round_)


def mlstm(core):
    nc, X, dram = core.nc, core.X, core.dram
    NH = 4
    DH = D // NH
    W1 = DH + 1
    HC = S + P
    n = B
    FORGET, INPUT = slice(0, NH), slice(32, 32 + NH)
    with ExitStack() as ctx:
        def sb(name, shape, dt=F32):
            return ctx.enter_context(nc.sbuf_tensor(f"L1x_{name}", shape, dt))

        def ps(name):
            return ctx.enter_context(nc.psum_tensor(f"L1x_{name}", [P, 512], F32))

        def sem(name):
            return ctx.enter_context(nc.semaphore(f"L1x_{name}"))

        gk = sb("gk", [P, 3 * KC, 64])
        bias = sb("bias", [NH, 2])
        neg_ib = sb("neg_ib", [NH, 1])
        scale_row = sb("scale_row", [P, D])
        mask32 = sb("mask32", [P, S])
        mask = sb("mask", [P, S], BF16)
        sel = sb("sel", [P, NH, P])
        one4 = sb("one4", [NH, S])
        ctxT = [sb(f"ctxT{i}", [P, KC, S]) for i in range(2)]
        v = [sb(f"v{i}", [P, TB, NH, W1]) for i in range(2)]
        xn = sb("xn", [P, TB, D])
        xnT = [sb(f"xnT{i}", [P, KC, S]) for i in range(2)]
        f_pre, f_abs, f_exp, f_log, lf, F, a_row, FM, E_row = (sb(s, [NH, S]) for s in (
            "f_pre", "f_abs", "f_exp", "f_log", "lf", "F", "a_row", "FM", "E_row"))
        M = [sb(f"M{i}", [P, S]) for i in range(2)]
        tok = [sb(f"tok{i}", [P, TB, 2 * NH]) for i in range(2)]
        decay = sb("decay", [P, 2, HC])
        c_T = sb("c_T", [P, 2, HC])
        norm, inv = sb("norm", [P, TB, NH]), sb("inv", [P, TB, NH])
        hs, hc, sq = (sb(s, [P, TB, NH, DH]) for s in ("hs", "hc", "sq"))
        hsum, var, lnv, r, tmp = (sb(s, [P, TB, NH]) for s in ("hsum", "var", "lnv", "r", "tmp"))
        eps_col = sb("eps_col", [P, 1])
        hy, hz = sb("hy", [P, TB, D]), sb("hz", [P, TB, D])
        pQ = [ps(f"pQ{i}") for i in range(2)]
        pD = [ps(f"pD{i}") for i in range(2)]
        pO = [ps(f"pO{i}") for i in range(TB)]
        pX, pG = ps("pX"), ps("pG")

        small_in, setup = sem("small_in"), sem("setup")
        ctx_in = [sem(f"ctx_in{i}") for i in range(2)]
        v_in = [sem(f"v_in{i}") for i in range(2)]
        xn_ready, xnT_full, xnT_ready = sem("xn_ready"), sem("xnT_full"), sem("xnT_ready")
        gates_full, f_ready, f_abs_ready, f_exp_ready, f_log_ready = (sem(s) for s in (
            "gates_full", "f_ready", "f_abs_ready", "f_exp_ready", "f_log_ready"))
        row_step = sem("row_step")
        E_ready = sem("E_ready")
        tok_full, tok_ready = sem("tok_full"), sem("tok_ready")
        qk_ready, d_ready = sem("qk_ready"), sem("d_ready")
        decay_ready, c_ready, pv_done = sem("decay_ready"), sem("c_ready"), sem("pv_done")
        end_step = sem("end_step")
        sq_ready, ln_ready, r_ready = sem("sq_ready"), sem("ln_ready"), sem("r_ready")
        o_taken, var_sum, newton = sem("o_taken"), sem("var_sum"), sem("newton")
        hy_ready, hz_ready = sem("hy_ready"), sem("hz_ready")
        x_new = sem("x_new")

        with nc.Block() as block:
            @block.sync
            def _(sp):
                sp.dma_start(gk[:, :, :], dram["L1x_gates"].rearrange("(c p) n -> p c n", p=P)).then_inc(small_in, 16)
                for i, name in enumerate(("L1x_fb", "L1x_ib")):
                    sp.dma_start(bias[:, i:i + 1], dram[name].rearrange("(p o) -> p o", o=1),
                                 allow_slow_non_contiguous=True).then_inc(small_in, 16)
                sp.dma_start(scale_row[:, :], dram["L1x_scale"].partition_broadcast(P)).then_inc(small_in, 16)
                sp.dma_start(mask32[:, :], dram["L1x_mask"]).then_inc(small_in, 16)
                sp.dma_start(sel[:, :, :], dram["L1x_sel"]).then_inc(small_in, 16)

                def load(b, par):
                    sp.dma_start(ctxT[par][:, :, :],
                                 dram["ctxT"].rearrange("b (c p) s -> b p c s", p=P)[bass.ds(b, 1)]
                                 .rearrange("o p c s -> p (o c) s")).then_inc(ctx_in[par], 16)
                    for j in range(TB):
                        sp.dma_start(v[par][:, j, :, 0:DH],
                                     dram["ctx"].rearrange("b (j p) (h d) -> b j p h d", p=P, h=NH)[bass.ds(b, 1), j]
                                     .rearrange("o p h d -> p (o h) d")).then_inc(v_in[par], 16)
                sp.wait_ge(setup, 1)
                load(0, 0)
                load(1, 1)

                def round_(k, par, half, has):
                    if has[2]:
                        sp.wait_ge(pv_done, NH * (k + 1))
                        load(k + 2, par)
                staggered(sp, n, round_)

            @block.scalar
            def _(act):
                nc.scalar.preload_act_table_set("natural_log_exp_and_others")

                def begin1(k, par):
                    act.wait_ge(xnT_full, k + 1)
                    nc.scalar.activation(xnT[par][:, :, :], pX[:, :].rearrange("p (c s) -> p c s", c=KC), ACT.Copy)\
                      .then_inc(xnT_ready, 1)

                def begin2(k, par):
                    act.wait_ge(f_ready, k + 1)
                    nc.scalar.activation(f_abs[:, :], f_pre[:, :], ACT.Abs).then_inc(f_abs_ready, 1)
                    act.wait_ge(f_abs_ready, k + 1)
                    nc.scalar.activation(f_exp[:, :], f_abs[:, :], ACT.Exp, scale=-1.0).then_inc(f_exp_ready, 1)
                    act.wait_ge(f_exp_ready, k + 1)
                    nc.scalar.activation(f_log[:, :], f_exp[:, :], ACT.Ln, bias=1.0).then_inc(f_log_ready, 1)

                def begin3(k, par):
                    act.wait_ge(row_step, 5 * k + 5)
                    nc.scalar.activation(E_row[:, :], FM[:, :], ACT.Exp, scale=-1.0, bias=neg_ib[:, :]).then_inc(E_ready, 1)
                    act.wait_ge(tok_full, k + 1)
                    nc.scalar.activation(tok[par][:, :, :],
                                         pG[:, S:S + TB * 2 * NH].rearrange("p (j g) -> p j g", j=TB), ACT.Copy)\
                      .then_inc(tok_ready, 1)

                def head(k, par, h):
                    if h == 0:
                        act.wait_ge(tok_ready, k + 1)
                    act.wait_ge(d_ready, k * NH + h + 1)
                    if not (isinstance(k, int) and k == 0 and h < 2):
                        act.wait_ge(c_ready, k * NH + h - 1)
                    nc.scalar.activation(decay[:, h % 2, 0:S], pD[h % 2][:, 0:S], ACT.Exp, bias=tok[par][:, 0, h:h + 1])
                    nc.scalar.activation(decay[:, h % 2, S:HC], pD[h % 2][:, S:HC], ACT.Exp,
                                         bias=tok[par][:, 1, h:h + 1]).then_inc(decay_ready, 1)

                def squares(k):
                    act.wait_ge(end_step, 6 * k + 6)
                    nc.scalar.activation(sq[:, :, :, :], hc[:, :, :, :], ACT.Square).then_inc(sq_ready, 1)

                def deviations(k):
                    act.wait_ge(ln_ready, k + 1)
                    nc.scalar.activation(lnv[:, :, :], var[:, :, :], ACT.Ln, bias=eps_col[:, :]).then_inc(r_ready, 1)
                    act.wait_ge(r_ready, 2 * k + 1)
                    nc.scalar.activation(r[:, :, :], lnv[:, :, :], ACT.Exp, scale=-0.5).then_inc(r_ready, 1)

                def round_(k, par, half, has):
                    if has[-1]:
                        squares(k - 1)
                    head(k, par, 0)
                    if has[1]:
                        begin1(k + 1, 1 - par)
                    if has[-1]:
                        deviations(k - 1)
                    head(k, par, 1)
                    if has[1]:
                        begin2(k + 1, 1 - par)
                    head(k, par, 2)
                    head(k, par, 3)
                    if has[1]:
                        begin3(k + 1, 1 - par)
                act.wait_ge(setup, 1)
                begin1(0, 0)
                begin2(0, 0)
                begin3(0, 0)
                staggered(act, n, round_)
                squares(n - 1)
                deviations(n - 1)

            @block.vector
            def _(dve):
                for i in range(2):
                    nc.vector.memset(M[i][:, :], 0.0)
                    nc.vector.memset(v[i][:, :, :, DH:W1], 1.0)
                nc.vector.memset(one4[:, :], 1.0)
                nc.vector.memset(eps_col[:, :], 1e-6)
                dve.wait_ge(small_in, 16 * 6)
                nc.vector.tensor_copy(mask[:, :], mask32[:, :])
                nc.vector.tensor_scalar(neg_ib[:, :], bias[:, 1:2], -1.0, None, ALU.mult).then_inc(setup, 1)
                dve.wait_ge(setup, 1)

                def begin1(k, par):
                    for j in range(TB):
                        t = TB * k + j
                        ins = nc.vector.tensor_scalar(xn[:, j, :], flat(X[:, bass.ds(t, 1), :]),
                                                      core.mean[:, bass.ds(t, 1)], core.rstd[:, bass.ds(t, 1)],
                                                      ALU.subtract, ALU.mult)
                    ins.then_inc(xn_ready, 1)

                def begin2(k, par):
                    dve.wait_ge(gates_full, k + 1)
                    nc.vector.tensor_scalar(f_pre[:, :], pG[FORGET, 0:S], bias[:, 0:1], None, ALU.add).then_inc(f_ready, 1)

                def begin3(k, par):
                    m = M[par][0:NH, :]
                    dve.wait_ge(f_log_ready, k + 1)
                    nc.vector.scalar_tensor_tensor(lf[:, :], f_pre[:, :], 0.0, f_log[:, :], ALU.min, ALU.subtract)\
                      .then_inc(row_step, 1)
                    dve.wait_ge(row_step, 5 * k + 1)
                    nc.vector.tensor_tensor_scan(F[:, :], one4[:, :], lf[:, :], neg_ib[:, :], ALU.mult, ALU.add)\
                      .then_inc(row_step, 1)
                    dve.wait_ge(row_step, 5 * k + 2)
                    nc.vector.tensor_tensor(a_row[:, :], pG[INPUT, 0:S], F[:, :], ALU.subtract).then_inc(row_step, 1)
                    dve.wait_ge(row_step, 5 * k + 3)
                    nc.vector.tensor_tensor_scan(m, a_row[:, :], a_row[:, :], -3.0e38, ALU.max, ALU.max)\
                      .then_inc(row_step, 1)
                    dve.wait_ge(row_step, 5 * k + 4)
                    nc.vector.tensor_tensor(FM[:, :], F[:, :], m, ALU.add).then_inc(row_step, 1)

                def head(k, par, h):
                    dve.wait_ge(qk_ready, k * NH + h + 1)
                    dve.wait_ge(decay_ready, k * NH + h + 1)
                    if not (isinstance(k, int) and k == 0 and h < 2):
                        dve.wait_ge(pv_done, k * NH + h - 1)
                    nc.vector.scalar_tensor_tensor(c_T[:, h % 2, :], pQ[h % 2][:, 0:HC], DH ** -0.5, decay[:, h % 2, :],
                                                   ALU.mult, ALU.mult).then_inc(c_ready, 1)

                def take_outputs(k, par):
                    base = [0]

                    def step(ins):
                        base[0] += 1
                        ins.then_inc(end_step, 1)
                        dve.wait_ge(end_step, 6 * k + base[0])
                    dve.wait_ge(pv_done, NH * (k + 1))
                    for j in range(TB):
                        sums = pO[j][:, 0:NH * W1].rearrange("p (h w) -> p h w", h=NH)[:, :, DH:W1]
                        ins = nc.vector.tensor_reduce(norm[:, j, :], sums, AX.X, ALU.max, apply_absolute_value=True)
                    step(ins)
                    step(nc.vector.tensor_tensor(norm[:, :, :], norm[:, :, :], tok[par][:, :, NH:2 * NH], ALU.max))
                    step(nc.vector.tensor_scalar(norm[:, :, :], norm[:, :, :], 1e-6, None, ALU.add))
                    step(nc.vector.reciprocal(inv[:, :, :], norm[:, :, :]))
                    for j in range(TB):
                        part = pO[j][:, 0:NH * W1].rearrange("p (h w) -> p h w", h=NH)[:, :, 0:DH]
                        ins = nc.vector.tensor_tensor(hs[:, j, :, :], part,
                                                      inv[:, j, :].unsqueeze(2).to_broadcast([P, NH, DH]), ALU.mult)
                    ins.then_inc(o_taken, 1)

                def centre(k):
                    dve.wait_ge(o_taken, k + 1)
                    nc.vector.tensor_reduce(hsum[:, :, :], hs[:, :, :, :], AX.X, ALU.add).then_inc(end_step, 1)
                    dve.wait_ge(end_step, 6 * k + 5)
                    nc.vector.scalar_tensor_tensor(
                        hc[:, :, :, :].rearrange("p j h d -> p (j h) d"),
                        hsum[:, :, :].rearrange("p j h -> p (j h)").unsqueeze(2).to_broadcast([P, TB * NH, DH]),
                        -1.0 / DH, hs[:, :, :, :].rearrange("p j h d -> p (j h) d"), ALU.mult, ALU.add)\
                        .then_inc(end_step, 1)

                def variances(k):
                    dve.wait_ge(sq_ready, k + 1)
                    nc.vector.tensor_reduce(var[:, :, :], sq[:, :, :, :], AX.X, ALU.add).then_inc(var_sum, 1)
                    dve.wait_ge(var_sum, k + 1)
                    nc.vector.tensor_scalar(var[:, :, :], var[:, :, :], 1.0 / DH, None, ALU.mult).then_inc(ln_ready, 1)

                def refine(k):
                    dve.wait_ge(r_ready, 2 * k + 2)
                    nc.vector.tensor_tensor(tmp[:, :, :], r[:, :, :], r[:, :, :], ALU.mult).then_inc(newton, 1)
                    dve.wait_ge(newton, 4 * k + 1)
                    nc.vector.scalar_tensor_tensor(tmp[:, :, :], var[:, :, :], 1e-6, tmp[:, :, :], ALU.add, ALU.mult)\
                      .then_inc(newton, 1)
                    dve.wait_ge(newton, 4 * k + 2)
                    nc.vector.tensor_scalar(tmp[:, :, :], tmp[:, :, :], -0.5, 1.5, ALU.mult, ALU.add).then_inc(newton, 1)
                    dve.wait_ge(newton, 4 * k + 3)
                    nc.vector.tensor_tensor(r[:, :, :], r[:, :, :], tmp[:, :, :], ALU.mult).then_inc(newton, 1)

                def update(k):
                    dve.wait_ge(newton, 4 * k + 4)
                    nc.vector.tensor_tensor(hy[:, :, :].rearrange("p j (h d) -> p (j h) d", h=NH),
                                            hc[:, :, :, :].rearrange("p j h d -> p (j h) d"),
                                            r[:, :, :].rearrange("p j h -> p (j h)").unsqueeze(2)
                                            .to_broadcast([P, TB * NH, DH]), ALU.mult).then_inc(hy_ready, 1)
                    dve.wait_ge(hy_ready, k + 1)
                    nc.vector.tensor_tensor(hz[:, :, :], hy[:, :, :],
                                            scale_row[:, :].unsqueeze(1).to_broadcast([P, TB, D]), ALU.mult)\
                      .then_inc(hz_ready, 1)
                    x_b = X[:, bass.ds(TB * k, TB), :]
                    dve.wait_ge(hz_ready, k + 1)
                    nc.vector.tensor_tensor(x_b, hz[:, :, :], x_b, ALU.add).then_inc(x_new, 1)
                    dve.wait_ge(x_new, k + 1)
                    for j in range(TB):
                        t = TB * k + j
                        nc.vector.bn_stats(flat(core.stats[:, bass.ds(t, 1), :]), flat(X[:, bass.ds(t, 1), :]))

                def round_(k, par, half, has):
                    if has[1]:
                        begin1(k + 1, 1 - par)
                    if has[-1]:
                        centre(k - 1)
                    head(k, par, 0)
                    if has[-1]:
                        variances(k - 1)
                    head(k, par, 1)
                    if has[1]:
                        begin2(k + 1, 1 - par)
                    if has[-1]:
                        refine(k - 1)
                    head(k, par, 2)
                    if has[-1]:
                        update(k - 1)
                    head(k, par, 3)
                    if has[1]:
                        begin3(k + 1, 1 - par)
                    take_outputs(k, par)
                begin1(0, 0)
                begin2(0, 0)
                begin3(0, 0)
                staggered(dve, n, round_)
                for part_of_end in (centre, variances, refine, update):
                    part_of_end(n - 1)

            @block.tensor
            def _(pe):
                def begin1(k, par):
                    pe.wait_ge(xn_ready, k + 1)
                    for c in range(KC):
                        for j in range(TB):
                            ins = nc.tensor.transpose(pX[:, c * S + j * P:c * S + (j + 1) * P],
                                                      xn[:, j, c * P:(c + 1) * P], core.ident[:, :])
                    ins.then_inc(xnT_full, 1)

                def begin2(k, par, half):
                    pe.wait_ge(xnT_ready, k + 1)
                    pe.wait_ge(ctx_in[par], 16 * (half + 1))
                    if not (isinstance(k, int) and k == 0):
                        pe.wait_ge(tok_ready, k)
                    parts = [xnT[par], ctxT[par], ctxT[par]]
                    for i in range(3 * KC):
                        ins = nc.tensor.matmul(pG[0:64, 0:S], gk[:, i, :], parts[i // KC][:, i % KC, :],
                                               start=i == 0, stop=i == 3 * KC - 1)
                    ins.then_inc(gates_full, 1)

                def begin3(k, par):
                    pe.wait_ge(E_ready, k + 1)
                    for j in range(TB):
                        for g, row in enumerate((a_row, E_row)):
                            at = S + (2 * j + g) * NH
                            ins = nc.tensor.matmul(pG[:, at:at + NH], row[:, j * P:(j + 1) * P], core.ident[0:NH, 0:NH],
                                                   start=True, stop=True)
                    ins.then_inc(tok_full, 1)

                def scores(k, par, h):
                    c, r_ = h // 2, slice((h % 2) * DH, (h % 2 + 1) * DH)
                    if not (isinstance(k, int) and k == 0 and h < 2):
                        pe.wait_ge(c_ready, k * NH + h - 1)
                    nc.tensor.matmul(pQ[h % 2][:, 0:S], ctxT[par][r_, c, 0:P], xnT[par][r_, c, :], start=True, stop=True)
                    nc.tensor.matmul(pQ[h % 2][:, S:HC], ctxT[par][r_, c, P:S], xnT[par][r_, c, P:S],
                                     start=True, stop=True).then_inc(qk_ready, 1)
                    if not (isinstance(k, int) and k == 0 and h < 2):
                        pe.wait_ge(decay_ready, k * NH + h - 1)
                    for cols, queries in ((slice(0, S), slice(0, S)), (slice(S, HC), slice(P, S))):
                        nc.tensor.matmul(pD[h % 2][:, cols], sel[:, h, :], M[par][:, queries], start=True, stop=False)
                        ins = nc.tensor.matmul(pD[h % 2][:, cols], core.ident_b[:, :], mask[:, 0:cols.stop - cols.start],
                                               start=False, stop=True)
                    ins.then_inc(d_ready, 1)

                def times_v(k, par, h):
                    pe.wait_ge(c_ready, k * NH + h + 1)
                    if h == 0 and not (isinstance(k, int) and k == 0):
                        pe.wait_ge(o_taken, k)
                    out = slice(h * W1, (h + 1) * W1)
                    nc.tensor.matmul(pO[0][:, out], c_T[:, h % 2, 0:P], v[par][:, 0, h, :], start=True, stop=True)
                    nc.tensor.matmul(pO[1][:, out], c_T[:, h % 2, P:S], v[par][:, 0, h, :], start=True, stop=False)
                    nc.tensor.matmul(pO[1][:, out], c_T[:, h % 2, S:HC], v[par][:, 1, h, :], start=False, stop=True)\
                      .then_inc(pv_done, 1)

                def round_(k, par, half, has):
                    pe.wait_ge(v_in[par], 32 * (half + 1))
                    scores(k, par, 0)
                    if has[1]:
                        begin1(k + 1, 1 - par)
                    scores(k, par, 1)
                    times_v(k, par, 0)
                    if has[1]:
                        begin2(k + 1, 1 - par, half + par)
                    scores(k, par, 2)
                    times_v(k, par, 1)
                    scores(k, par, 3)
                    times_v(k, par, 2)
                    times_v(k, par, 3)
                    if has[1]:
                        begin3(k + 1, 1 - par)
                pe.wait_ge(setup, 1)
                begin1(0, 0)
                begin2(0, 0, 0)
                begin3(0, 0)
                pe.wait_ge(tok_ready, 1)
                staggered(pe, n, round_)


def routed_low_rank(core):
    nc, X, dram = core.nc, core.X, core.dram
    E, R, PROJ = 4, 8, 64
    TEMP_MAX = float(np.log(1.0 / 0.01))
    n = B
    nt = TB * n
    with ExitStack() as ctx:
        def sb(name, shape, dt=F32):
            return ctx.enter_context(nc.sbuf_tensor(f"L1f_{name}", shape, dt))

        xnT = sb("xnT", [P, KC, NT * P])
        zT = sb("zT", [E * R, NT * P])
        logit = sb("logit", [P, NT, E + 1])
        weight = sb("weight", [P, NT, E])
        WT = sb("WT", [P, KC, D])
        WuT = sb("WuT", [P, D])

        first = ExitStack()
        with first:
            def sb1(name, shape, dt=F32):
                return first.enter_context(nc.sbuf_tensor(f"L1f_{name}", shape, dt))

            def sem1(name):
                return first.enter_context(nc.semaphore(f"L1f_{name}"))

            def ps1(name):
                return first.enter_context(nc.psum_tensor(f"L1f_{name}", [P, 512], F32))
            WpdT = sb1("WpdT", [P, KC, PROJ + E * R])
            bp = sb1("bp", [PROJ, 1])
            sim = sb1("sim", [PROJ, E])
            sim_sq, sim_n = sb1("sim_sq", [PROJ, E]), sb1("sim_n", [PROJ, E])
            ones = sb1("ones", [PROJ, PROJ])
            gate_w = sb1("gate_w", [P, E + 1])
            temp = sb1("temp", [P, 1])
            prefer = sb1("prefer", [P, E])
            xn = sb1("xn", [P, TB, D])
            proj = [sb1(f"proj{i}", [P, S]) for i in range(2)]
            root, fac = sb1("root", [P, NT]), sb1("fac", [P, NT])
            top, total = sb1("top", [P, NT]), sb1("total", [P, NT])
            l4, e4, m4 = (sb1(s, [P, NT, E]) for s in ("l4", "e4", "m4"))
            pX, pP, pL = ([ps1(f"{s}{i}") for i in range(2)] for s in ("pX", "pP", "pL"))
            w_in, xn_ready, xT_full, xT_ready = (sem1(s) for s in ("w_in", "xn_ready", "xT_full", "xT_ready"))
            p_full, p_ready, sq_ready, l_full, l_ready, z_ready = (sem1(s) for s in (
                "p_full", "p_ready", "sq_ready", "l_full", "l_ready", "z_ready"))
            ones_ready, sim_sum, sim_root, gate_ready, step, wu_zero = (sem1(s) for s in (
                "ones_ready", "sim_sum", "sim_root", "gate_ready", "step", "wu_zero"))
            root_ready, temp_ready, d_ready, e_ready, n_ready = (sem1(s) for s in (
                "root_ready", "temp_ready", "d_ready", "e_ready", "n_ready"))
            with nc.Block() as block:
                @block.sync
                def _(sp):
                    sp.dma_start(WpdT[:, :, :], dram["L1f_WpdT"].rearrange("(c p) n -> p c n", p=P)).then_inc(w_in, 16)
                    sp.dma_start(bp[:, :], dram["L1f_bp"].rearrange("(p o) -> p o", o=1),
                                 allow_slow_non_contiguous=True).then_inc(w_in, 16)
                    sp.dma_start(sim[:, :], dram["L1f_sim"]).then_inc(w_in, 16)
                    sp.dma_start(temp[:, :], dram["L1f_temp"].partition_broadcast(P)).then_inc(w_in, 16)
                    sp.dma_start(prefer[:, :], dram["L1f_prefer"].partition_broadcast(P)).then_inc(w_in, 16)
                    sp.dma_start(WT[:, :, :], dram["L1f_WT"].rearrange("(c p) n -> p c n", p=P)).then_inc(w_in, 16)
                    sp.wait_ge(wu_zero, 1)
                    sp.dma_start(WuT[0:E * R, :], dram["L1f_WuT"]).then_inc(w_in, 16)
                    sp.wait_ge(w_in, 16 * 7)

                @block.scalar
                def _(act):
                    act.wait_ge(sim_sum, 1)
                    nc.scalar.activation(sim_n[:, :], pP[0][0:PROJ, 0:E], ACT.Sqrt).then_inc(sim_root, 1)

                    def take_xT(k, par):
                        act.wait_ge(xT_full, k + 1)
                        nc.scalar.activation(xnT[:, :, bass.ds(k * S, S)],
                                             pX[par][:, :].rearrange("p (c s) -> p c s", c=KC), ACT.Copy)\
                          .then_inc(xT_ready, 1)

                    def round_(k, par, half, has):
                        if has[1]:
                            take_xT(k + 1, 1 - par)
                        act.wait_ge(p_full, k + 1)
                        if not (isinstance(k, int) and k < 2):
                            act.wait_ge(l_full, k - 1)
                        nc.scalar.activation(proj[par][0:PROJ, :], pP[par][0:PROJ, 0:S], ACT.Identity, bias=bp[:, :])\
                          .then_inc(p_ready, 1)
                        nc.scalar.activation(proj[par][PROJ:P, :], pP[par][0:PROJ, 0:S], ACT.Square, bias=bp[:, :])\
                          .then_inc(sq_ready, 1)
                        nc.scalar.activation(zT[:, bass.ds(k * S, S)], pP[par][PROJ:PROJ + E * R, 0:S], ACT.Copy)\
                          .then_inc(z_ready, 1)
                    take_xT(0, 0)
                    act.wait_ge(w_in, 16 * 7)
                    staggered(act, n, round_)
                    act.wait_ge(n_ready, 1)
                    nc.scalar.activation(root[:, 0:nt], fac[:, 0:nt], ACT.Sqrt).then_inc(root_ready, 1)
                    act.wait_ge(temp_ready, 1)
                    nc.scalar.activation(temp[:, :], temp[:, :], ACT.Exp).then_inc(e_ready, 1)
                    act.wait_ge(d_ready, 1)
                    nc.scalar.activation(e4[:, 0:nt, :], l4[:, 0:nt, :], ACT.Exp).then_inc(e_ready, 1)

                @block.vector
                def _(dve):
                    done = [0]

                    def then_wait(ins):
                        done[0] += 1
                        ins.then_inc(step, 1)
                        dve.wait_ge(step, done[0])

                    nc.vector.memset(ones[:, :], 1.0)
                    nc.vector.memset(WuT[:, :], 0.0).then_inc(wu_zero, 1)
                    nc.vector.memset(gate_w[:, :], 0.0)
                    dve.wait_ge(w_in, 16 * 7)
                    nc.vector.tensor_tensor(sim_sq[:, :], sim[:, :], sim[:, :], ALU.mult).then_inc(ones_ready, 1)
                    nc.vector.tensor_scalar(temp[:, :], temp[:, :], TEMP_MAX, None, ALU.min).then_inc(temp_ready, 1)
                    dve.wait_ge(sim_root, 1)
                    then_wait(nc.vector.tensor_scalar(sim_n[:, :], sim_n[:, :], 1e-12, None, ALU.max))
                    then_wait(nc.vector.reciprocal(sim_sq[:, :], sim_n[:, :]))
                    nc.vector.tensor_tensor(gate_w[0:PROJ, 0:E], sim[:, :], sim_sq[:, :], ALU.mult)
                    nc.vector.memset(gate_w[PROJ:P, E:E + 1], 1.0).then_inc(gate_ready, 1)

                    def normalize(k, par):
                        for j in range(TB):
                            t = TB * k + j
                            ins = nc.vector.tensor_scalar(xn[:, j, :], flat(X[:, bass.ds(t, 1), :]),
                                                          core.mean[:, bass.ds(t, 1)], core.rstd[:, bass.ds(t, 1)],
                                                          ALU.subtract, ALU.mult)
                        ins.then_inc(xn_ready, 1)

                    def round_(k, par, half, has):
                        if has[2]:
                            dve.wait_ge(xT_full, k + 2)
                            normalize(k + 2, par)
                        dve.wait_ge(l_full, k + 1)
                        nc.vector.tensor_copy(logit[:, bass.ds(TB * k, TB), :],
                                              pL[par][:, 0:TB * (E + 1)].rearrange("p (j e) -> p j e", j=TB))\
                          .then_inc(l_ready, 1)
                    normalize(0, 0)
                    dve.wait_ge(xT_full, 1)
                    normalize(1, 1)
                    staggered(dve, n, round_)
                    dve.wait_ge(l_ready, n)
                    nc.vector.tensor_copy(fac[:, 0:nt], logit[:, 0:nt, E]).then_inc(n_ready, 1)
                    dve.wait_ge(root_ready, 1)
                    dve.wait_ge(e_ready, 1)
                    then_wait(nc.vector.tensor_scalar(root[:, 0:nt], root[:, 0:nt], 1e-12, None, ALU.max))
                    then_wait(nc.vector.reciprocal(fac[:, 0:nt], root[:, 0:nt]))
                    then_wait(nc.vector.tensor_scalar(fac[:, 0:nt], fac[:, 0:nt], temp[:, :], None, ALU.mult))
                    wide = lambda ap: ap.unsqueeze(2).to_broadcast([P, nt, E])
                    then_wait(nc.vector.tensor_tensor(l4[:, 0:nt, :], logit[:, 0:nt, 0:E], wide(fac[:, 0:nt]), ALU.mult))
                    then_wait(nc.vector.tensor_reduce(top[:, 0:nt], l4[:, 0:nt, :], AX.X, ALU.max))
                    nc.vector.tensor_tensor(l4[:, 0:nt, :], l4[:, 0:nt, :], wide(top[:, 0:nt]), ALU.subtract)\
                      .then_inc(d_ready, 1)
                    dve.wait_ge(d_ready, 1)
                    then_wait(nc.vector.tensor_scalar(m4[:, 0:nt, :], l4[:, 0:nt, :], 0.0, None, ALU.is_ge))
                    then_wait(nc.vector.tensor_tensor(m4[:, 0:nt, :], m4[:, 0:nt, :],
                                                      prefer[:, :].unsqueeze(1).to_broadcast([P, nt, E]), ALU.mult))
                    then_wait(nc.vector.tensor_reduce(top[:, 0:nt], m4[:, 0:nt, :], AX.X, ALU.max))
                    then_wait(nc.vector.tensor_tensor(m4[:, 0:nt, :], m4[:, 0:nt, :], wide(top[:, 0:nt]), ALU.is_equal))
                    dve.wait_ge(e_ready, 2)
                    then_wait(nc.vector.tensor_reduce(total[:, 0:nt], e4[:, 0:nt, :], AX.X, ALU.add))
                    then_wait(nc.vector.reciprocal(top[:, 0:nt], total[:, 0:nt]))
                    nc.vector.tensor_tensor(weight[:, 0:nt, :], m4[:, 0:nt, :], wide(top[:, 0:nt]), ALU.mult)

                @block.tensor
                def _(pe):
                    pe.wait_ge(ones_ready, 1)
                    nc.tensor.matmul(pP[0][0:PROJ, 0:E], ones[:, :], sim_sq[:, :], start=True, stop=True)\
                      .then_inc(sim_sum, 1)

                    def transpose_x(k, par):
                        pe.wait_ge(xn_ready, k + 1)
                        if not (isinstance(k, int) and k < 2):
                            pe.wait_ge(xT_ready, k - 1)
                        for c in range(KC):
                            for j in range(TB):
                                ins = nc.tensor.transpose(pX[par][:, c * S + j * P:c * S + (j + 1) * P],
                                                          xn[:, j, c * P:(c + 1) * P], core.ident[:, :])
                        ins.then_inc(xT_full, 1)

                    def project(k, par):
                        pe.wait_ge(xT_ready, k + 1)
                        if not (isinstance(k, int) and k < 2):
                            pe.wait_ge(p_ready, k - 1)
                            pe.wait_ge(z_ready, k - 1)
                        for c in range(KC):
                            ins = nc.tensor.matmul(pP[par][0:PROJ + E * R, 0:S], WpdT[:, c, :],
                                                   xnT[:, c, bass.ds(k * S, S)], start=c == 0, stop=c == KC - 1)
                        ins.then_inc(p_full, 1)

                    def gate(k, par):
                        pe.wait_ge(p_ready, k + 1)
                        pe.wait_ge(sq_ready, k + 1)
                        if not (isinstance(k, int) and k < 2):
                            pe.wait_ge(l_ready, k - 1)
                        for j in range(TB):
                            ins = nc.tensor.matmul(pL[par][:, j * (E + 1):(j + 1) * (E + 1)],
                                                   proj[par][:, j * P:(j + 1) * P], gate_w[:, :], start=True, stop=True)
                        ins.then_inc(l_full, 1)

                    def round_(k, par, half, has):
                        if has[1]:
                            transpose_x(k + 1, 1 - par)
                            project(k + 1, 1 - par)
                        gate(k, par)
                    pe.wait_ge(w_in, 16 * 7)
                    pe.wait_ge(sim_root, 1)
                    transpose_x(0, 0)
                    project(0, 0)
                    pe.wait_ge(gate_ready, 1)
                    staggered(pe, n, round_)

        second = ExitStack()
        with second:
            def sb2(name, shape, dt=F32):
                return second.enter_context(nc.sbuf_tensor(f"L1f_{name}", shape, dt))

            def sem2(name):
                return second.enter_context(nc.semaphore(f"L1f_{name}"))

            def ps2(name):
                return second.enter_context(nc.psum_tensor(f"L1f_{name}", [P, 512], F32))
            wide8 = [sb2(f"wide8{i}", [P, TB, E, R]) for i in range(2)]
            zw = [sb2(f"zw{i}", [P, S]) for i in range(2)]
            xTs = [sb2(f"xTs{i}", [P, KC, S]) for i in range(2)]
            pW = [ps2(f"pW{i}") for i in range(2)]
            pY = [ps2(f"pY{i}") for i in range(2)]
            wide_ready, w_full, zw_ready, xs_ready, y_ready, x_new, zero = (sem2(s) for s in (
                "wide_ready", "w_full", "zw_ready", "xs_ready", "y_ready", "x_new", "zero"))
            with nc.Block() as block:
                @block.scalar
                def _(act):
                    def bring(k, par):
                        nc.scalar.activation(xTs[par][:, :, :], xnT[:, :, bass.ds(k * S, S)], ACT.Copy)\
                          .then_inc(xs_ready, 1)

                    def round_(k, par, half, has):
                        if has[2]:
                            act.wait_ge(y_ready, k + 1)
                            bring(k + 2, par)
                    bring(0, 0)
                    bring(1, 1)
                    staggered(act, n, round_)

                @block.vector
                def _(dve):
                    for i in range(2):
                        ins = nc.vector.memset(zw[i][:, :], 0.0)
                    ins.then_inc(zero, 1)
                    dve.wait_ge(zero, 1)

                    def widen(k, par):
                        nc.vector.tensor_copy(wide8[par][:, :, :, :].rearrange("p j e r -> p (j e) r"),
                                              weight[:, bass.ds(TB * k, TB), :].rearrange("p j e -> p (j e)")
                                              .unsqueeze(2).to_broadcast([P, TB * E, R])).then_inc(wide_ready, 1)

                    def round_(k, par, half, has):
                        dve.wait_ge(w_full, k + 1)
                        nc.vector.tensor_tensor(zw[par][0:E * R, :], pW[par][0:E * R, 0:S], zT[:, bass.ds(k * S, S)],
                                                ALU.mult).then_inc(zw_ready, 1)
                        if has[2]:
                            widen(k + 2, par)
                        dve.wait_ge(y_ready, k + 1)
                        x_b = X[:, bass.ds(TB * k, TB), :]
                        nc.vector.tensor_tensor(x_b, pY[par][:, :].rearrange("p (j d) -> p j d", j=TB), x_b, ALU.add)\
                          .then_inc(x_new, 1)
                        dve.wait_ge(x_new, k + 1)
                        for j in range(TB):
                            t = TB * k + j
                            nc.vector.bn_stats(flat(core.stats[:, bass.ds(t, 1), :]), flat(X[:, bass.ds(t, 1), :]))
                    widen(0, 0)
                    widen(1, 1)
                    staggered(dve, n, round_)

                @block.tensor
                def _(pe):
                    def weights(k, par):
                        pe.wait_ge(wide_ready, k + 1)
                        if not (isinstance(k, int) and k < 2):
                            pe.wait_ge(zw_ready, k - 1)
                        for j in range(TB):
                            ins = nc.tensor.transpose(pW[par][0:E * R, j * P:(j + 1) * P],
                                                      wide8[par][:, j, :, :].rearrange("p e r -> p (e r)"),
                                                      core.ident[:, :])
                        ins.then_inc(w_full, 1)

                    def round_(k, par, half, has):
                        if has[1]:
                            weights(k + 1, 1 - par)
                        pe.wait_ge(xs_ready, k + 1)
                        if not (isinstance(k, int) and k < 2):
                            pe.wait_ge(x_new, k - 1)
                        pe.wait_ge(zw_ready, k + 1)
                        for j in range(TB):
                            out = pY[par][:, j * D:(j + 1) * D]
                            for c in range(KC):
                                nc.tensor.matmul(out, xTs[par][:, c, j * P:(j + 1) * P], WT[:, c, :],
                                                 start=c == 0, stop=False)
                            ins = nc.tensor.matmul(out, zw[par][:, j * P:(j + 1) * P], WuT[:, :], start=False, stop=True)
                        ins.then_inc(y_ready, 1)
                    pe.wait_ge(zero, 1)
                    weights(0, 0)
                    staggered(pe, n, round_)


def int8_ffn(core):
    nc, X, dram = core.nc, core.X, core.dram
    F = 704
    FC = -(-F // P)
    n = B
    with ExitStack() as ctx:
        def sb(name, shape, dt=F32):
            return ctx.enter_context(nc.sbuf_tensor(f"L2f_{name}", shape, dt))

        def ps(name):
            return ctx.enter_context(nc.psum_tensor(f"L2f_{name}", [P, 512], F32))

        def sem(name):
            return ctx.enter_context(nc.semaphore(f"L2f_{name}"))

        hT = sb("hT", [P, FC, NT * P])
        wg, wu = (sb(n_, [P, KC, FC * P], BF16) for n_ in ("wg", "wu"))
        wd = sb("wd", [P, FC, D], BF16)
        sg_col, su_col = sb("sg_col", [P, FC]), sb("su_col", [P, FC])
        gate_scale, up_scale = sb("gate_scale", [P, FC]), sb("up_scale", [P, FC])
        down_row = sb("down_row", [P, D])
        ones = sb("ones", [P, P])
        xabs = sb("xabs", [P, NT])
        habs = sb("habs", [P, n])
        top = sb("top", [P, 2])
        top_row = sb("top_row", [1, P])
        top_one = sb("top_one", [1, 2])
        clip = sb("clip", [P, 2])
        sx, inv_sx, sh, inv_sh = (sb(n_, [P, 1]) for n_ in ("sx", "inv_sx", "sh", "inv_sh"))

        block1 = ExitStack()
        with block1:
            def sb1(name, shape, dt=F32):
                return block1.enter_context(nc.sbuf_tensor(f"L2f_{name}", shape, dt))
            w32 = [sb1(f"w32_{i}", [P, FC, D]) for i in range(2)]
            wd32 = sb1("wd32", [P, KC, FC * P])
            wr = sb1("wr", [P, FC * D])
            wi = sb1("wi", [P, FC * D], BF16)
            wmax, winv = sb1("wmax", [P, FC]), sb1("winv", [P, FC])
            sd_col = sb1("sd_col", [P, KC])
            diag = sb1("diag", [P, KC, P])
            xt = sb1("xt", [P, TB, D])
            pW = [block1.enter_context(nc.psum_tensor(f"L2f_pW{i}", [P, 512], F32)) for i in range(2)]
            pR = block1.enter_context(nc.psum_tensor("L2f_pR", [P, 512], F32))
            w_in = [block1.enter_context(nc.semaphore(f"L2f_w_in{i}")) for i in range(3)]
            clip_in = block1.enter_context(nc.semaphore("L2f_clip_in"))
            sem1 = lambda name: block1.enter_context(nc.semaphore(f"L2f_{name}"))
            wstep, wi_ready, wT_full, wT_taken = sem1("wstep"), sem1("wi_ready"), sem1("wT_full"), sem1("wT_taken")
            x_step, diag_ready, row_ready, sig_ready = sem1("x_step"), sem1("diag_ready"), sem1("row_ready"), sem1("sig_ready")
            top_ready, topT_ready, one_ready, all_ready = (sem1(s) for s in ("top_ready", "topT_ready", "one_ready",
                                                                          "all_ready"))
            with nc.Block() as block:
                @block.sync
                def _(sp):
                    for i, name in enumerate(("L2f_wg", "L2f_wu")):
                        sp.dma_start(w32[i][:, :, :], dram[name].rearrange("(c p) n -> p c n", p=P)).then_inc(w_in[i], 16)
                    sp.dma_start(wd32[:, :, :], dram["L2f_wd"].rearrange("(c p) n -> p c n", p=P)).then_inc(w_in[2], 16)
                    for i, name in enumerate(("L2f_clip_x", "L2f_clip_down")):
                        sp.dma_start(clip[:, i:i + 1], dram[name].partition_broadcast(P)).then_inc(clip_in, 16)

                plans = [(w32[0], FC, KC, wg), (w32[1], FC, KC, wu), (wd32, KC, FC, wd)]
                blocks = [(i, c, m) for i, (_, rows_, cols_, _) in enumerate(plans)
                          for c in range(rows_) for m in range(cols_)]
                groups = [blocks[j:j + 4] for j in range(0, len(blocks), 4)]

                @block.scalar
                def _(act):
                    act.wait_ge(clip_in, 32)
                    nc.scalar.activation(clip[:, :], clip[:, :], ACT.Sigmoid).then_inc(sig_ready, 1)
                    for g, group in enumerate(groups):
                        act.wait_ge(wT_full, g + 1)
                        for q, (i, c, m) in enumerate(group):
                            ins = nc.scalar.activation(plans[i][3][:, m, c * P:(c + 1) * P],
                                                       pW[g % 2][:, q * P:(q + 1) * P], ACT.Copy)
                        ins.then_inc(wT_taken, 1)

                @block.vector
                def _(dve):
                    steps = [0]

                    def then_wait(ins):
                        steps[0] += 1
                        ins.then_inc(wstep, 1)
                        dve.wait_ge(wstep, steps[0])

                    nc.vector.memset(ones[:, :], 1.0)
                    for i, (w, rows_, cols_, _) in enumerate(plans):
                        width = cols_ * P
                        dve.wait_ge(w_in[i], 16)
                        then_wait(nc.vector.tensor_reduce(wmax[:, 0:rows_], w[:, :, :], AX.X, ALU.max,
                                                          apply_absolute_value=True))
                        scale = (sg_col, su_col, sd_col)[i]
                        then_wait(nc.vector.tensor_scalar(scale[:, 0:rows_], wmax[:, 0:rows_], 1e-30, 1.0 / 127.0,
                                                          ALU.max, ALU.mult))
                        then_wait(nc.vector.reciprocal(winv[:, 0:rows_], scale[:, 0:rows_]))
                        if i:
                            dve.wait_ge(wT_full, sum(1 for group in groups if group[0][0] < i))
                        for c in range(rows_):
                            ins = nc.vector.tensor_scalar(wr[:, c * width:(c + 1) * width], w[:, c, :],
                                                          winv[:, c:c + 1], ROUND, ALU.mult, ALU.add)
                        then_wait(ins)
                        nc.vector.tensor_scalar(wi[:, :], wr[:, :], ROUND, None, ALU.subtract).then_inc(wi_ready, 1)
                    for c in range(KC):
                        ins = nc.vector.tensor_scalar(diag[:, c, :], core.ident[:, :], sd_col[:, c:c + 1], None, ALU.mult)
                    ins.then_inc(diag_ready, 1)
                    dve.wait_ge(row_ready, 1)
                    nc.vector.tensor_copy(down_row[:, :], pR[:, 0:D])
                    with dve.Fori(0, n) as i:
                        for j in range(TB):
                            t = TB * i + j
                            nc.vector.tensor_scalar(xt[:, j, :], flat(X[:, bass.ds(t, 1), :]),
                                                    core.mean[:, bass.ds(t, 1)], core.rstd[:, bass.ds(t, 1)],
                                                    ALU.subtract, ALU.mult).then_inc(x_step, 1)
                            dve.wait_ge(x_step, 2 * t + 1)
                            nc.vector.tensor_reduce(xabs[:, bass.ds(t, 1)], xt[:, j, :], AX.X, ALU.max,
                                                    apply_absolute_value=True).then_inc(x_step, 1)
                    dve.wait_ge(x_step, 2 * TB * n)
                    nc.vector.tensor_reduce(top[:, 0:1], xabs[:, 0:TB * n], AX.X, ALU.max).then_inc(top_ready, 1)
                    dve.wait_ge(topT_ready, 1)
                    nc.vector.tensor_reduce(top_one[:, 0:1], pR[0:1, 256:256 + P], AX.X, ALU.max).then_inc(one_ready, 1)
                    dve.wait_ge(all_ready, 1)
                    dve.wait_ge(sig_ready, 1)
                    then_wait(nc.vector.tensor_scalar(sx[:, :], pR[:, 384:385], clip[:, 0:1], 1.0 / 127.0,
                                                      ALU.mult, ALU.mult))
                    then_wait(nc.vector.reciprocal(inv_sx[:, :], sx[:, :]))
                    nc.vector.tensor_scalar(gate_scale[:, :], sg_col[:, :], sx[:, :], None, ALU.mult)
                    nc.vector.tensor_scalar(up_scale[:, :], su_col[:, :], sx[:, :], None, ALU.mult)
                    nc.vector.tensor_scalar(core.rstd[:, :], core.rstd[:, :], inv_sx[:, :], None, ALU.mult)

                @block.tensor
                def _(pe):
                    seen = -1
                    for g, group in enumerate(groups):
                        if group[-1][0] != seen:
                            seen = group[-1][0]
                            pe.wait_ge(wi_ready, seen + 1)
                        if g >= 2:
                            pe.wait_ge(wT_taken, g - 1)
                        for q, (i, c, m) in enumerate(group):
                            at = (c * plans[i][2] + m) * P
                            ins = nc.tensor.matmul(pW[g % 2][:, q * P:(q + 1) * P], wi[:, at:at + P],
                                                   core.ident_b[:, :], start=True, stop=True)
                        ins.then_inc(wT_full, 1)
                    pe.wait_ge(diag_ready, 1)
                    for c in range(KC):
                        ins = nc.tensor.matmul(pR[:, c * P:(c + 1) * P], ones[:, :], diag[:, c, :],
                                               start=True, stop=True)
                    ins.then_inc(row_ready, 1)
                    pe.wait_ge(top_ready, 1)
                    nc.tensor.transpose(pR[0:1, 256:256 + P], top[:, 0:1], core.ident[:, :]).then_inc(topT_ready, 1)
                    pe.wait_ge(one_ready, 1)
                    nc.tensor.matmul(pR[:, 384:385], ones[0:1, :], top_one[:, 0:1], start=True, stop=True)\
                      .then_inc(all_ready, 1)

        block2 = ExitStack()
        with block2:
            def sb2(name, shape, dt=F32):
                return block2.enter_context(nc.sbuf_tensor(f"L2f_{name}", shape, dt))

            def sem2(name):
                return block2.enter_context(nc.semaphore(f"L2f_{name}"))
            xs = sb2("xs", [P, TB, D])
            xc = sb2("xc", [P, TB, D])
            a = sb2("a", [P, 2, TB, D], BF16)
            aT = sb2("aT", [P, 2, KC, S], BF16)
            sg = sb2("sg", [P, FC, S])
            NP2 = FC // 2
            pA = block2.enter_context(nc.psum_tensor("L2f_pA", [P, 512], F32))
            pG = [block2.enter_context(nc.psum_tensor(f"L2f_pG{i}", [P, 512], F32)) for i in range(NP2)]
            pU = [block2.enter_context(nc.psum_tensor(f"L2f_pU{i}", [P, 512], F32)) for i in range(NP2)]
            astep, a_ready, aT_full, aT_ready = sem2("astep"), sem2("a_ready"), sem2("aT_full"), sem2("aT_ready")
            g_ready, u_ready, sg_ready, h_ready = sem2("g_ready"), sem2("u_ready"), sem2("sg_ready"), sem2("h_ready")
            with nc.Block() as block:
                @block.scalar
                def _(act):
                    def take_aT(k, par):
                        act.wait_ge(aT_full, k + 1)
                        nc.scalar.activation(aT[:, par, :, :], pA[:, :].rearrange("p (c s) -> p c s", c=KC), ACT.Copy)\
                          .then_inc(aT_ready, 1)

                    def round_(k, par, half, has):
                        if has[1]:
                            take_aT(k + 1, 1 - par)
                        for g in range(NP2):
                            act.wait_ge(g_ready, NP2 * k + g + 1)
                            if not (isinstance(k, int) and k == 0):
                                act.wait_ge(h_ready, NP2 * k - NP2 + g + 1)
                            for c in range(2):
                                cc = 2 * g + c
                                ins = nc.scalar.activation(sg[:, cc, :], pG[g][:, c * S:(c + 1) * S], ACT.Silu,
                                                           scale=gate_scale[:, cc:cc + 1])
                            ins.then_inc(sg_ready, 1)
                    take_aT(0, 0)
                    staggered(act, n, round_)

                @block.vector
                def _(dve):
                    def integers(k, par):
                        for j in range(TB):
                            t = TB * k + j
                            nc.vector.tensor_scalar(xs[:, j, :], flat(X[:, bass.ds(t, 1), :]),
                                                    core.mean[:, bass.ds(t, 1)], core.rstd[:, bass.ds(t, 1)],
                                                    ALU.subtract, ALU.mult).then_inc(astep, 1)
                        dve.wait_ge(astep, 3 * k + 2)
                        nc.vector.tensor_scalar(xc[:, :, :], xs[:, :, :], 127.0, -128.0, ALU.min, ALU.max).then_inc(astep, 1)
                        dve.wait_ge(astep, 3 * k + 3)
                        nc.vector.tensor_scalar(a[:, par, :, :], xc[:, :, :], ROUND, ROUND, ALU.add, ALU.subtract)\
                          .then_inc(a_ready, 1)

                    def round_(k, par, half, has):
                        for g in range(NP2):
                            dve.wait_ge(sg_ready, NP2 * k + g + 1)
                            dve.wait_ge(u_ready, NP2 * k + g + 1)
                            for c in range(2):
                                cc = 2 * g + c
                                ins = nc.vector.scalar_tensor_tensor(
                                    hT[:, cc, bass.ds(k * S, S)], pU[g][:, c * S:(c + 1) * S],
                                    up_scale[:, cc:cc + 1], sg[:, cc, :], ALU.mult, ALU.mult)
                            ins.then_inc(h_ready, 1)
                            if g == 0 and has[2]:
                                integers(k + 2, par)
                        dve.wait_ge(h_ready, NP2 * k + NP2)
                        nc.vector.tensor_reduce(habs[:, bass.ds(k, 1)], hT[:, :, bass.ds(k * S, S)], AX.XY, ALU.max,
                                                apply_absolute_value=True)
                    integers(0, 0)
                    integers(1, 1)
                    staggered(dve, n, round_)

                @block.tensor
                def _(pe):
                    def transpose_a(k, par):
                        pe.wait_ge(a_ready, k + 1)
                        if not (isinstance(k, int) and k == 0):
                            pe.wait_ge(aT_ready, k)
                        for c in range(KC):
                            for j in range(TB):
                                ins = nc.tensor.matmul(pA[:, c * S + j * P:c * S + (j + 1) * P],
                                                       a[:, par, j, c * P:(c + 1) * P], core.ident_b[:, :],
                                                       start=True, stop=True)
                        ins.then_inc(aT_full, 1)

                    def round_(k, par, half, has):
                        if has[1]:
                            transpose_a(k + 1, 1 - par)
                        pe.wait_ge(aT_ready, k + 1)
                        for g in range(NP2):
                            if not (isinstance(k, int) and k == 0):
                                pe.wait_ge(h_ready, NP2 * k - NP2 + g + 1)
                            for w, bank, ready in ((wg, pG[g], g_ready), (wu, pU[g], u_ready)):
                                for c in range(2):
                                    for kc in range(KC):
                                        cc = 2 * g + c
                                        ins = nc.tensor.matmul(bank[:, c * S:(c + 1) * S],
                                                               w[:, kc, cc * P:(cc + 1) * P], aT[:, par, kc, :],
                                                               start=kc == 0, stop=kc == KC - 1)
                                ins.then_inc(ready, 1)
                    transpose_a(0, 0)
                    staggered(pe, n, round_)

        block3 = ExitStack()
        with block3:
            def sb3(name, shape, dt=F32):
                return block3.enter_context(nc.sbuf_tensor(f"L2f_{name}", shape, dt))

            def sem3(name):
                return block3.enter_context(nc.semaphore(f"L2f_{name}"))
            hr = sb3("hr", [P, 2, FC * S])
            hq = sb3("hq", [P, 2, FC, S], BF16)
            out_scale = sb3("out_scale", [P, D])
            yt = sb3("yt", [P, TB, D])
            pY = [block3.enter_context(nc.psum_tensor(f"L2f_pY{i}", [P, 512], F32)) for i in range(2)]
            pR = block3.enter_context(nc.psum_tensor("L2f_pR3", [P, 512], F32))
            top_ready, topT_ready, one_ready, all_ready = (sem3(s) for s in ("top3", "topT3", "one3", "all3"))
            step3, scales_ready = sem3("step3"), sem3("scales_ready")
            hr_ready, clipped, hq_ready, y_ready, y_taken, x_new = (sem3(s) for s in ("hr_ready", "clipped",
                                                                    "hq_ready", "y_ready", "y_taken", "x_new3"))
            with nc.Block() as block:
                @block.scalar
                def _(act):
                    act.wait_ge(scales_ready, 1)
                    def scale_h(k, par):
                        nc.scalar.activation(hr[:, par, :].rearrange("p (c s) -> p c s", c=FC),
                                             hT[:, :, bass.ds(k * S, S)], ACT.Copy, bias=ROUND, scale=inv_sh[:, :])\
                          .then_inc(hr_ready, 1)

                    def round_(k, par, half, has):
                        if has[2]:
                            act.wait_ge(hq_ready, k + 1)
                            scale_h(k + 2, par)
                    scale_h(0, 0)
                    scale_h(1, 1)
                    staggered(act, n, round_)

                @block.vector
                def _(dve):
                    steps = [0]

                    def then_wait(ins):
                        steps[0] += 1
                        ins.then_inc(step3, 1)
                        dve.wait_ge(step3, steps[0])
                    nc.vector.tensor_reduce(top[:, 1:2], habs[:, :], AX.X, ALU.max).then_inc(top_ready, 1)
                    dve.wait_ge(topT_ready, 1)
                    nc.vector.tensor_reduce(top_one[:, 1:2], pR[0:1, 256:256 + P], AX.X, ALU.max).then_inc(one_ready, 1)
                    dve.wait_ge(all_ready, 1)
                    then_wait(nc.vector.tensor_scalar(sh[:, :], pR[:, 384:385], clip[:, 1:2], 1.0 / 127.0,
                                                      ALU.mult, ALU.mult))
                    nc.vector.reciprocal(inv_sh[:, :], sh[:, :]).then_inc(scales_ready, 1)
                    then_wait(nc.vector.tensor_scalar(out_scale[:, :], down_row[:, :], sh[:, :], None, ALU.mult))

                    def integers(k, par):
                        dve.wait_ge(hr_ready, k + 1)
                        nc.vector.tensor_scalar(hr[:, par, :], hr[:, par, :], ROUND + 127.0, ROUND - 128.0,
                                                ALU.min, ALU.max).then_inc(clipped, 1)
                        dve.wait_ge(clipped, k + 1)
                        nc.vector.tensor_scalar(hq[:, par, :, :].rearrange("p c s -> p (c s)"), hr[:, par, :],
                                                ROUND, None, ALU.subtract).then_inc(hq_ready, 1)

                    def round_(k, par, half, has):
                        if has[1]:
                            integers(k + 1, 1 - par)
                        dve.wait_ge(y_ready, k + 1)
                        for j in range(TB):
                            nc.vector.tensor_tensor(yt[:, j, :], pY[par][:, j * D:(j + 1) * D], out_scale[:, :],
                                                    ALU.mult).then_inc(y_taken, 1)
                        for j in range(TB):
                            x_t = flat(X[:, bass.ds(TB * k + j, 1), :])
                            dve.wait_ge(y_taken, TB * k + j + 1)
                            nc.vector.tensor_tensor(x_t, yt[:, j, :], x_t, ALU.add).then_inc(x_new, 1)
                        for j in range(TB):
                            x_t = flat(X[:, bass.ds(TB * k + j, 1), :])
                            dve.wait_ge(x_new, TB * k + j + 1)
                            nc.vector.bn_stats(flat(core.stats[:, bass.ds(TB * k + j, 1), :]), x_t)
                    integers(0, 0)
                    staggered(dve, n, round_)

                @block.tensor
                def _(pe):
                    pe.wait_ge(top_ready, 1)
                    nc.tensor.transpose(pR[0:1, 256:256 + P], top[:, 1:2], core.ident[:, :]).then_inc(topT_ready, 1)
                    pe.wait_ge(one_ready, 1)
                    nc.tensor.matmul(pR[:, 384:385], ones[0:1, :], top_one[:, 1:2], start=True, stop=True)\
                      .then_inc(all_ready, 1)

                    def round_(k, par, half, has):
                        pe.wait_ge(hq_ready, k + 1)
                        if not (isinstance(k, int) and k < 2):
                            pe.wait_ge(y_taken, TB * k - TB)
                        for j in range(TB):
                            for cc in range(FC):
                                ins = nc.tensor.matmul(pY[par][:, j * D:(j + 1) * D], hq[:, par, cc, j * P:(j + 1) * P],
                                                       wd[:, cc, :], start=cc == 0, stop=cc == FC - 1)
                        ins.then_inc(y_ready, 1)
                    staggered(pe, n, round_)


EXPERTS = 8
TILE = 256
MAX_TILES = 2 * B * S // TILE + EXPERTS


def routed_experts(core):
    nc, X, dram = core.nc, core.X, core.dram
    E, HID = EXPERTS, 1024
    HCH = HID // P
    n = B
    nt = TB * n
    gathered, expert_out = core.gathered, core.expert_out
    with ExitStack() as ctx:
        def sb(name, shape, dt=F32):
            return ctx.enter_context(nc.sbuf_tensor(f"L3f_{name}", shape, dt))

        slot = [sb(f"slot{i}", [P, NT], I32) for i in range(2)]
        weight = [sb(f"weight{i}", [P, NT]) for i in range(2)]
        bounds = sb("bounds", [1, 2 * E], I32)
        W1 = [sb(f"W1_{i}", [P, KC, HID]) for i in range(2)]
        W2 = [sb(f"W2_{i}", [P, HCH, D]) for i in range(2)]
        b1 = sb("b1", [P, E, HCH])
        b2 = [sb(f"b2_{i}", [P, D]) for i in range(2)]
        w_in = [ctx.enter_context(nc.semaphore(f"L3f_w_in{i}")) for i in range(2)]
        b1_in = ctx.enter_context(nc.semaphore("L3f_b1_in"))
        y_stored = ctx.enter_context(nc.semaphore("L3f_y_stored"))

        def load_expert(eng, e):
            par = e % 2
            eng.dma_start(W1[par][:, :, :], dram["L3f_W1"][e].rearrange("(c p) n -> p c n", p=P)).then_inc(w_in[par], 16)
            eng.dma_start(W2[par][:, :, :], dram["L3f_W2"][e].rearrange("(c p) n -> p c n", p=P)).then_inc(w_in[par], 16)
            eng.dma_start(b2[par][:, :], dram["L3f_b2"][e].partition_broadcast(P)).then_inc(w_in[par], 16)

        first = ExitStack()
        with first:
            def sb1(name, shape, dt=F32):
                return first.enter_context(nc.sbuf_tensor(f"L3f_{name}", shape, dt))

            def sem1(name):
                return first.enter_context(nc.semaphore(f"L3f_{name}"))

            def ps1(name):
                return first.enter_context(nc.psum_tensor(f"L3f_{name}", [P, 512], F32))
            XN = sb1("XN", [P, NT, D])
            xs = [sb1(f"xs{i}", [P, TB, D]) for i in range(2)]
            xT = [sb1(f"xT{i}", [P, KC, S]) for i in range(2)]
            Wg, bg, prefer = sb1("Wg", [P, KC, E]), sb1("bg", [P, E]), sb1("prefer", [P, E])
            tri, ones = sb1("tri", [P, P]), sb1("ones", [P, P])
            g, p8, hot1, hot2, both, pos = (sb1(s, [P, NT, E]) for s in ("g", "p8", "hot1", "hot2", "both", "pos"))
            top, total, p1, p2 = (sb1(s, [P, NT]) for s in ("top", "total", "p1", "p2"))
            per, cum, cex = (sb1(s, [P, E, NT]) for s in ("per", "cum", "cex"))
            onesT = sb1("onesT", [P, E * NT])
            cnt, tiles, tile_end, tile_start, base = (sb1(s, [P, E]) for s in ("cnt", "tiles", "tile_end",
                                                                               "tile_start", "base"))
            pX, pL = ([ps1(f"{s}{i}") for i in range(2)] for s in ("pX", "pL"))
            pW, pT = ps1("pW"), ps1("pT")
            c_in, xn_ready, xT_full, xT_ready, l_full, l_ready = (sem1(s) for s in (
                "c_in", "xn_ready", "xT_full", "xT_ready", "l_full", "l_ready"))
            step, d_ready, e_ready, counted, slots_ready, ones_ready, scattered = (sem1(s) for s in (
                "step", "d_ready", "e_ready", "counted", "slots_ready", "ones_ready", "scattered"))
            with nc.Block() as block:
                @block.sync
                def _(sp):
                    sp.dma_start(Wg[:, :, :], dram["L3f_Wg"].rearrange("(c p) n -> p c n", p=P)).then_inc(c_in, 16)
                    sp.dma_start(bg[:, :], dram["L3f_bg"].partition_broadcast(P)).then_inc(c_in, 16)
                    sp.dma_start(prefer[:, :], dram["L3f_prefer"].partition_broadcast(P)).then_inc(c_in, 16)
                    sp.dma_start(tri[:, :], dram["L3f_tri"]).then_inc(c_in, 16)
                    sp.dma_start(b1[:, :, :], dram["L3f_b1"].rearrange("e (c p) -> p e c", p=P),
                                 allow_slow_non_contiguous=True).then_inc(b1_in, 16)
                    load_expert(sp, 0)
                    load_expert(sp, 1)

                @block.scalar
                def _(act):
                    def round_(k, par, half, has):
                        act.wait_ge(xT_full, k + 1)
                        if not (isinstance(k, int) and k < 2):
                            act.wait_ge(l_full, k - 1)
                        nc.scalar.activation(xT[par][:, :, :], pX[par][:, :].rearrange("p (c s) -> p c s", c=KC),
                                             ACT.Copy).then_inc(xT_ready, 1)
                    staggered(act, n, round_)
                    act.wait_ge(d_ready, 1)
                    nc.scalar.activation(p8[:, 0:nt, :], g[:, 0:nt, :], ACT.Exp).then_inc(e_ready, 1)
                    act.wait_ge(d_ready, 2)
                    nc.scalar.activation(p2[:, 0:nt], p2[:, 0:nt], ACT.Exp).then_inc(e_ready, 1)

                @block.vector
                def _(dve):
                    nc.vector.memset(ones[:, :], 1.0)
                    nc.vector.memset(onesT[:, :], 1.0).then_inc(ones_ready, 1)

                    def normalize(k, par):
                        for j in range(TB):
                            t = TB * k + j
                            ins = nc.vector.tensor_scalar(xs[par][:, j, :], flat(X[:, bass.ds(t, 1), :]),
                                                          core.mean[:, bass.ds(t, 1)], core.rstd[:, bass.ds(t, 1)],
                                                          ALU.subtract, ALU.mult)
                        ins.then_inc(xn_ready, 1)
                        dve.wait_ge(xn_ready, k + 1)
                        nc.vector.tensor_copy(XN[:, bass.ds(TB * k, TB), :], xs[par][:, :, :])

                    def round_(k, par, half, has):
                        if has[1]:
                            if not (isinstance(k, int) and k < 1):
                                dve.wait_ge(xT_full, k)
                            normalize(k + 1, 1 - par)
                        dve.wait_ge(l_full, k + 1)
                        nc.vector.tensor_tensor(g[:, bass.ds(TB * k, TB), :],
                                                pL[par][:, 0:TB * E].rearrange("p (j e) -> p j e", j=TB),
                                                bg[:, :].unsqueeze(1).to_broadcast([P, TB, E]), ALU.add)\
                          .then_inc(l_ready, 1)
                    normalize(0, 0)
                    dve.wait_ge(c_in, 64)
                    staggered(dve, n, round_)
                    done = [0]

                    def then_wait(ins):
                        done[0] += 1
                        ins.then_inc(step, 1)
                        dve.wait_ge(step, done[0])

                    G, P8, H1, H2, BO, PO = (a[:, 0:nt, :] for a in (g, p8, hot1, hot2, both, pos))
                    wide = lambda ap: ap[:, 0:nt].unsqueeze(2).to_broadcast([P, nt, E])
                    every = lambda ap: ap[:, :].unsqueeze(1).to_broadcast([P, nt, E])
                    tt, red = nc.vector.tensor_tensor, nc.vector.tensor_reduce
                    dve.wait_ge(l_ready, n)
                    then_wait(red(top[:, 0:nt], G, AX.X, ALU.max))
                    tt(G, G, wide(top), ALU.subtract).then_inc(d_ready, 1)
                    dve.wait_ge(e_ready, 1)
                    then_wait(red(total[:, 0:nt], P8, AX.X, ALU.add))
                    then_wait(nc.vector.reciprocal(top[:, 0:nt], total[:, 0:nt]))
                    then_wait(tt(P8, P8, wide(top), ALU.mult))
                    for hot, best in ((H1, p1), (H2, p2)):
                        then_wait(red(best[:, 0:nt], P8, AX.X, ALU.max))
                        then_wait(tt(hot, P8, wide(best), ALU.is_equal))
                        then_wait(tt(hot, hot, every(prefer), ALU.mult))
                        then_wait(red(top[:, 0:nt], hot, AX.X, ALU.max))
                        then_wait(tt(hot, wide(top), every(prefer), ALU.is_equal))
                        if best is p1:
                            then_wait(nc.vector.scalar_tensor_tensor(
                                P8.rearrange("p t e -> p (t e)"), H1.rearrange("p t e -> p (t e)"), -2.0,
                                P8.rearrange("p t e -> p (t e)"), ALU.mult, ALU.add))
                    then_wait(tt(BO, H1, H2, ALU.add))
                    tt(p2[:, 0:nt], p2[:, 0:nt], p1[:, 0:nt], ALU.subtract).then_inc(d_ready, 1)
                    dve.wait_ge(e_ready, 2)
                    then_wait(nc.vector.tensor_scalar(total[:, 0:nt], p2[:, 0:nt], 1.0, None, ALU.add))
                    then_wait(nc.vector.reciprocal(weight[0][:, 0:nt], total[:, 0:nt]))
                    then_wait(tt(weight[1][:, 0:nt], weight[0][:, 0:nt], p2[:, 0:nt], ALU.mult))
                    dve.wait_ge(counted, 1)
                    then_wait(nc.vector.tensor_copy(per[:, :, 0:nt],
                                                    pT[:, 0:nt * E].rearrange("p (t e) -> p e t", e=E)))
                    if nt < NT:
                        then_wait(nc.vector.memset(per[:, :, nt:NT], 0.0))
                    lin = lambda ap: ap[:, :, :].rearrange("p e t -> p (e t)")
                    then_wait(nc.vector.tensor_tensor_scan(lin(cum), onesT[:, :], lin(per), 0.0, ALU.mult, ALU.add))
                    then_wait(tt(cex[:, :, :], cum[:, :, :], per[:, :, :], ALU.subtract))
                    then_wait(tt(cnt[:, :], cum[:, :, NT - 1], cex[:, :, 0], ALU.subtract))
                    then_wait(nc.vector.tensor_scalar(tiles[:, :], cnt[:, :], TILE / 2 - 0.5, 1.0 / TILE, ALU.add, ALU.mult))
                    then_wait(nc.vector.tensor_scalar(tiles[:, :], tiles[:, :], ROUND, ROUND, ALU.add, ALU.subtract))
                    then_wait(nc.vector.tensor_scalar(tiles[:, :], tiles[:, :], 1.0, None, ALU.max))
                    then_wait(nc.vector.tensor_tensor_scan(tile_end[:, :], onesT[:, 0:E], tiles[:, :], 0.0,
                                                           ALU.mult, ALU.add))
                    then_wait(tt(tile_start[:, :], tile_end[:, :], tiles[:, :], ALU.subtract))
                    nc.vector.tensor_copy(bounds[:, 0:E], tile_start[0:1, :])
                    nc.vector.tensor_copy(bounds[:, E:2 * E], tile_end[0:1, :])
                    then_wait(nc.vector.scalar_tensor_tensor(base[:, :], tile_start[:, :], float(TILE), cex[:, :, 0],
                                                             ALU.mult, ALU.subtract))
                    then_wait(tt(PO, pW[:, 0:nt * E].rearrange("p (t e) -> p t e", e=E),
                                 cex[:, :, 0:nt].rearrange("p e t -> p t e"), ALU.add))
                    then_wait(tt(PO, PO, every(base), ALU.add))
                    for i, hot in enumerate((H1, H2)):
                        then_wait(tt(hot, hot, PO, ALU.mult))
                        then_wait(red(top[:, 0:nt], hot, AX.X, ALU.add))
                        nc.vector.tensor_copy(slot[i][:, 0:nt], top[:, 0:nt]).then_inc(slots_ready, 1)
                        dve.wait_ge(slots_ready, i + 1)

                @block.tensor
                def _(pe):
                    pe.wait_ge(c_in, 64)

                    def transpose_x(k, par):
                        pe.wait_ge(xn_ready, k + 1)
                        if not (isinstance(k, int) and k < 2):
                            pe.wait_ge(xT_ready, k - 1)
                        for c in range(KC):
                            for j in range(TB):
                                ins = nc.tensor.transpose(pX[par][:, c * S + j * P:c * S + (j + 1) * P],
                                                          xs[par][:, j, c * P:(c + 1) * P], core.ident[:, :])
                        ins.then_inc(xT_full, 1)

                    def round_(k, par, half, has):
                        if has[1]:
                            transpose_x(k + 1, 1 - par)
                        pe.wait_ge(xT_ready, k + 1)
                        if not (isinstance(k, int) and k < 2):
                            pe.wait_ge(l_ready, k - 1)
                        for j in range(TB):
                            for c in range(KC):
                                ins = nc.tensor.matmul(pL[par][:, j * E:(j + 1) * E], xT[par][:, c, j * P:(j + 1) * P],
                                                       Wg[:, c, :], start=c == 0, stop=c == KC - 1)
                        ins.then_inc(l_full, 1)
                    transpose_x(0, 0)
                    staggered(pe, n, round_)
                    pe.wait_ge(ones_ready, 1)
                    pe.wait_ge(d_ready, 2)
                    chosen = both[:, 0:nt, :].rearrange("p t e -> p (t e)")
                    nc.tensor.matmul(pW[:, 0:nt * E], tri[:, :], chosen, start=True, stop=True)
                    nc.tensor.matmul(pT[:, 0:nt * E], ones[:, :], chosen, start=True, stop=True).then_inc(counted, 1)

                @block.gpsimd
                def _(pool):
                    pool.wait_ge(core.cleared, 32)
                    pool.wait_ge(slots_ready, 2)
                    for t in range(nt):
                        for i in range(2):
                            pool.indirect_dma_start(gathered, bass.IndirectOffsetOnAxis(ap=slot[i][:, t:t + 1], axis=0),
                                                    XN[:, t, :], None).then_inc(scattered, 16)
                    pool.wait_ge(scattered, 16 * 2 * nt)

        second = ExitStack()
        with second:
            def sb2(name, shape, dt=F32):
                return second.enter_context(nc.sbuf_tensor(f"L3f_{name}", shape, dt))

            def sem2(name):
                return second.enter_context(nc.semaphore(f"L3f_{name}"))

            def ps2(name):
                return second.enter_context(nc.psum_tensor(f"L3f_{name}", [P, 512], F32))
            xg = sb2("xg", [P, TB, D])
            xgT = sb2("xgT", [P, KC, TILE])
            hT = sb2("hT", [P, HCH, TILE])
            y = sb2("y", [P, TB, D])
            start = sb2("start", [1, 4])
            pX2 = ps2("pX2")
            pH = [ps2(f"pH{i}") for i in range(4)]
            pY = [ps2(f"pY{i}") for i in range(TB)]
            xg_in, T_full, T_ready, y_full, y_ready = (sem2(s) for s in (
                "xg_in", "T_full", "T_ready", "y_full", "y_ready"))
            h_full = [sem2(f"h_full{i}") for i in range(2)]
            h_ready = [sem2(f"h_ready{i}") for i in range(2)]
            HALF = HCH // 2
            with nc.Block() as block:
                def expert_range(eng, e):
                    lo = eng.value_load(bounds[0:1, e:e + 1], min_val=e, max_val=MAX_TILES - 1)
                    hi = eng.value_load(bounds[0:1, E + e:E + e + 1], min_val=e + 1, max_val=MAX_TILES)
                    return lo, hi

                @block.sync
                def _(sp):
                    def load_rows(s):
                        sp.dma_start(xg[:, :, :],
                                     gathered.rearrange("(t j p) d -> t p j d", p=P, j=TB)[bass.ds(s, 1)]
                                     .rearrange("o p j d -> p (o j) d")).then_inc(xg_in, 16)
                    load_rows(0)
                    for e in range(E):
                        lo, hi = expert_range(sp, e)
                        with sp.Fori(lo, hi) as s:
                            sp.wait_ge(T_full, s + 1)
                            load_rows(s + 1)
                            sp.wait_ge(y_ready, s + 2)
                            sp.dma_start(expert_out.rearrange("(t j p) d -> t p j d", p=P, j=TB)[bass.ds(s, 1)]
                                         .rearrange("o p j d -> p (o j) d"), y[:, :, :]).then_inc(y_stored, 16)
                        if e + 2 < E:
                            load_expert(sp, e + 2)

                @block.tensor
                def _(pe):
                    def transpose_rows(s):
                        pe.wait_ge(xg_in, s * 16 + 16)
                        for c in range(KC):
                            for j in range(TB):
                                ins = nc.tensor.transpose(pX2[:, c * TILE + j * P:c * TILE + (j + 1) * P],
                                                          xg[:, j, c * P:(c + 1) * P], core.ident[:, :])
                        ins.then_inc(T_full, 1)
                    transpose_rows(0)
                    for e in range(E):
                        par = e % 2
                        lo, hi = expert_range(pe, e)
                        pe.wait_ge(w_in[par], 48 * (e // 2 + 1))
                        with pe.Fori(lo, hi) as s:
                            pe.wait_ge(T_ready, s + 1)
                            for c in range(HCH):
                                who, m = c % 2, c // 2
                                if c >= 4:
                                    pe.wait_ge(h_ready[who], s * HALF + m)
                                else:
                                    pe.wait_ge(h_ready[who], s * HALF + 1)
                                for kc in range(KC):
                                    ins = nc.tensor.matmul(pH[c % 4][:, 0:TILE], W1[par][:, kc, c * P:(c + 1) * P],
                                                           xgT[:, kc, :], start=kc == 0, stop=kc == KC - 1)
                                ins.then_inc(h_full[who], 1)
                            transpose_rows(s + 1)
                            pe.wait_ge(y_ready, s + 1)
                            for c in range(HCH):
                                pe.wait_ge(h_ready[c % 2], s * HALF + c // 2 + 2)
                                for j in range(TB):
                                    ins = nc.tensor.matmul(pY[j][:, 0:D], hT[:, c, j * P:(j + 1) * P],
                                                           W2[par][:, c, :], start=c == 0, stop=c == HCH - 1)
                            ins.then_inc(y_full, 1)

                @block.scalar
                def _(act):
                    act.wait_ge(b1_in, 16)
                    nc.scalar.activation(start[:, 0:1], b1[0:1, 0, 0:1], ACT.Copy).then_inc(h_ready[0], 1)

                    def take_T(s):
                        act.wait_ge(T_full, s + 1)
                        nc.scalar.activation(xgT[:, :, :], pX2[:, :].rearrange("p (c s) -> p c s", c=KC), ACT.Copy)\
                          .then_inc(T_ready, 1)
                    take_T(0)
                    for e in range(E):
                        lo, hi = expert_range(act, e)
                        with act.Fori(lo, hi) as s:
                            for m in range(HALF):
                                c = 2 * m
                                act.wait_ge(h_full[0], s * HALF + m + 1)
                                nc.scalar.activation(hT[:, c, :], pH[c % 4][:, 0:TILE], ACT.Relu, bias=b1[:, e, c:c + 1])\
                                  .then_inc(h_ready[0], 1)
                            take_T(s + 1)

                @block.vector
                def _(dve):
                    for i, (count, by) in enumerate(((h_ready[1], 1), (y_ready, 1), (y_stored, 16))):
                        nc.vector.memset(start[:, i + 1:i + 2], 0.0).then_inc(count, by)
                    dve.wait_ge(b1_in, 16)
                    for e in range(E):
                        lo, hi = expert_range(dve, e)
                        dve.wait_ge(w_in[e % 2], 48 * (e // 2 + 1))
                        with dve.Fori(lo, hi) as s:
                            for m in range(HALF):
                                c = 2 * m + 1
                                dve.wait_ge(h_full[1], s * HALF + m + 1)
                                nc.vector.tensor_scalar(hT[:, c, :], pH[c % 4][:, 0:TILE], b1[:, e, c:c + 1], 0.0,
                                                        ALU.add, ALU.max).then_inc(h_ready[1], 1)
                            dve.wait_ge(y_full, s + 1)
                            dve.wait_ge(y_stored, s * 16 + 16)
                            for j in range(TB):
                                ins = nc.vector.tensor_tensor(y[:, j, :], pY[j][:, 0:D], b2[e % 2][:, :], ALU.add)
                            ins.then_inc(y_ready, 1)

        third = ExitStack()
        with third:
            RING = 4
            yg = third.enter_context(nc.sbuf_tensor("L3f_yg", [P, RING, 2, D], F32))
            part = third.enter_context(nc.sbuf_tensor("L3f_part", [P, 2, D], F32))
            yg_in = [third.enter_context(nc.semaphore(f"L3f_yg_in{i}")) for i in range(RING)]
            part_ready = third.enter_context(nc.semaphore("L3f_part_ready"))
            x_new = third.enter_context(nc.semaphore("L3f_x_new"))
            all_stored = third.enter_context(nc.semaphore("L3f_all_stored"))
            with nc.Block() as block:
                @block.gpsimd
                def _(pool):
                    pool.wait_ge(all_stored, 1)
                    for t in range(nt):
                        if t >= RING:
                            pool.wait_ge(x_new, t - RING + 1)
                        for i in range(2):
                            pool.indirect_dma_start(yg[:, t % RING, i, :], None, expert_out,
                                                    bass.IndirectOffsetOnAxis(ap=slot[i][:, t:t + 1], axis=0))\
                                .then_inc(yg_in[t % RING], 16)

                @block.vector
                def _(dve):
                    tiles_all = dve.value_load(bounds[0:1, 2 * E - 1:2 * E], min_val=E, max_val=MAX_TILES)
                    dve.wait_ge(y_stored, tiles_all * 16 + 16)
                    nc.vector.memset(part[:, 0, 0:1], 0.0).then_inc(all_stored, 1)
                    dve.wait_ge(all_stored, 1)
                    for t in range(nt):
                        dve.wait_ge(yg_in[t % RING], 32 * (t // RING + 1))
                        nc.vector.scalar_tensor_tensor(part[:, t % 2, :], yg[:, t % RING, 0, :], weight[0][:, t:t + 1],
                                                       X[:, t, :], ALU.mult, ALU.add).then_inc(part_ready, 1)
                        dve.wait_ge(part_ready, t + 1)
                        nc.vector.scalar_tensor_tensor(X[:, t, :], yg[:, t % RING, 1, :], weight[1][:, t:t + 1],
                                                       part[:, t % 2, :], ALU.mult, ALU.add).then_inc(x_new, 1)


def build(nc, dram):
    with ExitStack() as ctx:
        core = Core(nc, ctx, dram)
        load_residual(core)
        norm_params(core, "L0x_norm")
        attention(core, "L0x", 16, "L0_wq", "L0_wk", "L0_wv", "L0_wo", 0.25, "L0_bq", "L0_bk", "L0_bv", "L0_bo", clear=True)
        norm_params(core, "L0f_norm")
        ternary_ffn(core)
        reuse_semaphores(core)
        norm_params(core, "L1x_norm")
        mlstm(core)
        norm_params(core, "L1f_norm")
        routed_low_rank(core)
        reuse_semaphores(core)
        norm_params(core, "L2x_norm", second_eps=1e-5)
        attention(core, "L2x", 64, "L2_wq", "L2_wk", "L2_wv", "L2_wo", 0.125, b_o="L2_bo",
                  gamma="L2_gamma", beta="L2_beta", gate="L2_gate")
        reuse_semaphores(core)
        norm_params(core, "L2f_norm")
        int8_ffn(core)
        reuse_semaphores(core)
        norm_params(core, "L3x_norm")
        attention(core, "L3x", 16, "L3_wq", "L3_wk", "L3_wv", "L3_wo", 0.25)
        norm_params(core, "L3f_norm")
        routed_experts(core)
        store_residual(core)


def kernel(**inputs):
    import concourse.bacc as bacc
    from concourse.bass_utils import run_bass_kernel_spmd as run

    a = {k: np.asarray(x) for k, x in inputs.items()}
    t = lambda w: np.ascontiguousarray(w.T)

    def dim_major(w, dims_first=False):
        lead = w.shape[:-1]
        w = w.reshape(*lead, 16, 2, 8) if dims_first else np.moveaxis(w.reshape(*lead, 2, 8, 16), -1, -3)
        return np.ascontiguousarray(np.swapaxes(w, -3, -2).reshape(*lead, D)) 

    def head_major(w):
        return np.ascontiguousarray(w.reshape(w.shape[0], D // H, H).transpose(0, 2, 1).reshape(w.shape[0], D))

    arrays = {
        "x": a["x"], "ctx": a["ctx_1024"], "ctxT": np.ascontiguousarray(a["ctx_1024"].transpose(0, 2, 1)),
        "ident": np.eye(P, dtype=np.float32),
        "head_select": ((np.arange(P)[:, None] % H == np.arange(H)) & (np.arange(P)[:, None] < 2 * H)).astype(np.float32),
        "L0_wq": dim_major(t(a["L0_xattn_w_q"])), "L0_wk": dim_major(t(a["L0_xattn_w_k"])), "L0_wv": t(a["L0_xattn_w_v"]),
        "L0_wo": t(a["L0_xattn_w_o"]), "L0_bq": dim_major(a["L0_xattn_b_q"]), "L0_bk": dim_major(a["L0_xattn_b_k"]),
        "L0_bv": a["L0_xattn_b_v"], "L0_bo": a["L0_xattn_b_o"],
        "L2_wq": a["L2_xattn_w_q"], "L2_wk": np.ascontiguousarray(a["L2_xattn_w_kv"][:, :1024]),
        "L2_wv": np.ascontiguousarray(a["L2_xattn_w_kv"][:, 1024:]), "L2_wo": a["L2_xattn_w_out"],
        "L2_bo": a["L2_xattn_b_out"], "L2_gate": a["L2_xattn_gate"], "L2_gamma": a["L2_xattn_ln_gamma"],
        "L2_beta": a["L2_xattn_ln_beta"],
        "L3_wq": dim_major(t(a["L3_xattn_Wq"]), True), "L3_wk": dim_major(t(a["L3_xattn_Wk"]), True),
        "L3_wv": head_major(t(a["L3_xattn_Wk"])),
        "L3_wo": np.ascontiguousarray(head_major(a["L3_xattn_Wo"]).T),
        "L0f_wg": t(a["L0_ffn_w_gate"]), "L0f_wu": t(a["L0_ffn_w_up"]), "L0f_wd": t(a["L0_ffn_w_down"]),
        "L2f_wg": np.pad(a["L2_ffn_w_gate"], ((0, 64), (0, 0))), "L2f_wu": np.pad(a["L2_ffn_w_up"], ((0, 64), (0, 0))),
        "L2f_wd": np.pad(a["L2_ffn_w_down"], ((0, 0), (0, 64))),
        "L2f_clip_x": a["L2_ffn_clip_x"], "L2f_clip_down": a["L2_ffn_clip_down"],
        "L1x_gates": np.concatenate([np.pad(a["L1_xattn_fgate_kernel"], ((0, 0), (0, 28))),
                                     np.pad(a["L1_xattn_igate_kernel"], ((0, 0), (0, 28)))], 1),
        "L1x_fb": a["L1_xattn_fgate_bias"], "L1x_ib": a["L1_xattn_igate_bias"], "L1x_scale": a["L1_xattn_outnorm_scale"],
        "L1x_mask": np.where(np.arange(P)[:, None] > np.arange(S)[None, :], -1e30, 0.0).astype(np.float32),
        "L1x_sel": -np.repeat((np.arange(P)[:, None] == np.arange(4)[None, :])[:, :, None], P, 2).astype(np.float32),
        "L1f_WpdT": np.concatenate([t(a["L1_ffn_Wp"])] + [np.pad(t(a[f"L1_ffn_Wd{e}"]), ((0, 0), (0, 8 - 2 ** e)))
                                                          for e in range(4)], 1),
        "L1f_WuT": np.concatenate([np.pad(t(a[f"L1_ffn_Wu{e}"]), ((0, 8 - 2 ** e), (0, 0))) for e in range(4)], 0),
        "L1f_WT": t(a["L1_ffn_W"]), "L1f_bp": a["L1_ffn_bp"], "L1f_sim": a["L1_ffn_sim"], "L1f_temp": a["L1_ffn_temp"],
        "L1f_prefer": np.arange(4, 0, -1).astype(np.float32),
        "L3f_W1": a["L3_ffn_W1"], "L3f_b1": a["L3_ffn_b1"], "L3f_W2": a["L3_ffn_W2"], "L3f_b2": a["L3_ffn_b2"],
        "L3f_Wg": a["L3_ffn_Wg"], "L3f_bg": a["L3_ffn_bg"], "L3f_prefer": np.arange(8, 0, -1).astype(np.float32),
        "L3f_tri": (np.arange(P)[:, None] < np.arange(P)[None, :]).astype(np.float32),
    }
    nc = bacc.Bacc("TRN2", target_bir_lowering=False, num_devices=1)
    dram = {n: nc.dram_tensor(f"in_{n}", x.shape, mybir.dt.from_np(x.dtype), kind="ExternalInput").ap()
            for n, x in arrays.items()}
    dram["out"] = nc.dram_tensor("out", a["x"].shape, F32, kind="ExternalOutput").ap()
    build(nc, dram)
    r = run(nc, [{f"in_{n}": x for n, x in arrays.items()}], core_ids=[0])
    return r.results[0]["out"]
```
